# Optimizing a Trainium2 kernel written in Bass

```python
import numpy as np
import jax
import jax.numpy as jnp

def _softmax(x, axis=-1):
    return jax.nn.softmax(x, axis=axis)

def _gelu(x):
    return jax.nn.gelu(x, approximate=True)

def _silu(x):
    return jax.nn.silu(x)

def _sigmoid(x):
    return jax.nn.sigmoid(x)

def _layernorm(x, axis=-1, eps=1e-05):
    m = jnp.mean(x, axis=axis, keepdims=True)
    v = jnp.var(x, axis=axis, keepdims=True)
    return (x - m) / jnp.sqrt(v + eps)

def _scatter_add(tgt, idx, src, axis=0):
    return tgt.at[idx].add(src)

def _segment_sum(src, seg, n):
    return jax.ops.segment_sum(src, seg, n)
kernel_name = 'mk_audio_tower_d2_tok_audfeat1024_r4_4ab846'

def setup_inputs(seed: int=0):
    np.random.seed(seed)
    _w = jnp.asarray

    def _rec_inputs():
        import jax
        import jax.numpy as jnp
        _rk = jax.random.key(seed)
        x = -0.000125008 + 0.999885 * jax.random.normal(jax.random.fold_in(_rk, 1), (16, 750, 64), jnp.float32)
        return x
    x = _rec_inputs()

    def _L0_tok_setup():
        import jax, jax.numpy as jnp
        import numpy as np
        from jax import lax
        N_CHANNELS = 64
        FRONTEND_DIM = 256
        TEMPORAL_KERNEL = 32
        TEMPORAL_STRIDE = 4
        GAUSS_SIGMA = 2.0
        GAUSS_KSIZE = int(GAUSS_SIGMA * 4) + 1
        GAUSS_PAD = GAUSS_KSIZE // 2
        LN_EPS = 1e-05

        def _gaussian_kernel():
            t = jnp.arange(GAUSS_KSIZE, dtype=jnp.float32) - (GAUSS_KSIZE - 1) / 2
            g = jnp.exp(-t ** 2 / (2.0 * GAUSS_SIGMA ** 2))
            return g / g.sum()

        def _depthwise_conv1d(x_nct, w_c1k, stride, pad):
            return lax.conv_general_dilated(x_nct, w_c1k, window_strides=(stride,), padding=[(pad, pad)], dimension_numbers=('NCH', 'OIH', 'NCH'), feature_group_count=N_CHANNELS)
        key = jax.random.key(seed)
        k1, k2, k3, k4, k5, k6 = jax.random.split(key, 6)
        B, T, C, D = (16, 2048, N_CHANNELS, FRONTEND_DIM)
        x = jax.random.normal(k1, (B, T, C), dtype=jnp.float32)
        w_temporal = jax.random.normal(k2, (C, 1, TEMPORAL_KERNEL), dtype=jnp.float32) * (1.0 / TEMPORAL_KERNEL)
        w_proj = jax.random.normal(k3, (D, C), dtype=jnp.float32) * (1.0 / np.sqrt(C))
        b_proj = jax.random.normal(k4, (D,), dtype=jnp.float32) * 0.01
        ln_gamma = jnp.ones((D,), dtype=jnp.float32)
        ln_beta = jnp.zeros((D,), dtype=jnp.float32)
        return {'x': x, 'w_temporal': w_temporal, 'w_proj': w_proj, 'b_proj': b_proj, 'ln_gamma': ln_gamma, 'ln_beta': ln_beta}
    _L0_tok_all = _L0_tok_setup()
    _L0_tok_in = {k: v for k, v in _L0_tok_all.items() if k in ('w_temporal', 'w_proj', 'b_proj', 'ln_gamma', 'ln_beta')}
    del _L0_tok_all

    def _L0_attn_setup():
        import jax, jax.numpy as jnp
        import numpy as np
        B, T, NE, H = (4, 256, 256, 16)
        HS = NE // H
        EPS = 0.00064

        def _forward(x, time_maa_x, time_maa, maa_w1, maa_w2, decay_w1, decay_w2, aaa_w1, aaa_w2, kkk_w1, kkk_w2, gate_w1, gate_w2, ma_w1, ma_w2, mk_w1, mk_w2, time_decay, time_faaaa, time_aaaaa, time_misc_a, time_misc_k, Wr, Wk, Wv, Wo, ln_w, ln_b):
            Bx, Tx, C = x.shape
            xx = jnp.pad(x, ((0, 0), (1, 0), (0, 0)))[:, :Tx] - x
            mix = x + xx * time_maa_x
            lo = jnp.tanh(jnp.einsum('btc,dc->btd', mix, maa_w1)).reshape(Bx, Tx, 4, 32)
            lo = jnp.einsum('btgk,gkc->gbtc', lo, maa_w2)
            xm = x[None] + xx[None] * (lo + time_maa)
            xrg, xwa, xk, xv = (xm[0], xm[1], xm[2], xm[3])
            r = xrg @ Wr.T
            g = jnp.tanh(xrg @ gate_w1.T) @ gate_w2
            k = xk @ Wk.T
            v = xv @ Wv.T
            w2 = jnp.tanh(xwa @ decay_w1.T) @ decay_w2
            w = -jax.nn.softplus(-(time_decay + w2)) - 0.5
            kk = k + jnp.tanh(xk @ kkk_w1.T) @ kkk_w2
            kkh = kk.reshape(Bx, Tx, H, HS)
            kk = (kkh / jnp.maximum(jnp.linalg.norm(kkh, axis=-1, keepdims=True), 1e-12)).reshape(Bx, Tx, C)
            a = jax.nn.sigmoid(time_aaaaa + xwa @ aaa_w1.T @ aaa_w2)
            ma = jax.nn.sigmoid(time_misc_a + xwa @ ma_w1.T @ ma_w2)
            k = k * ma + k * a * (1.0 - ma)
            mk = jax.nn.sigmoid(time_misc_k + xk @ mk_w1.T @ mk_w2)
            k = k * jnp.exp(w * mk)
            b = -kk * a

            def to_th(t):
                return t.reshape(Bx, Tx, H, HS).transpose(1, 0, 2, 3)
            qt, wt, kt, vt, at, bt = map(to_th, (r, w, k, v, kk, b))
            wt = jnp.exp(-jnp.exp(wt))

            def step(s, inp):
                q_, w_, k_, v_, a_, b_ = inp
                sa = jnp.einsum('bhij,bhj->bhi', s, a_)
                s = s * w_[:, :, None, :] + sa[..., None] * b_[:, :, None, :] + v_[..., None] * k_[:, :, None, :]
                return (s, jnp.einsum('bhij,bhj->bhi', s, q_))
            s0 = jnp.zeros((Bx, H, HS, HS), x.dtype)
            _, y = jax.lax.scan(step, s0, (qt, wt, kt, vt, at, bt))
            y = y.transpose(1, 0, 2, 3).reshape(Bx, Tx, C)
            yg = y.reshape(Bx, Tx, H, HS)
            mu = yg.mean(-1, keepdims=True)
            var = ((yg - mu) ** 2).mean(-1, keepdims=True)
            y = ((yg - mu) / jnp.sqrt(var + EPS)).reshape(Bx, Tx, C) * ln_w + ln_b
            rk = (r.reshape(Bx, Tx, H, HS) * k.reshape(Bx, Tx, H, HS) * time_faaaa.reshape(H, HS)).sum(-1, keepdims=True)
            y = y + (rk * v.reshape(Bx, Tx, H, HS)).reshape(Bx, Tx, C)
            return y * g @ Wo.T
        key = jax.random.key(seed)
        ks = jax.random.split(key, 30)

        def rn(k, shape, s):
            return jax.random.normal(k, shape, jnp.float32) * s
        d = {}
        d['x'] = jax.random.normal(ks[0], (B, T, NE), jnp.float32)
        d['time_maa_x'] = jax.random.uniform(ks[1], (NE,), jnp.float32)
        d['time_maa'] = jax.random.uniform(ks[2], (4, 1, 1, NE), jnp.float32)
        d['maa_w1'] = rn(ks[3], (128, NE), 0.02)
        d['maa_w2'] = rn(ks[4], (4, 32, NE), 0.02)
        d['decay_w1'] = rn(ks[5], (64, NE), 0.02)
        d['decay_w2'] = rn(ks[6], (64, NE), 0.02)
        d['aaa_w1'] = rn(ks[7], (16, NE), 0.02)
        d['aaa_w2'] = rn(ks[8], (16, NE), 0.02)
        d['kkk_w1'] = rn(ks[9], (16, NE), 0.02)
        d['kkk_w2'] = rn(ks[10], (16, NE), 0.02)
        d['gate_w1'] = rn(ks[11], (128, NE), 0.02)
        d['gate_w2'] = rn(ks[12], (128, NE), 0.02)
        d['ma_w1'] = rn(ks[13], (16, NE), 0.02)
        d['ma_w2'] = rn(ks[14], (16, NE), 0.02)
        d['mk_w1'] = rn(ks[15], (16, NE), 0.02)
        d['mk_w2'] = rn(ks[16], (16, NE), 0.02)
        d['time_decay'] = jnp.linspace(-6.5, -1.5, NE, dtype=jnp.float32)
        d['time_faaaa'] = rn(ks[17], (NE,), 0.02)
        d['time_aaaaa'] = rn(ks[18], (NE,), 0.02)
        d['time_misc_a'] = rn(ks[19], (NE,), 0.02)
        d['time_misc_k'] = rn(ks[20], (NE,), 0.02)
        d['Wr'] = rn(ks[21], (NE, NE), 0.5 / NE ** 0.5)
        d['Wk'] = rn(ks[22], (NE, NE), 0.05 / NE ** 0.5)
        d['Wv'] = rn(ks[23], (NE, NE), 0.5 / NE ** 0.5)
        d['Wo'] = rn(ks[24], (NE, NE), 1.0 / NE ** 0.5)
        d['ln_w'] = jnp.ones((NE,), jnp.float32)
        d['ln_b'] = jnp.zeros((NE,), jnp.float32)
        return d
    _L0_attn_all = _L0_attn_setup()
    _L0_attn_in = {k: v for k, v in _L0_attn_all.items() if k in ('time_maa_x', 'time_maa', 'maa_w1', 'maa_w2', 'decay_w1', 'decay_w2', 'aaa_w1', 'aaa_w2', 'kkk_w1', 'kkk_w2', 'gate_w1', 'gate_w2', 'ma_w1', 'ma_w2', 'mk_w1', 'mk_w2', 'time_decay', 'time_faaaa', 'time_aaaaa', 'time_misc_a', 'time_misc_k', 'Wr', 'Wk', 'Wv', 'Wo', 'ln_w', 'ln_b')}
    del _L0_attn_all

    def _L0_ffn_setup():
        import jax, jax.numpy as jnp
        import numpy as np
        B, S, D = (8, 1024, 256)
        E, R, K = (6, 16, 2)
        key = jax.random.key(seed)
        ks = jax.random.split(key, 9)
        sc = 0.02
        return {'x': jax.random.normal(ks[0], (B, S, D), jnp.float32), 'base_W': jax.random.normal(ks[1], (D, D), jnp.float32) * sc, 'base_b': jax.random.normal(ks[2], (D,), jnp.float32) * sc, 'shared_A': jax.random.normal(ks[3], (R, D), jnp.float32) * sc, 'shared_B': jax.random.normal(ks[4], (D, R), jnp.float32) * sc, 'routed_A': jax.random.normal(ks[5], (E, R, D), jnp.float32) * sc, 'routed_B': jax.random.normal(ks[6], (E, D, R), jnp.float32) * sc, 'router_W': jax.random.normal(ks[7], (E, D), jnp.float32) * sc, 'router_b': jax.random.normal(ks[8], (E,), jnp.float32) * sc}
    _L0_ffn_all = _L0_ffn_setup()
    _L0_ffn_in = {k: v for k, v in _L0_ffn_all.items() if k in ('base_W', 'base_b', 'shared_A', 'shared_B', 'routed_A', 'routed_B', 'router_W', 'router_b')}
    del _L0_ffn_all

    def _L1_attn_setup():
        import jax, jax.numpy as jnp
        import numpy as np
        T, B, E, H, HID, SIG = (256, 4, 256, 16, 256, 64)
        key = jax.random.key(seed)
        ks = jax.random.split(key, 16)
        sc = 0.02
        return {'x': jax.random.normal(ks[0], (T, B, E), jnp.float32), 'Wq': jax.random.normal(ks[1], (E, E), jnp.float32) * sc, 'bq': jnp.zeros((E,), jnp.float32), 'Wk': jax.random.normal(ks[2], (E, E), jnp.float32) * sc, 'bk': jnp.zeros((E,), jnp.float32), 'Wv': jax.random.normal(ks[3], (E, E), jnp.float32) * sc, 'bv': jnp.zeros((E,), jnp.float32), 'Wo': jax.random.normal(ks[4], (E, E), jnp.float32) * sc, 'bo': jnp.zeros((E,), jnp.float32), 'W1': jax.random.normal(ks[5], (HID, E), jnp.float32) * sc, 'b1': jnp.zeros((HID,), jnp.float32), 'W2': jax.random.normal(ks[6], (SIG, HID), jnp.float32) * sc, 'b2': jnp.zeros((SIG,), jnp.float32), 'head_signatures': jax.random.normal(ks[7], (H, SIG), jnp.float32)}
    _L1_attn_all = _L1_attn_setup()
    _L1_attn_in = {k: v for k, v in _L1_attn_all.items() if k in ('Wq', 'bq', 'Wk', 'bk', 'Wv', 'bv', 'Wo', 'bo', 'W1', 'b1', 'W2', 'b2', 'head_signatures')}
    del _L1_attn_all

    def _L1_ffn_setup():
        import jax, jax.numpy as jnp
        import numpy as np
        B, N, D = (4, 512, 256)
        SPARSITY = 0.01
        key = jax.random.key(seed)
        k1, k2, k3 = jax.random.split(key, 3)
        x = jax.random.normal(k1, (B, N, D), dtype=jnp.float32)
        spatial = jax.random.normal(k2, (D, D), dtype=jnp.float32) * 0.02
        freq = jnp.fft.fft(spatial, axis=-1)
        k = int(D * SPARSITY)
        mag = jnp.abs(freq)
        kth = jax.lax.top_k(mag, k)[0][:, -1:]
        w_sparse = jnp.where(mag >= kth, freq, 0.0 + 0j)
        bias = jax.random.normal(k3, (D,), dtype=jnp.float32) * 0.01
        return {'x': x, 'w_freq_real': jnp.real(w_sparse).astype(jnp.float32), 'w_freq_imag': jnp.imag(w_sparse).astype(jnp.float32), 'bias': bias}
    _L1_ffn_all = _L1_ffn_setup()
    _L1_ffn_in = {k: v for k, v in _L1_ffn_all.items() if k in ('w_freq_real', 'w_freq_imag', 'bias')}
    del _L1_ffn_all
    return {'x': x, 'L0_tok_w_temporal': _L0_tok_in['w_temporal'], 'L0_tok_w_proj': _L0_tok_in['w_proj'], 'L0_tok_b_proj': _L0_tok_in['b_proj'], 'L0_tok_ln_gamma': _L0_tok_in['ln_gamma'], 'L0_tok_ln_beta': _L0_tok_in['ln_beta'], 'L0_attn_time_maa_x': _L0_attn_in['time_maa_x'], 'L0_attn_time_maa': _L0_attn_in['time_maa'], 'L0_attn_maa_w1': _L0_attn_in['maa_w1'], 'L0_attn_maa_w2': _L0_attn_in['maa_w2'], 'L0_attn_decay_w1': _L0_attn_in['decay_w1'], 'L0_attn_decay_w2': _L0_attn_in['decay_w2'], 'L0_attn_aaa_w1': _L0_attn_in['aaa_w1'], 'L0_attn_aaa_w2': _L0_attn_in['aaa_w2'], 'L0_attn_kkk_w1': _L0_attn_in['kkk_w1'], 'L0_attn_kkk_w2': _L0_attn_in['kkk_w2'], 'L0_attn_gate_w1': _L0_attn_in['gate_w1'], 'L0_attn_gate_w2': _L0_attn_in['gate_w2'], 'L0_attn_ma_w1': _L0_attn_in['ma_w1'], 'L0_attn_ma_w2': _L0_attn_in['ma_w2'], 'L0_attn_mk_w1': _L0_attn_in['mk_w1'], 'L0_attn_mk_w2': _L0_attn_in['mk_w2'], 'L0_attn_time_decay': _L0_attn_in['time_decay'], 'L0_attn_time_faaaa': _L0_attn_in['time_faaaa'], 'L0_attn_time_aaaaa': _L0_attn_in['time_aaaaa'], 'L0_attn_time_misc_a': _L0_attn_in['time_misc_a'], 'L0_attn_time_misc_k': _L0_attn_in['time_misc_k'], 'L0_attn_Wr': _L0_attn_in['Wr'], 'L0_attn_Wk': _L0_attn_in['Wk'], 'L0_attn_Wv': _L0_attn_in['Wv'], 'L0_attn_Wo': _L0_attn_in['Wo'], 'L0_attn_ln_w': _L0_attn_in['ln_w'], 'L0_attn_ln_b': _L0_attn_in['ln_b'], 'L0_ffn_base_W': _L0_ffn_in['base_W'], 'L0_ffn_base_b': _L0_ffn_in['base_b'], 'L0_ffn_shared_A': _L0_ffn_in['shared_A'], 'L0_ffn_shared_B': _L0_ffn_in['shared_B'], 'L0_ffn_routed_A': _L0_ffn_in['routed_A'], 'L0_ffn_routed_B': _L0_ffn_in['routed_B'], 'L0_ffn_router_W': _L0_ffn_in['router_W'], 'L0_ffn_router_b': _L0_ffn_in['router_b'], 'L1_attn_Wq': _L1_attn_in['Wq'], 'L1_attn_bq': _L1_attn_in['bq'], 'L1_attn_Wk': _L1_attn_in['Wk'], 'L1_attn_bk': _L1_attn_in['bk'], 'L1_attn_Wv': _L1_attn_in['Wv'], 'L1_attn_bv': _L1_attn_in['bv'], 'L1_attn_Wo': _L1_attn_in['Wo'], 'L1_attn_bo': _L1_attn_in['bo'], 'L1_attn_W1': _L1_attn_in['W1'], 'L1_attn_b1': _L1_attn_in['b1'], 'L1_attn_W2': _L1_attn_in['W2'], 'L1_attn_b2': _L1_attn_in['b2'], 'L1_attn_head_signatures': _L1_attn_in['head_signatures'], 'L1_ffn_w_freq_real': _L1_ffn_in['w_freq_real'], 'L1_ffn_w_freq_imag': _L1_ffn_in['w_freq_imag'], 'L1_ffn_bias': _L1_ffn_in['bias']}

def reference(x, L0_tok_w_temporal, L0_tok_w_proj, L0_tok_b_proj, L0_tok_ln_gamma, L0_tok_ln_beta, L0_attn_time_maa_x, L0_attn_time_maa, L0_attn_maa_w1, L0_attn_maa_w2, L0_attn_decay_w1, L0_attn_decay_w2, L0_attn_aaa_w1, L0_attn_aaa_w2, L0_attn_kkk_w1, L0_attn_kkk_w2, L0_attn_gate_w1, L0_attn_gate_w2, L0_attn_ma_w1, L0_attn_ma_w2, L0_attn_mk_w1, L0_attn_mk_w2, L0_attn_time_decay, L0_attn_time_faaaa, L0_attn_time_aaaaa, L0_attn_time_misc_a, L0_attn_time_misc_k, L0_attn_Wr, L0_attn_Wk, L0_attn_Wv, L0_attn_Wo, L0_attn_ln_w, L0_attn_ln_b, L0_ffn_base_W, L0_ffn_base_b, L0_ffn_shared_A, L0_ffn_shared_B, L0_ffn_routed_A, L0_ffn_routed_B, L0_ffn_router_W, L0_ffn_router_b, L1_attn_Wq, L1_attn_bq, L1_attn_Wk, L1_attn_bk, L1_attn_Wv, L1_attn_bv, L1_attn_Wo, L1_attn_bo, L1_attn_W1, L1_attn_b1, L1_attn_W2, L1_attn_b2, L1_attn_head_signatures, L1_ffn_w_freq_real, L1_ffn_w_freq_imag, L1_ffn_bias):
    import jax
    import jax.numpy as jnp

    def _L0_tok_ref(x, w_temporal, w_proj, b_proj, ln_gamma, ln_beta):
        import jax, jax.numpy as jnp
        import numpy as np
        from jax import lax
        N_CHANNELS = 64
        FRONTEND_DIM = 256
        TEMPORAL_KERNEL = 32
        TEMPORAL_STRIDE = 4
        GAUSS_SIGMA = 2.0
        GAUSS_KSIZE = int(GAUSS_SIGMA * 4) + 1
        GAUSS_PAD = GAUSS_KSIZE // 2
        LN_EPS = 1e-05

        def _gaussian_kernel():
            t = jnp.arange(GAUSS_KSIZE, dtype=jnp.float32) - (GAUSS_KSIZE - 1) / 2
            g = jnp.exp(-t ** 2 / (2.0 * GAUSS_SIGMA ** 2))
            return g / g.sum()

        def _depthwise_conv1d(x_nct, w_c1k, stride, pad):
            return lax.conv_general_dilated(x_nct, w_c1k, window_strides=(stride,), padding=[(pad, pad)], dimension_numbers=('NCH', 'OIH', 'NCH'), feature_group_count=N_CHANNELS)
        x_nct = jnp.transpose(x, (0, 2, 1))
        gk = jnp.broadcast_to(_gaussian_kernel()[None, None, :], (N_CHANNELS, 1, GAUSS_KSIZE))
        x_smooth = _depthwise_conv1d(x_nct, gk, stride=1, pad=GAUSS_PAD)
        x_strided = _depthwise_conv1d(x_smooth, w_temporal, stride=TEMPORAL_STRIDE, pad=0)
        x_strided = jnp.transpose(x_strided, (0, 2, 1))
        h = jnp.einsum('btc,dc->btd', x_strided, w_proj) + b_proj
        mu = jnp.mean(h, axis=-1, keepdims=True)
        xc = h - mu
        var = jnp.mean(xc * xc, axis=-1, keepdims=True)
        out = xc * lax.rsqrt(var + LN_EPS) * ln_gamma + ln_beta
        return out

    def _L0_attn_ref(x, time_maa_x, time_maa, maa_w1, maa_w2, decay_w1, decay_w2, aaa_w1, aaa_w2, kkk_w1, kkk_w2, gate_w1, gate_w2, ma_w1, ma_w2, mk_w1, mk_w2, time_decay, time_faaaa, time_aaaaa, time_misc_a, time_misc_k, Wr, Wk, Wv, Wo, ln_w, ln_b):
        import jax, jax.numpy as jnp
        import numpy as np
        B, T, NE, H = (4, 256, 256, 16)
        HS = NE // H
        EPS = 0.00064

        def _forward(x, time_maa_x, time_maa, maa_w1, maa_w2, decay_w1, decay_w2, aaa_w1, aaa_w2, kkk_w1, kkk_w2, gate_w1, gate_w2, ma_w1, ma_w2, mk_w1, mk_w2, time_decay, time_faaaa, time_aaaaa, time_misc_a, time_misc_k, Wr, Wk, Wv, Wo, ln_w, ln_b):
            Bx, Tx, C = x.shape
            xx = jnp.pad(x, ((0, 0), (1, 0), (0, 0)))[:, :Tx] - x
            mix = x + xx * time_maa_x
            lo = jnp.tanh(jnp.einsum('btc,dc->btd', mix, maa_w1)).reshape(Bx, Tx, 4, 32)
            lo = jnp.einsum('btgk,gkc->gbtc', lo, maa_w2)
            xm = x[None] + xx[None] * (lo + time_maa)
            xrg, xwa, xk, xv = (xm[0], xm[1], xm[2], xm[3])
            r = xrg @ Wr.T
            g = jnp.tanh(xrg @ gate_w1.T) @ gate_w2
            k = xk @ Wk.T
            v = xv @ Wv.T
            w2 = jnp.tanh(xwa @ decay_w1.T) @ decay_w2
            w = -jax.nn.softplus(-(time_decay + w2)) - 0.5
            kk = k + jnp.tanh(xk @ kkk_w1.T) @ kkk_w2
            kkh = kk.reshape(Bx, Tx, H, HS)
            kk = (kkh / jnp.maximum(jnp.linalg.norm(kkh, axis=-1, keepdims=True), 1e-12)).reshape(Bx, Tx, C)
            a = jax.nn.sigmoid(time_aaaaa + xwa @ aaa_w1.T @ aaa_w2)
            ma = jax.nn.sigmoid(time_misc_a + xwa @ ma_w1.T @ ma_w2)
            k = k * ma + k * a * (1.0 - ma)
            mk = jax.nn.sigmoid(time_misc_k + xk @ mk_w1.T @ mk_w2)
            k = k * jnp.exp(w * mk)
            b = -kk * a

            def to_th(t):
                return t.reshape(Bx, Tx, H, HS).transpose(1, 0, 2, 3)
            qt, wt, kt, vt, at, bt = map(to_th, (r, w, k, v, kk, b))
            wt = jnp.exp(-jnp.exp(wt))

            def step(s, inp):
                q_, w_, k_, v_, a_, b_ = inp
                sa = jnp.einsum('bhij,bhj->bhi', s, a_)
                s = s * w_[:, :, None, :] + sa[..., None] * b_[:, :, None, :] + v_[..., None] * k_[:, :, None, :]
                return (s, jnp.einsum('bhij,bhj->bhi', s, q_))
            s0 = jnp.zeros((Bx, H, HS, HS), x.dtype)
            _, y = jax.lax.scan(step, s0, (qt, wt, kt, vt, at, bt))
            y = y.transpose(1, 0, 2, 3).reshape(Bx, Tx, C)
            yg = y.reshape(Bx, Tx, H, HS)
            mu = yg.mean(-1, keepdims=True)
            var = ((yg - mu) ** 2).mean(-1, keepdims=True)
            y = ((yg - mu) / jnp.sqrt(var + EPS)).reshape(Bx, Tx, C) * ln_w + ln_b
            rk = (r.reshape(Bx, Tx, H, HS) * k.reshape(Bx, Tx, H, HS) * time_faaaa.reshape(H, HS)).sum(-1, keepdims=True)
            y = y + (rk * v.reshape(Bx, Tx, H, HS)).reshape(Bx, Tx, C)
            return y * g @ Wo.T
        return _forward(x, time_maa_x, time_maa, maa_w1, maa_w2, decay_w1, decay_w2, aaa_w1, aaa_w2, kkk_w1, kkk_w2, gate_w1, gate_w2, ma_w1, ma_w2, mk_w1, mk_w2, time_decay, time_faaaa, time_aaaaa, time_misc_a, time_misc_k, Wr, Wk, Wv, Wo, ln_w, ln_b)

    def _L0_ffn_ref(x, base_W, base_b, shared_A, shared_B, routed_A, routed_B, router_W, router_b):
        import jax, jax.numpy as jnp
        import numpy as np
        B, S, D = (8, 1024, 256)
        E, R, K = (6, 16, 2)
        base_out = jax.lax.stop_gradient(jnp.einsum('bsi,oi->bso', x, base_W) + base_b)
        shared_out = jnp.einsum('bsr,or->bso', jnp.einsum('bsi,ri->bsr', x, shared_A), shared_B)
        logits = jnp.einsum('bsi,ei->bse', x, router_W) + router_b
        gate = jax.nn.softmax(logits, axis=-1)
        topk_w, topk_i = jax.lax.top_k(gate, K)
        sparse_w = jnp.sum(jax.nn.one_hot(topk_i, E, dtype=gate.dtype) * topk_w[..., None], axis=-2)
        sparse_w = sparse_w / (jnp.sum(sparse_w, axis=-1, keepdims=True) + 1e-06)
        h = jnp.einsum('bsi,eri->bser', x, routed_A)
        routed_outs = jnp.einsum('bser,eor->bseo', h, routed_B)
        routed_out = jnp.einsum('bseo,bse->bso', routed_outs, sparse_w)
        return base_out + shared_out + routed_out

    def _L1_attn_ref(x, Wq, bq, Wk, bk, Wv, bv, Wo, bo, W1, b1, W2, b2, head_signatures):
        import jax, jax.numpy as jnp
        import numpy as np
        T, B, E, H, HID, SIG = (256, 4, 256, 16, 256, 64)
        T_, B_, E_ = x.shape
        H_ = head_signatures.shape[0]
        d = E_ // H_
        scaling = d ** (-0.5)
        q = (x @ Wq.T + bq) * scaling
        k = x @ Wk.T + bk
        v = x @ Wv.T + bv

        def split_heads(z):
            return z.reshape(T_, B_, H_, d).transpose(1, 2, 0, 3)
        qh, kh, vh = (split_heads(q), split_heads(k), split_heads(v))
        scores = jnp.einsum('bhtd,bhsd->bhts', qh, kh)
        attn = jax.nn.softmax(scores, axis=-1)
        o = jnp.einsum('bhts,bhsd->bhtd', attn, vh)
        t = jax.nn.relu(x @ W1.T + b1) @ W2.T + b2
        logits = t @ head_signatures.T
        gate = jax.nn.softmax(logits, axis=-1)
        gate = gate.transpose(1, 2, 0)
        o = o * gate[..., None]
        out = o.transpose(2, 0, 1, 3).reshape(T_, B_, E_)
        return out @ Wo.T + bo

    def _L1_ffn_ref(x, w_freq_real, w_freq_imag, bias):
        import jax, jax.numpy as jnp
        import numpy as np
        B, N, D = (4, 512, 256)
        SPARSITY = 0.01
        w = jax.lax.complex(w_freq_real, w_freq_imag)
        x_freq = jnp.fft.fft(x, axis=-1)
        y_freq = jnp.einsum('bnd,do->bno', x_freq, w)
        y = jnp.real(jnp.fft.ifft(y_freq, axis=-1))
        return y + bias
    h = _L0_tok_ref(x, L0_tok_w_temporal, L0_tok_w_proj, L0_tok_b_proj, L0_tok_ln_gamma, L0_tok_ln_beta)
    h = h + _L0_attn_ref(_layernorm(h, axis=-1), L0_attn_time_maa_x, L0_attn_time_maa, L0_attn_maa_w1, L0_attn_maa_w2, L0_attn_decay_w1, L0_attn_decay_w2, L0_attn_aaa_w1, L0_attn_aaa_w2, L0_attn_kkk_w1, L0_attn_kkk_w2, L0_attn_gate_w1, L0_attn_gate_w2, L0_attn_ma_w1, L0_attn_ma_w2, L0_attn_mk_w1, L0_attn_mk_w2, L0_attn_time_decay, L0_attn_time_faaaa, L0_attn_time_aaaaa, L0_attn_time_misc_a, L0_attn_time_misc_k, L0_attn_Wr, L0_attn_Wk, L0_attn_Wv, L0_attn_Wo, L0_attn_ln_w, L0_attn_ln_b)
    h = h + _L0_ffn_ref(_layernorm(h, axis=-1), L0_ffn_base_W, L0_ffn_base_b, L0_ffn_shared_A, L0_ffn_shared_B, L0_ffn_routed_A, L0_ffn_routed_B, L0_ffn_router_W, L0_ffn_router_b)
    h = h + _L1_attn_ref(_layernorm(h, axis=-1), L1_attn_Wq, L1_attn_bq, L1_attn_Wk, L1_attn_bk, L1_attn_Wv, L1_attn_bv, L1_attn_Wo, L1_attn_bo, L1_attn_W1, L1_attn_b1, L1_attn_W2, L1_attn_b2, L1_attn_head_signatures)
    h = h + _L1_ffn_ref(_layernorm(h, axis=-1), L1_ffn_w_freq_real, L1_ffn_w_freq_imag, L1_ffn_bias)
    return h

_drawn_inputs = setup_inputs


def setup_inputs(seed=0):
    import zlib

    import numpy as np

    out = dict(_drawn_inputs(seed))
    spreads = {'L0_tok_ln_gamma': (1.0, 0.2),
     'L0_tok_ln_beta': (0.0, 0.1),
     'L0_attn_ln_w': (1.0, 0.6),
     'L0_attn_ln_b': (0.0, 0.8),
     'L1_attn_bq': (0.0, 0.8),
     'L1_attn_bk': (0.0, 0.8),
     'L1_attn_bv': (0.0, 0.8),
     'L1_attn_bo': (0.0, 0.1),
     'L1_attn_b1': (0.0, 0.8),
     'L1_attn_b2': (0.0, 0.8)}
    factors = {'L0_attn_time_maa_x': 8.0,
     'L0_attn_time_maa': 3.598,
     'L0_attn_maa_w1': 8.0,
     'L0_attn_maa_w2': 8.0,
     'L0_attn_decay_w1': 8.0,
     'L0_attn_decay_w2': 8.0,
     'L0_attn_aaa_w1': 8.0,
     'L0_attn_aaa_w2': 8.0,
     'L0_attn_kkk_w1': 8.0,
     'L0_attn_kkk_w2': 7.598,
     'L0_attn_ma_w1': 8.0,
     'L0_attn_ma_w2': 8.0,
     'L0_attn_mk_w1': 8.0,
     'L0_attn_mk_w2': 8.0,
     'L0_attn_time_decay': 4.854,
     'L0_attn_time_faaaa': 8.0,
     'L0_attn_time_aaaaa': 8.0,
     'L0_attn_time_misc_a': 8.0,
     'L0_attn_time_misc_k': 8.0,
     'L0_ffn_base_b': 3.116,
     'L0_ffn_routed_A': 3.523,
     'L0_ffn_routed_B': 3.416,
     'L0_ffn_router_W': 4.23,
     'L0_ffn_router_b': 8.0,
     'L1_attn_Wq': 8.0,
     'L1_attn_Wk': 8.0,
     'L1_attn_Wv': 8.0,
     'L1_attn_Wo': 8.0,
     'L1_attn_W1': 8.0,
     'L1_attn_W2': 8.0,
     'L1_attn_head_signatures': 8.0,
     'L1_ffn_bias': 7.455}
    for name, (base, spread) in spreads.items():
        noise = np.random.default_rng([zlib.crc32(name.encode()), seed]).standard_normal(out[name].shape)
        drawn = base * np.exp(spread * noise) if base else spread * noise
        out[name] = jnp.asarray(drawn.astype(out[name].dtype))
    for name, factor in factors.items():
        out[name] = (out[name] * factor).astype(out[name].dtype)
    return out
```

```python
import math
from contextlib import ExitStack

import concourse.bass as bass
from concourse import mybir

P = 128
B, T_IN, C_IN = 16, 750, 64
D = 256
KT, STRIDE, KG, PAD = 32, 4, 9, 4
T = (T_IN - KT) // STRIDE + 1
TC = 30
CHUNKS = T // TC
N = TC * B
SM = STRIDE * (TC - 1) + KT
SM1 = P - (KG - 1)
SM2 = SM - SM1
XROWS2 = SM2 + KG - 1
HEADS, HS = 16, 16
EXPERTS, RANK = 6, 16
TILES = [(0, 128), (128, 128), (256, 128), (384, 96)]
NT = len(TILES)
NEG = -1.0e30
BANK_T = 15
UN = 3
NORMS = 6
SMALL = 21

F32 = mybir.dt.float32
BF16 = mybir.dt.bfloat16
ALU = mybir.AluOpType
ACT = mybir.ActivationFunctionType
AX = mybir.AxisListType.X
LN_EXP = "natural_log_exp_and_others"

PACK = [
    ("w_temporal", KT), ("w_proj", D), ("gauss", SM1), ("ident", P), ("b_proj", 2), ("ln_gamma", 2), ("ln_beta", 2),
    ("ones256", P), ("head_ones", P), ("head_mean", P), ("scan_mask", N * 2),
    ("maa_x", 2), ("maa", 8), ("maa_w1", 2 * 128), ("maa_w2", D), ("wa_w1", 2 * 112), ("wa_w2", D),
    ("k_w1", 2 * 48), ("k_w2", D), ("gate_w1", 2 * 128), ("gate_w2", D), ("Wr", 2 * D), ("Wk", 2 * D), ("Wv", 2 * D),
    ("Wo", 2 * D), ("decay", 2), ("faaaa", 2), ("aaaaa", 2), ("misc_a", 2), ("misc_k", 2), ("ln_w", 2), ("ln_b", 2),
    ("base_W", 2 * D), ("base_b", 2), ("shared_A", D), ("shared_B", D), ("routed_A", 2 * 96), ("routed_B", D),
    ("router_W", 2 * 6), ("router_b", 6), ("expert_before", 36),
    ("Wq1", 2 * D), ("Wk1", 2 * D), ("Wv1", 2 * D), ("Wo1", 2 * D), ("W1", 2 * D), ("W2", 2 * 64), ("sig", 16),
    ("bq", 2), ("bk", 2), ("bv", D), ("bo", 2), ("b1", 2), ("b2", 1), ("head_mask", 8),
    ("pair_ind", P), ("pair_neg", 512), ("ones_row", P), ("f_bias", D),
]
SETUP = [("wfr", 2 * D), ("wfi", 2 * D), ("Fr", 2 * D), ("Fi", 2 * D), ("nFi", 2 * D), ("Gr", 2 * D), ("nGi", 2 * D)]


def offsets(pack):
    at, out = 0, {}
    for name, n in pack:
        out[name] = (at, n)
        at += n
    return out, at


def tower(nc: bass.Bass, x: bass.AP, params: bass.AP, dft: bass.AP, out: bass.AP):
    where, n_params = offsets(PACK)
    where_s, n_setup = offsets(SETUP)
    ctx = ExitStack()
    with ctx:
        def sb(name, shape, dt=F32):
            return ctx.enter_context(nc.sbuf_tensor(name, shape, dt))

        def pb(name, shape, dt=F32):
            return ctx.enter_context(nc.psum_tensor(name, shape, dt))

        sems = {}

        def s(name):
            if name not in sems:
                sems[name] = ctx.enter_context(nc.semaphore("s_" + name))
            return sems[name]

        state = pb("state", [P, 2, 512])
        pp = pb("pp", [P, 6, 512])
        PA, PB, PC = pp[:, 0:2, 0:N], pp[:, 2:4, 0:N], pp[:, 4:6, 0:N]

        u = pp[:, 4, 0:32].rearrange("p (a i) -> p a i", a=2)
        prm = sb("prm", [P, n_params])

        def w(name, rows=P, r0=0):
            a, n = where[name]
            return prm[r0:r0 + rows, a:a + n]

        def w2(name, half, rows=P, r0=0):
            a, n = where[name]
            return prm[r0:r0 + rows, a + half * (n // 2):a + (half + 1) * (n // 2)]

        def col(name, k=0, rows=P, r0=0):
            a, _ = where[name]
            return prm[r0:r0 + rows, a + k:a + k + 1]

        diag = sb("diag", [P, KT, P])
        baseW = sb("baseW", [P, 2, D])
        dftM = sb("dftM", [P, 2, D])
        indb = sb("indb", [2, P], BF16)
        negb = sb("negb", [2, 512], BF16)
        bqs = sb("bqs", [P, 2])
        bkm = sb("bkm", [P, 2, 8])
        half_c = sb("half_c", [P, 1])
        zero_c = sb("zero_c", [P, 1])
        eps_c = sb("eps_c", [P, 3])

        x1 = sb("x1", [P, B * C_IN])
        x2 = sb("x2", [XROWS2, B * C_IN])
        Xs = sb("Xs", [P, 8, SM])
        Xc = sb("Xc", [P, TC * 8])

        def act_t(name):
            return sb(name, [P, 2, N])

        H = act_t("H")
        XN = sb("XN", [P, 2, B + N])
        xc, sq = act_t("xc"), act_t("sq")
        xxb = sb("xxb", [P, 1024])
        xx = xxb[:, 0:2 * N].rearrange("p (a n) -> p a n", a=2)
        xn = act_t("xn")
        rstd = sb("rstd", [P, N])
        arena = sb("arena", [P, 16 * 960])
        Mq = arena[:, 0:BANK_T * 512].rearrange("p (t a i j) -> p t a i j", a=2, i=HS, j=HS)

        def ar(k, n=1):
            return arena[:, k * 960:(k + n) * 960].rearrange("p (a n) -> p a n", a=2 * n)

        (xrg, xwa, xk, xv, tmp0, tmp1, K0, ga, gma, gmk, mz, nz, t1, kk, k2, Pinv) = [ar(k) for k in range(16)]
        tmps = [tmp0, tmp1]
        xm = [xrg, xwa, xk, xv]
        R, V, GR = act_t("R"), act_t("V"), sb("GR", [P, 4 * N])
        G, RKV = [GR[:, k * 2 * N:(k + 1) * 2 * N].rearrange("p (a n) -> p a n", a=2) for k in range(2)]
        Pd = sb("Pd", [P, 2, B + N])
        low = sb("low", [P, N])
        l_wa = sb("l_wa", [112, N])
        l_k = sb("l_k", [48, N])
        l_g = sb("l_g", [P, N])
        ld = arena[:, 5 * 960:6 * 960]
        cum = arena[:, 3 * 960:4 * 960]
        A_s, B_s, K_s, Q_s, V_s = [arena[:, k * 960:(k + 1) * 960].rearrange("p (t a i) -> p t a i", a=2, i=HS)
                                   for k in range(8, 13)]
        P_s = sb("P_s", [P, 2, HS])
        S_sb = sb("S_sb", [P, 2, HS, HS])
        steps_sb = sb("steps_sb", [P, (2 + UN) * 512])
        Ma, ub = [steps_sb[:, k * 512:(k + 1) * 512].rearrange("p (a i j) -> p a i j", a=2, i=HS) for k in range(2)]
        vk = steps_sb[:, 1024:].rearrange("p (t a i j) -> p t a i j", a=2, i=HS, j=HS)
        arena_rst = ar(0)
        kx = ar(0, 8).rearrange("p (a h) n -> p a h n", a=2)
        q1 = ar(8)
        hid = ar(9)
        PT = [arena[:, 10560 + i * 2048:10560 + (i + 1) * 2048].rearrange("p (h n) -> p h n", h=16) for i in range(2)]
        P1 = GR[:, 0:1024].rearrange("p (k h n) -> p k h n", k=2, n=32)
        Vx = steps_sb[:, 0:2048].rearrange("p (i a b n) -> p i a b n", i=NT, a=8, b=2)
        lg = sb("lg", [P, NT, 6])
        fs = [sb(f"fs{i}", [P, NT, 6]) for i in range(4)]
        f1 = [sb(f"f1{i}", [P, NT, 1]) for i in range(4)]
        cmp1 = sb("cmp1", [P, NT, 6, 6])
        cmp2 = sb("cmp2", [P, NT, 6, 6])
        sw96 = xxb[:, 0:NT * 96].rearrange("p (i e r) -> p i e r", i=NT, e=6)
        h96 = low[0:96, :]
        hl = sb("hl", [P, NT, 16])
        hl2 = sb("hl2", [P, NT, 16])
        mx = sb("mx", [P, NT, 16])
        Z = sb("Z", [P, NT, 16])
        gz = xxb[:, :].rearrange("p (i h d) -> p i h d", i=NT, h=16)
        tsg = l_g[0:64, :]
        Gx, O = R, V
        Out = GR[:, 0:NT * D].rearrange("p (i n) -> p i n", i=NT)

        def ws(name, half):
            a, n = where_s[name]
            return arena[:, a + half * D:a + (half + 1) * D]

        At = [Xs[:, :, :].rearrange("p a n -> p (a n)")[:, 0:512].rearrange("p (a n) -> p a n", a=2),
              Xs[:, :, :].rearrange("p a n -> p (a n)")[:, 512:1024].rearrange("p (a n) -> p a n", a=2)]

        xw = x.rearrange("(n s) c -> n s c", s=1)
        block = ctx.enter_context(nc.Block())

        def tb(ap):
            return ap.rearrange("p a (t b) -> p a t b", b=B)

        def bh(ap):
            return ap.unsqueeze(1).broadcast_to([P, 2, N])

        @block.sync
        def _(sp):
            sp.dma_start(prm[:, :], params).then_inc(s("params_in"), 16)
            sp.dma_start(arena[:, 0:n_setup], dft).then_inc(s("dft_in"), 16)
            with sp.Fori(0, CHUNKS) as c:
                sp.wait_ge(s("smooth_ps"), c)
                sp.dma_start(x1[:, :], x[bass.ds(c * (STRIDE * TC), P), :]).then_inc(s("x_in"), 16)
                sp.dma_start(x2[:, :], x[bass.ds(c * (STRIDE * TC) + SM1, XROWS2), :]).then_inc(s("x_in"), 16)
                sp.wait_ge(s("out_sb"), c + 1)
                for i, (t0, n) in enumerate(TILES):
                    dst = out.rearrange("b t c -> t b c")[bass.ds(c * TC + t0 // B, n // B)]
                    sp.dma_start(dst, Out[0:n, i, :]).then_inc(s("out_dram"), 16)
            sp.wait_ge(s("out_dram"), 16 * NT * CHUNKS)

        @block.tensor
        def _(pe):
            mm = nc.tensor.matmul
            ident = w("ident")
            pe.wait_ge(s("params_in"), 16)
            pe.wait_ge(s("dft_in"), 16)
            for h in range(2):
                last = mm(pp[:, 0, h * D:(h + 1) * D], w("shared_A", 16)[:, h * P:(h + 1) * P], w("shared_B", 16),
                          start=True, stop=True)
            last.then_inc(s("fold_ps"), 1)
            for im in range(2):
                for m in range(2):
                    for k in range(2):
                        first, second = (("wfr", "Fr"), ("wfi", "nFi")) if im == 0 else (("wfi", "Fr"), ("wfr", "Fi"))
                        mm(pp[:, 1 + im, m * D:(m + 1) * D], ws(first[0], k)[:, m * P:(m + 1) * P], ws(first[1], k),
                           start=(k == 0), stop=False)
                        last = mm(pp[:, 1 + im, m * D:(m + 1) * D], ws(second[0], k)[:, m * P:(m + 1) * P],
                                  ws(second[1], k), start=False, stop=(k == 1))
            last.then_inc(s("fw_ps"), 1)
            pe.wait_ge(s("fw_sb"), 1)
            for m in range(2):
                for k in range(2):
                    mm(pp[:, 3, m * D:(m + 1) * D], At[0][:, k, m * P:(m + 1) * P], ws("Gr", k),
                       start=(k == 0), stop=False)
                    last = mm(pp[:, 3, m * D:(m + 1) * D], At[1][:, k, m * P:(m + 1) * P], ws("nGi", k),
                              start=False, stop=(k == 1))
            last.then_inc(s("dftM_ps"), 1)
            pe.wait_ge(s("setup"), 1)
            pe.wait_ge(s("setup_act"), 1)

            def stats(src, dst, sem):
                mm(dst, w("ones256"), src[:, 0, :], start=True, stop=False)
                mm(dst, w("ones256"), src[:, 1, :], start=False, stop=True).then_inc(sem, 1)

            def dense(dst, wt, src, sem, m=P):
                for h in range(2):
                    for k in range(2):
                        last = mm(dst[:, h, :], w2(wt, k)[:, h * P:h * P + m], src[:, k, :],
                                  start=(k == 0), stop=(k == 1))
                last.then_inc(sem, 1)

            def lowrank(dst, wt, src, sem):
                for k in range(2):
                    last = mm(dst, w2(wt, k), src[:, k, :], start=(k == 0), stop=(k == 1))
                last.then_inc(sem, 1)

            def expand(dst, wt, r0, rows, src, sem):
                for h in range(2):
                    last = mm(dst[:, h, :], w(wt, rows, r0)[:, h * P:(h + 1) * P], src[r0:r0 + rows, :],
                              start=True, stop=True)
                last.then_inc(sem, 1)

            def per_head(dst, ones, src, sem):
                for h in range(2):
                    last = mm(dst[:, h, :], w(ones), src[:, h, :], start=True, stop=True)
                last.then_inc(sem, 1)

            with pe.Fori(0, CHUNKS) as c:
                pe.wait_ge(s("x_in"), c * 32 + 32)
                pe.wait_ge(s("O_sb"), c)
                pe.wait_ge(s("l1_res"), c)
                pe.wait_ge(s("ln4_xn"), c)
                for b in range(8):
                    dst = pp[:, b // 3, (b % 3) * SM:(b % 3 + 1) * SM]
                    mm(dst[:, 0:SM1], x1[:, b * P:(b + 1) * P], w("gauss"), start=True, stop=True)
                    last = mm(dst[:, SM1:SM], x2[:, b * P:(b + 1) * P], w("gauss", XROWS2)[:, 0:SM2],
                              start=True, stop=True)
                last.then_inc(s("smooth_ps"), 1)
                pe.wait_ge(s("smooth_sb"), c + 1)
                pe.wait_ge(s("out_sb"), c)
                for k in range(KT):
                    last = mm(pp[:, 4, 0:TC * 8], diag[:, k, :],
                              Xs[:, :, k:k + STRIDE * (TC - 1) + 1:STRIDE].rearrange("p a t -> p t a"),
                              start=(k == 0), stop=(k == KT - 1))
                last.then_inc(s("conv_ps"), 1)
                pe.wait_ge(s("conv_sb"), c + 1)
                for h in range(2):
                    for g in range(2):
                        last = mm(pp[:, 2 * g + h, 0:TC * 8], w("w_proj", 64, 64 * g)[:, h * P:(h + 1) * P],
                                  Xc[64 * g:64 * g + 64, :], start=True, stop=True)
                last.then_inc(s("proj_ps"), 1)
                pe.wait_ge(s("proj_sb"), c + 1)
                stats(H, pp[:, 2, 0:N], s("ln_mean"))
                pe.wait_ge(s("ln_sq"), c * NORMS + 1)
                stats(sq, pp[:, 3, 0:N], s("ln_var"))
                pe.wait_ge(s("h0"), c + 1)
                stats(H, pp[:, 4, 0:N], s("ln_mean"))
                pe.wait_ge(s("ln_sq"), c * NORMS + 2)
                stats(sq, pp[:, 5, 0:N], s("ln_var"))
                pe.wait_ge(s("mix"), c + 1)
                lowrank(pp[:, 2, 0:N], "maa_w1", xn, s("lo_ps"))
                pe.wait_ge(s("lo_sb"), c + 1)
                for g in range(4):
                    if g >= 2:
                        pe.wait_ge(s("tmp"), c * 4 + g - 1)
                    expand([PA, PC][g % 2], "maa_w2", 32 * g, 32, low, s("lo2_ps"))
                pe.wait_ge(s("xm"), c * 4 + 2)
                lowrank(pp[0:112, 2, 0:N], "wa_w1", xwa, s("wa_ps"))
                pe.wait_ge(s("xm"), c * 4 + 3)
                lowrank(pp[0:48, 3, 0:N], "k_w1", xk, s("k1_ps"))
                lowrank(pp[:, 0, 0:N], "gate_w1", xrg, s("g1_ps"))
                pe.wait_ge(s("xm"), c * 4 + 4)
                dense(PC, "Wr", xrg, s("r_ps"))
                pe.wait_ge(s("g1_sb"), c + 1)
                dense(PA, "Wk", xk, s("k_ps"))
                pe.wait_ge(s("k1_sb"), c + 1)
                pe.wait_ge(s("wa_sb"), c + 1)
                dense(PB, "Wv", xv, s("v_ps"))
                pe.wait_ge(s("r_sb"), c + 1)
                expand(PC, "wa_w2", 64, 16, l_wa, s("a_ps"))
                pe.wait_ge(s("k_sb"), c + 1)
                expand(PA, "wa_w2", 96, 16, l_wa, s("ma_ps"))
                pe.wait_ge(s("v_sb"), c + 1)
                expand(PB, "wa_w2", 0, 64, l_wa, s("z_ps"))
                pe.wait_ge(s("a_sb"), c + 1)
                expand(PC, "k_w2", 32, 16, l_k, s("mk_ps"))
                pe.wait_ge(s("ma_sb"), c + 1)
                expand(PA, "k_w2", 0, 16, l_k, s("kkl_ps"))
                pe.wait_ge(s("z_sb"), c + 1)
                pe.wait_ge(s("z_abs"), c + 1)
                for h in range(2):
                    last = mm(PB[:, h, :], w("gate_w2")[:, h * P:(h + 1) * P], l_g[:, :], start=True, stop=True)
                last.then_inc(s("g_ps"), 1)
                pe.wait_ge(s("mk_sb"), c + 1)
                pe.wait_ge(s("kk_sq"), c + 1)
                per_head(PC, "head_ones", sq, s("ss_ps"))
                pe.wait_ge(s("rkp"), c + 1)
                per_head(PA, "head_ones", xx, s("rk_ps"))
                pe.wait_ge(s("g_sb"), c + 1)
                pe.wait_ge(s("S_sb"), c + 1)
                for hh in range(2):
                    mm(state[:, hh, 0:256], ident, S_sb[:, hh, :, :], start=True, stop=False,
                       skip_group_check=True).then_inc(s(f"upd{hh}"), 1)
                for bank in range(2):
                    with pe.Fori(0, BANK_T // UN) as i:
                        for q in range(UN):
                            t = i * UN + (bank * BANK_T + q)
                            for hh in range(2):
                                pe.wait_ge(s("vk"), c * TC + t + 1)
                                pe.wait_ge(s(f"Ma{hh}"), c * TC + t + 1)
                                mm(state[:, hh, 0:256], ident, vk[:, q, hh, :, :], start=False, stop=False,
                                   skip_group_check=True)
                            for hh in range(2):
                                pe.wait_ge(s(f"ub{hh}"), c * TC + t + 1)
                                mm(state[:, hh, 0:256], ident, ub[:, hh, :, :], start=False, stop=False,
                                   skip_group_check=True).then_inc(s(f"upd{hh}"), 1)
                        pe.wait_ge(s("Mq"), c * TC + i * UN + (bank * BANK_T + UN))
                        for j in range(HS):
                            last = mm(PB[:, bank, bass.ds(i * (UN * 32), UN * 32)], ident,
                                      Mq[:, bass.ds(i * UN, UN), :, :, j], start=(j == 0), stop=(j == HS - 1))
                        last.then_inc(s("y_ps"), 1)
                pe.wait_ge(s("y_ch"), c + 1)
                per_head(PC, "head_mean", xn, s("ln_mean"))
                pe.wait_ge(s("ln_sq"), c * NORMS + 3)
                per_head(PA, "head_mean", sq, s("ln_var"))
                pe.wait_ge(s("y_gated"), c + 1)
                dense(PB, "Wo", xn, s("wo_ps"))
                pe.wait_ge(s("h1"), c + 1)
                stats(H, pp[:, 4, 0:N], s("ln_mean"))
                pe.wait_ge(s("ln_sq"), c * NORMS + 4)
                stats(sq, pp[:, 5, 0:N], s("ln_var"))
                pe.wait_ge(s("ln2_xn"), c + 1)
                for i, (t0, n) in enumerate(TILES):
                    dst = pp[0:n, 0, 8 * i:8 * i + 6]
                    for k in range(2):
                        mm(dst, xn[:, k, t0:t0 + n], w2("router_W", k), start=(k == 0), stop=False)
                    last = mm(dst, w("ones_row", 1)[:, 0:n], w("router_b", 1), start=False, stop=True)
                last.then_inc(s("router_ps"), 1)
                lowrank(pp[0:96, 1, 0:N], "routed_A", xn, s("h96_ps"))
                for h in range(2):
                    for k in range(2):
                        mm(PB[:, h, :], baseW[:, k, h * P:(h + 1) * P], xn[:, k, :], start=(k == 0), stop=False,
                           skip_group_check=True)
                pe.wait_ge(s("sw96"), c + 1)
                for i, (t0, n) in enumerate(TILES):
                    last = mm(pp[0:96, 4, t0:t0 + n], sw96[0:n, i, :, :], ident[0:n, 0:n], start=True, stop=True)
                last.then_inc(s("w96_ps"), 1)
                pe.wait_ge(s("hw"), c + 1)
                for h in range(2):
                    last = mm(PB[:, h, :], w("routed_B", 96)[:, h * P:(h + 1) * P], h96[:, :], start=False, stop=True,
                              skip_group_check=True)
                last.then_inc(s("ffn_ps"), 1)
                pe.wait_ge(s("h2"), c + 1)
                stats(H, pp[:, 0, 0:N], s("ln_mean"))
                pe.wait_ge(s("ln_sq"), c * NORMS + 5)
                stats(sq, pp[:, 1, 0:N], s("ln_var"))
                pe.wait_ge(s("ln3_xn"), c + 1)
                dense(PC, "W1", xn, s("hid_ps"))
                dense(PA, "Wq1", xn, s("q_ps"))
                dense(PB, "Wk1", xn, s("k1b_ps"))
                pe.wait_ge(s("hid_sb"), c + 1)
                for k in range(2):
                    last = mm(pp[0:64, 4, 0:N], w2("W2", k), hid[:, k, :], start=(k == 0), stop=(k == 1))
                last.then_inc(s("tsg_ps"), 1)
                pe.wait_ge(s("q_sb"), c + 1)
                for i, (t0, n) in enumerate(TILES):
                    dst = pp[0:n, i // 2, (i % 2) * D:(i % 2 + 1) * D]
                    for k in range(2):
                        mm(dst, xn[:, k, t0:t0 + n], w2("Wv1", k), start=(k == 0), stop=False)
                    last = mm(dst, w("ones_row", 1)[:, 0:n], w("bv", 1), start=False, stop=True)
                last.then_inc(s("v1_ps"), 1)
                pe.wait_ge(s("tsg_sb"), c + 1)
                for i, (t0, n) in enumerate(TILES):
                    last = mm(pp[0:n, 5, 16 * i:16 * i + 16], tsg[:, t0:t0 + n], w("sig", 64), start=True, stop=True)
                last.then_inc(s("hl_ps"), 1)
                pe.wait_ge(s("kx"), c + 1)

                def av(i):
                    t0, n = TILES[i]
                    pe.wait_ge(s("PT"), c * NT + i + 1)
                    for h in range(16):
                        hp, hh = h // 2, h % 2
                        r = 32 * (hp % 4)
                        last = mm(pp[r:r + 32, hp // 4, t0:t0 + n], Vx[0:n, i, hp, hh, :], PT[i % 2][0:n, h, 0:n],
                                  start=(hh == 0), stop=(hh == 1), skip_group_check=True)
                    last.then_inc(s("av_ps"), 1)

                for i, (t0, n) in enumerate(TILES):
                    if i >= 2:
                        pe.wait_ge(s("P1"), c * NT + i - 1)
                    bank = pp[:, 2 + i % 2, :]
                    mm(bank[0:n, :], indb[:, 0:n], negb[:, :], start=True, stop=False, skip_group_check=True)
                    for qd in range(n // 32):
                        for h in range(2):
                            last = mm(bank[32 * qd:32 * qd + 32, h * 256:(h + 1) * 256],
                                      q1[:, h, t0 + 32 * qd:t0 + 32 * qd + 32],
                                      kx[:, h, :, t0 + 32 * qd:t0 + 32 * qd + 32], start=False, stop=True,
                                      skip_group_check=True)
                    last.then_inc(s("sc_ps"), 1)
                    if i == 0:
                        pe.wait_ge(s("Vx"), c + 1)
                    else:
                        av(i - 1)
                av(NT - 1)
                pe.wait_ge(s("gz"), c + 1)
                for h in range(2):
                    for i, (t0, n) in enumerate(TILES):
                        last = mm(pp[:, 4 + h, t0:t0 + n], gz[0:n, i, 8 * h:8 * h + 8, :], ident[0:n, 0:n],
                                  start=True, stop=True)
                last.then_inc(s("gx_ps"), 1)
                pe.wait_ge(s("O_sb"), c + 1)
                dense(PB, "Wo1", O, s("wo1_ps"))
                pe.wait_ge(s("l1_res"), c + 1)
                stats(H, pp[:, 0, 0:N], s("ln_mean"))
                pe.wait_ge(s("ln_sq"), c * NORMS + 6)
                stats(sq, pp[:, 1, 0:N], s("ln_var"))
                pe.wait_ge(s("ln4_xn"), c + 1)
                for i, (t0, n) in enumerate(TILES):
                    dst = pp[0:n, 4 + i // 2, (i % 2) * D:(i % 2 + 1) * D]
                    for k in range(2):
                        mm(dst, xn[:, k, t0:t0 + n], dftM[:, k, :], start=(k == 0), stop=False, skip_group_check=True)
                    for k in range(2):
                        mm(dst[:, k * P:(k + 1) * P], H[:, k, t0:t0 + n], ident, start=False, stop=False,
                           skip_group_check=True)
                    last = mm(dst, w("ones_row", 1)[:, 0:n], w("f_bias", 1), start=False, stop=True,
                              skip_group_check=True)
                last.then_inc(s("out_ps"), 1)

        @block.scalar
        def _(act):
            a = nc.scalar.activation
            act.wait_ge(s("params_in"), 16)
            a(bqs[:, :], w("bq"), ACT.Identity, scale=0.25)
            act.wait_ge(s("fw_ps"), 1)
            a(At[0], pp[:, 1, :], ACT.Identity)
            a(At[1], pp[:, 2, :], ACT.Identity).then_inc(s("fw_sb"), 1)
            act.wait_ge(s("dftM_ps"), 1)
            a(dftM[:, :, :], pp[:, 3, :], ACT.Identity).then_inc(s("setup_act"), 1)
            act.wait_ge(s("setup"), 1)
            act.wait_ge(s("setup_act"), 1)

            def halves(dst, src, f, sem, bias=None, scale=None):
                for h in range(2):
                    kw = {}
                    if bias is not None:
                        kw["bias"] = bias(h)
                    if scale is not None:
                        kw["scale"] = scale if isinstance(scale, float) else scale(h)
                    last = a(dst[:, h, :], src[:, h, :], f, **kw)
                last.then_inc(sem, 1)

            def inv_std(c, k, var, dst=rstd[:, :], eps=eps_c[:, 0:1]):
                act.wait_ge(s("ln_var"), c * NORMS + k + 1)
                a(dst, var, ACT.Ln, bias=eps).then_inc(s("ln_log"), 1)
                act.wait_ge(s("ln_log"), c * NORMS + k + 1)
                a(dst, dst, ACT.Exp, scale=-0.5).then_inc(s("ln_rstd"), 1)

            nc.scalar.preload_act_table_set(LN_EXP)
            with act.Fori(0, CHUNKS) as c:
                act.wait_ge(s("smooth_ps"), c + 1)
                a(Xs[:, 0:6, :], pp[:, 0:2, 0:3 * SM], ACT.Identity)
                a(Xs[:, 6:8, :], pp[:, 2, 0:2 * SM], ACT.Identity).then_inc(s("smooth_sb"), 1)
                act.wait_ge(s("conv_ps"), c + 1)
                a(Xc[:, :], pp[:, 4, 0:TC * 8], ACT.Identity).then_inc(s("conv_sb"), 1)
                act.wait_ge(s("proj_ps"), c + 1)
                act.wait_ge(s("out_ps"), c)
                for g in range(2):
                    for h in range(2):
                        last = a(tb(H[:, :, :])[:, h, :, 8 * g:8 * g + 8],
                                 pp[:, 2 * g + h, 0:TC * 8].rearrange("p (t b) -> p t b", b=8), ACT.Identity,
                                 bias=col("b_proj", h))
                last.then_inc(s("proj_sb"), 1)
                act.wait_ge(s("ln_xc"), c * NORMS + 1)
                a(sq[:, :, :], xc[:, :, :], ACT.Square).then_inc(s("ln_sq"), 1)
                inv_std(c, 0, pp[:, 3, 0:N])
                act.wait_ge(s("ln0_xn"), c + 1)
                halves(H, xn, ACT.Identity, s("h0"), bias=lambda h: col("ln_beta", h), scale=lambda h: col("ln_gamma", h))
                act.wait_ge(s("ln_xc"), c * NORMS + 2)
                a(sq[:, :, :], xc[:, :, :], ACT.Square).then_inc(s("ln_sq"), 1)
                inv_std(c, 1, pp[:, 5, 0:N])
                act.wait_ge(s("lo_ps"), c + 1)
                a(low[:, :], pp[:, 2, 0:N], ACT.Tanh).then_inc(s("lo_sb"), 1)
                act.wait_ge(s("wa_ps"), c + 1)
                a(l_wa[0:64, :], pp[0:64, 2, 0:N], ACT.Tanh)
                a(l_wa[64:112, :], pp[64:112, 2, 0:N], ACT.Identity).then_inc(s("wa_sb"), 1)
                act.wait_ge(s("k1_ps"), c + 1)
                a(l_k[0:16, :], pp[0:16, 3, 0:N], ACT.Tanh)
                a(l_k[32:48, :], pp[32:48, 3, 0:N], ACT.Identity).then_inc(s("k1_sb"), 1)
                act.wait_ge(s("g1_ps"), c + 1)
                a(l_g[:, :], pp[:, 0, 0:N], ACT.Tanh).then_inc(s("g1_sb"), 1)
                act.wait_ge(s("r_ps"), c + 1)
                a(R[:, :, :], PC, ACT.Identity).then_inc(s("r_sb"), 1)
                act.wait_ge(s("k_ps"), c + 1)
                a(K0, PA, ACT.Identity).then_inc(s("k_sb"), 1)
                act.wait_ge(s("v_ps"), c + 1)
                a(V[:, :, :], PB, ACT.Identity).then_inc(s("v_sb"), 1)
                act.wait_ge(s("a_ps"), c + 1)
                halves(ga, PC, ACT.Sigmoid, s("a_sb"), bias=lambda h: col("aaaaa", h))
                act.wait_ge(s("ma_ps"), c + 1)
                halves(gma, PA, ACT.Sigmoid, s("ma_sb"), bias=lambda h: col("misc_a", h))
                act.wait_ge(s("z_sb"), c + 1)
                halves(nz, PB, ACT.Abs, s("z_abs"), bias=lambda h: col("decay", h))
                act.wait_ge(s("mk_ps"), c + 1)
                halves(gmk, PC, ACT.Sigmoid, s("mk_sb"), bias=lambda h: col("misc_k", h))
                act.wait_ge(s("g_ps"), c + 1)
                act.wait_ge(s("out_dram"), c * (16 * NT))
                a(G[:, :, :], PB, ACT.Identity).then_inc(s("g_sb"), 1)
                act.wait_ge(s("kkr"), c + 1)
                a(sq[:, :, :], kk, ACT.Square).then_inc(s("kk_sq"), 1)
                nc.scalar.preload_act_table_set(LN_EXP)
                act.wait_ge(s("rn"), c + 1)
                a(xc[:, :, :], xc[:, :, :], ACT.Ln, scale=2.0 ** 30).then_inc(s("norm_log"), 1)
                act.wait_ge(s("norm_log"), c + 1)
                a(xc[:, :, :], xc[:, :, :], ACT.Exp, scale=-0.5, bias=eps_c[:, 2:3]).then_inc(s("norm"), 1)
                act.wait_ge(s("z_abs"), c + 1)
                a(nz, nz, ACT.Exp, scale=-1.0).then_inc(s("a_e1"), 1)
                act.wait_ge(s("a_e1"), c + 1)
                a(nz, nz, ACT.Ln, bias=1.0).then_inc(s("l1p"), 1)
                act.wait_ge(s("lsig"), c + 1)
                a(ld[:, :].rearrange("p (a b t) -> p a t b", a=2, t=TC), tb(mz), ACT.Exp,
                  bias=half_c[:, 0:1]).then_inc(s("ld"), 1)
                act.wait_ge(s("wm"), c + 1)
                a(t1, t1, ACT.Exp).then_inc(s("ek"), 1)
                act.wait_ge(s("cum"), c + 1)
                act.wait_ge(s("Pcopied"), c)
                cumv = cum[:, :].rearrange("p (a b t) -> p a t b", a=2, t=TC)
                a(tb(Pd[:, :, B:]), cumv, ACT.Exp, scale=-1.0)
                a(tb(Pinv), cumv, ACT.Exp).then_inc(s("Pd"), 1)
                act.wait_ge(s("ln_xc"), c * NORMS + 3)
                a(sq[:, :, :], xc[:, :, :], ACT.Square).then_inc(s("ln_sq"), 1)
                inv_std(c, 2, PA, arena_rst, eps_c[:, 1:2])
                act.wait_ge(s("gn_yn"), c + 1)
                halves(xx, xn, ACT.Identity, s("gn_aff"), bias=lambda h: col("ln_b", h), scale=lambda h: col("ln_w", h))
                act.wait_ge(s("ln_xc"), c * NORMS + 4)
                a(sq[:, :, :], xc[:, :, :], ACT.Square).then_inc(s("ln_sq"), 1)
                inv_std(c, 3, pp[:, 5, 0:N])
                act.wait_ge(s("h96_ps"), c + 1)
                a(h96[:, :], pp[0:96, 1, 0:N], ACT.Identity).then_inc(s("h96_sb"), 1)
                act.wait_ge(s("lg_sub"), c + 1)
                a(lg[:, :, :], lg[:, :, :], ACT.Exp).then_inc(s("lg_exp"), 1)
                act.wait_ge(s("ln_xc"), c * NORMS + 5)
                a(sq[:, :, :], xc[:, :, :], ACT.Square).then_inc(s("ln_sq"), 1)
                inv_std(c, 4, pp[:, 1, 0:N])
                act.wait_ge(s("hid_ps"), c + 1)
                halves(hid, PC, ACT.Relu, s("hid_sb"), bias=lambda h: col("b1", h))
                act.wait_ge(s("q_ps"), c + 1)
                halves(q1, PA, ACT.Identity, s("q_sb"), bias=lambda h: bqs[:, h:h + 1], scale=0.25)
                act.wait_ge(s("tsg_ps"), c + 1)
                a(tsg[:, :], pp[0:64, 4, 0:N], ACT.Identity, bias=col("b2", 0, 64)).then_inc(s("tsg_sb"), 1)
                act.wait_ge(s("k1b_ps"), c + 1)
                for h in range(2):
                    for hd in range(8):
                        last = a(kx[:, h, hd, :], PB[:, h, :], ACT.Identity, bias=bkm[:, h, hd:hd + 1],
                                 scale=col("head_mask", hd))
                last.then_inc(s("kx"), 1)
                act.wait_ge(s("hl_sub"), c + 1)
                a(hl[:, :, :], hl[:, :, :], ACT.Exp).then_inc(s("hl_exp"), 1)
                for i, (t0, n) in enumerate(TILES):
                    act.wait_ge(s("P1"), c * NT + i + 1)
                    a(P1[0:n, i % 2, :, :], P1[0:n, i % 2, :, :], ACT.Exp).then_inc(s("P1e"), 1)
                act.wait_ge(s("gx_ps"), c + 1)
                a(Gx[:, :, :], PC, ACT.Identity).then_inc(s("gx_sb"), 1)
                act.wait_ge(s("ln_xc"), c * NORMS + 6)
                a(sq[:, :, :], xc[:, :, :], ACT.Square).then_inc(s("ln_sq"), 1)
                inv_std(c, 5, pp[:, 1, 0:N])
                act.wait_ge(s("out_ps"), c + 1)
                a(Out[:, 0:3, :], pp[:, 4:6, :].rearrange("p a (b n) -> p (a b) n", b=2)[:, 0:3, :], ACT.Identity)
                a(Out[0:96, 3, :], pp[0:96, 5, 256:512], ACT.Identity).then_inc(s("out_sb"), 1)

        @block.vector
        def _(dve):
            v = nc.vector
            tt_, stt, ts = v.tensor_tensor, v.scalar_tensor_tensor, v.tensor_scalar
            v.memset(XN[:, :, :], 0.0)
            v.memset(S_sb[:, :, :, :], 0.0)
            v.memset(Pd[:, :, 0:B], 1.0)
            v.memset(half_c[:, :], -0.5)
            v.memset(eps_c[:, 0:1], 1e-5)
            v.memset(eps_c[:, 1:2], 6.4e-4)
            v.memset(eps_c[:, 2:3], 15.0 * math.log(2.0))
            v.memset(lg[:, :, :], 0.0)
            v.memset(hl[:, :, :], 0.0)
            v.memset(Z[:, :, :], 1.0)
            dve.wait_ge(s("params_in"), 16)
            tt_(diag[:, :, :], w("ident").unsqueeze(1).broadcast_to([P, KT, P]),
                w("w_temporal").unsqueeze(2).broadcast_to([P, KT, P]), ALU.mult)
            for h in range(2):
                ts(bkm[:, h, :], w("head_mask"), col("bk", h), None, ALU.mult)
            v.tensor_copy(indb[:, :], w("pair_ind", 2))
            v.tensor_copy(negb[:, :], w("pair_neg", 2))
            dve.wait_ge(s("fold_ps"), 1)
            tt_(baseW[:, :, :], pp[:, 0, :], w("base_W"), ALU.add).then_inc(s("setup"), 1)
            dve.wait_ge(s("setup"), 1)
            dve.wait_ge(s("setup_act"), 1)

            def norm(c, k, src, mean, dst, pairwise=False, rst=None):
                r = rst if rst is not None else rstd[:, :]
                dve.wait_ge(s("ln_mean"), c * NORMS + k + 1)
                tt_(xc[:, :, :], src, mean if pairwise else bh(mean), ALU.subtract).then_inc(s("ln_xc"), 1)
                dve.wait_ge(s("ln_rstd"), c * NORMS + k + 1)
                dve.wait_ge(s("ln_xc"), c * NORMS + k + 1)
                return tt_(dst, xc[:, :, :], r if pairwise else bh(r), ALU.mult)

            with dve.Fori(0, CHUNKS) as c:
                dve.wait_ge(s("proj_sb"), c + 1)
                norm(c, 0, H[:, :, :], pp[:, 2, 0:N], xn[:, :, :]).then_inc(s("ln0_xn"), 1)
                v.tensor_copy(XN[:, :, 0:B], XN[:, :, N:N + B]).then_inc(s("carry"), 1)
                dve.wait_ge(s("h0"), c + 1)
                dve.wait_ge(s("carry"), c + 1)
                norm(c, 1, H[:, :, :], pp[:, 4, 0:N], XN[:, :, B:]).then_inc(s("ln1_xn"), 1)
                dve.wait_ge(s("ln1_xn"), c + 1)
                tt_(xx[:, :, :], XN[:, :, 0:N], XN[:, :, B:], ALU.subtract).then_inc(s("xx"), 1)
                dve.wait_ge(s("xx"), c + 1)
                for h in range(2):
                    last = stt(out=xn[:, h, :], in0=xx[:, h, :], scalar=col("maa_x", h), in1=XN[:, h, B:],
                               op0=ALU.mult, op1=ALU.add)
                last.then_inc(s("mix"), 1)
                for g in range(4):
                    src = [PA, PC][g % 2]
                    dve.wait_ge(s("lo2_ps"), c * 4 + g + 1)
                    if g >= 2:
                        dve.wait_ge(s("xm"), c * 4 + g - 1)
                    for h in range(2):
                        last = stt(out=tmps[g % 2][:, h, :], in0=src[:, h, :], scalar=col("maa", 2 * g + h),
                                   in1=xx[:, h, :], op0=ALU.add, op1=ALU.mult)
                    last.then_inc(s("tmp"), 1)
                dve.wait_ge(s("z_ps"), c + 1)
                for h in range(2):
                    last = ts(mz[:, h, :], PB[:, h, :], col("decay", h), 0.0, ALU.add, ALU.min)
                last.then_inc(s("z_sb"), 1)
                dve.wait_ge(s("kkl_ps"), c + 1)
                dve.wait_ge(s("k_sb"), c + 1)
                tt_(kk, PA, K0, ALU.add).then_inc(s("kkr"), 1)
                dve.wait_ge(s("ss_ps"), c + 1)
                ts(xc[:, :, :], PC, 1e-24, None, ALU.max).then_inc(s("rn"), 1)
                dve.wait_ge(s("norm"), c + 1)
                dve.wait_ge(s("kk_sq"), c + 1)
                tt_(kk, kk, xc[:, :, :], ALU.mult).then_inc(s("kkn"), 1)
                dve.wait_ge(s("l1p"), c + 1)
                dve.wait_ge(s("z_sb"), c + 1)
                tt_(mz, mz, nz, ALU.subtract).then_inc(s("lsig"), 1)
                dve.wait_ge(s("lsig"), c + 1)
                dve.wait_ge(s("mk_sb"), c + 1)
                stt(out=t1, in0=mz, scalar=-0.5, in1=gmk, op0=ALU.add, op1=ALU.mult).then_inc(s("wm"), 1)
                dve.wait_ge(s("ld"), c + 1)
                v.tensor_tensor_scan(cum[:, :], w("scan_mask"), ld[:, :], 0.0, ALU.mult, ALU.add).then_inc(s("cum"), 1)
                dve.wait_ge(s("kmix"), c + 1)
                dve.wait_ge(s("ek"), c + 1)
                tt_(k2, k2, t1, ALU.mult).then_inc(s("k2"), 1)
                dve.wait_ge(s("k2"), c + 1)
                for h in range(2):
                    last = stt(out=xx[:, h, :], in0=R[:, h, :], scalar=col("faaaa", h), in1=k2[:, h, :],
                               op0=ALU.mult, op1=ALU.mult)
                last.then_inc(s("rkp"), 1)
                dve.wait_ge(s("Pd"), c + 1)
                tt_(xm[0], kk, Pd[:, :, 0:N], ALU.mult)
                tt_(xm[1], k2, Pinv, ALU.mult)
                tt_(xm[2], R[:, :, :], Pd[:, :, B:], ALU.mult)
                dve.wait_ge(s("bneg"), c + 1)
                stt(out=xm[3], in0=t1, scalar=-1.0, in1=Pinv, op0=ALU.mult, op1=ALU.mult).then_inc(s("scaled"), 1)
                dve.wait_ge(s("scaled"), c + 1)

                def to_scan(dst, src):
                    return v.transpose(dst.rearrange("p t a i -> p t (a i)"),
                                       src.rearrange("p a (t b) -> p t a b", b=B))

                to_scan(A_s[:, :, :, :], xm[0])
                to_scan(V_s[:, :, :, :], V[:, :, :])
                to_scan(K_s[:, :, :, :], xm[1]).then_inc(s("vk_in"), 1)
                to_scan(B_s[:, :, :, :], xm[3])
                to_scan(Q_s[:, :, :, :], xm[2])
                v.transpose(P_s[:, :, :].rearrange("p a i -> p (a i)"), Pd[:, :, N:N + B]).then_inc(s("Pcopied"), 1)
                dve.wait_ge(s("rk_ps"), c + 1)
                tt_(RKV[:, :, :], PA, V[:, :, :], ALU.mult).then_inc(s("rkv"), 1)
                v.tensor_copy(S_sb[:, 0, 0, 0:1], S_sb[:, 0, 0, 0:1]).then_inc(s("S_sb"), 1)

                def s_times(dst, hh, vec, t):
                    return tt_(dst, state[:, hh, 0:256].rearrange("p (i j) -> p i j", j=HS),
                               vec.unsqueeze(1).broadcast_to([P, HS, HS]), ALU.mult)

                def step(t, tm, k):
                    for hh in range(2):
                        dve.wait_ge(s(f"upd{hh}"), k + (c + 1))
                        s_times(Ma[:, hh, :, :], hh, A_s[:, t, hh, :], t).then_inc(s(f"Ma{hh}"), 1)
                    for hh in range(2):
                        dve.wait_ge(s(f"Ma{hh}"), k + 1)
                        v.tensor_reduce(u[:, hh, :], Ma[:, hh, :, :], AX, ALU.add).then_inc(s(f"u{hh}"), 1)
                    for hh in range(2):
                        dve.wait_ge(s(f"u{hh}"), k + 1)
                        tt_(ub[:, hh, :, :], u[:, hh, :].unsqueeze(2).broadcast_to([P, HS, HS]),
                            B_s[:, t, hh, :].unsqueeze(1).broadcast_to([P, HS, HS]), ALU.mult)\
                            .then_inc(s(f"ub{hh}"), 1)
                    for hh in range(2):
                        dve.wait_ge(s(f"upd{hh}"), k + (c + 2))
                        last = s_times(Mq[:, tm, hh, :, :], hh, Q_s[:, t, hh, :], t)
                    last.then_inc(s("Mq"), 1)

                for bank in range(2):
                    with dve.Fori(0, BANK_T // UN) as i:
                        dve.wait_ge(s("Pcopied"), c + 1)
                        if bank == 1:
                            dve.wait_ge(s("y_ps"), c * (2 * BANK_T // UN) + i + 1)
                        for q in range(UN):
                            t = i * UN + (bank * BANK_T + q)
                            step(t, i * UN + q, c * TC + t)
                for hh in range(2):
                    dve.wait_ge(s(f"upd{hh}"), c * (TC + 1) + (TC + 1))
                    last = s_times(S_sb[:, hh, :, :], hh, P_s[:, hh, :], 0)
                last.then_inc(s("S_next"), 1)
                dve.wait_ge(s("y_ps"), c * (2 * BANK_T // UN) + 2 * BANK_T // UN)
                v.transpose(tb(xn[:, :, :]).rearrange("p a t b -> p t a b"),
                            PB.rearrange("p g (t n) -> p g t n", n=32)).then_inc(s("y_ch"), 1)
                dve.wait_ge(s("y_ch"), c + 1)
                norm(c, 2, xn[:, :, :], PC, xn[:, :, :], True, arena_rst).then_inc(s("gn_yn"), 1)
                dve.wait_ge(s("gn_aff"), c + 1)
                tt_(xc[:, :, :], xx[:, :, :], RKV[:, :, :], ALU.add).then_inc(s("y_bonus"), 1)
                dve.wait_ge(s("y_bonus"), c + 1)
                tt_(xn[:, :, :], xc[:, :, :], G[:, :, :], ALU.mult).then_inc(s("y_gated"), 1)
                dve.wait_ge(s("wo_ps"), c + 1)
                tt_(H[:, :, :], PB, H[:, :, :], ALU.add).then_inc(s("h1"), 1)

                dve.wait_ge(s("h1"), c + 1)
                norm(c, 3, H[:, :, :], pp[:, 4, 0:N], xn[:, :, :]).then_inc(s("ln2_xn"), 1)
                steps = [0]

                def chain(ins):
                    steps[0] += 1
                    ins.then_inc(s("small"), 1)
                    dve.wait_ge(s("small"), c * SMALL + steps[0])

                def b6(ap):
                    return ap.broadcast_to([P, NT, 6])

                dve.wait_ge(s("router_ps"), c + 1)
                rl = pp[:, 0, 0:32].rearrange("p (a n) -> p a n", n=8)[:, :, 0:6]
                v.tensor_copy(lg[:, 0:3, :], rl[:, 0:3, :])
                chain(v.tensor_copy(lg[0:96, 3, :], rl[0:96, 3, :]))
                chain(v.tensor_reduce(f1[0][:, :, :], lg[:, :, :], AX, ALU.max))
                tt_(lg[:, :, :], lg[:, :, :], b6(f1[0][:, :, :]), ALU.subtract).then_inc(s("lg_sub"), 1)
                dve.wait_ge(s("lg_exp"), c + 1)
                chain(v.tensor_reduce(f1[1][:, :, :], lg[:, :, :], AX, ALU.add))
                chain(v.reciprocal(f1[2][:, :, :], f1[1][:, :, :]))
                gt = fs[0][:, :, :]
                chain(tt_(gt, lg[:, :, :], b6(f1[2][:, :, :]), ALU.mult))
                other = gt.unsqueeze(2).broadcast_to([P, NT, 6, 6])
                this = gt.unsqueeze(3).broadcast_to([P, NT, 6, 6])
                tt_(cmp1[:, :, :, :], other, this, ALU.is_gt)
                chain(tt_(cmp2[:, :, :, :], other, this, ALU.is_equal))
                chain(tt_(cmp2[:, :, :, :], cmp2[:, :, :, :],
                          w("expert_before").rearrange("p (a b) -> p a b", b=6).unsqueeze(1).broadcast_to([P, NT, 6, 6]),
                          ALU.mult))
                chain(tt_(cmp1[:, :, :, :], cmp1[:, :, :, :], cmp2[:, :, :, :], ALU.add))
                chain(v.tensor_reduce(fs[1][:, :, :], cmp1[:, :, :, :], AX, ALU.add))
                chain(stt(out=fs[2][:, :, :], in0=fs[1][:, :, :], scalar=1.5, in1=gt, op0=ALU.is_lt, op1=ALU.mult))
                chain(v.tensor_reduce(f1[3][:, :, :], fs[2][:, :, :], AX, ALU.add))
                chain(ts(f1[0][:, :, :], f1[3][:, :, :], 1e-6, None, ALU.add))
                chain(v.reciprocal(f1[1][:, :, :], f1[0][:, :, :]))
                chain(tt_(fs[3][:, :, :], fs[2][:, :, :], b6(f1[1][:, :, :]), ALU.mult))
                v.tensor_copy(sw96[:, :, :, :], fs[3][:, :, :].unsqueeze(3).broadcast_to([P, NT, 6, 16]))\
                    .then_inc(s("sw96"), 1)
                dve.wait_ge(s("w96_ps"), c + 1)
                dve.wait_ge(s("h96_sb"), c + 1)
                tt_(h96[:, :], h96[:, :], pp[0:96, 4, 0:N], ALU.mult).then_inc(s("hw"), 1)
                dve.wait_ge(s("ffn_ps"), c + 1)
                for h in range(2):
                    last = stt(out=H[:, h, :], in0=PB[:, h, :], scalar=col("base_b", h), in1=H[:, h, :],
                               op0=ALU.add, op1=ALU.add)
                last.then_inc(s("h2"), 1)

                dve.wait_ge(s("h2"), c + 1)
                norm(c, 4, H[:, :, :], pp[:, 0, 0:N], xn[:, :, :]).then_inc(s("ln3_xn"), 1)
                dve.wait_ge(s("v1_ps"), c + 1)
                dve.wait_ge(s("Vx0"), c + 1)
                for i, (t0, n) in enumerate(TILES):
                    src = pp[0:n, i // 2, (i % 2) * D:(i % 2 + 1) * D].rearrange("p (a b d) -> p a b d", b=2, d=16)
                    for hh in range(2):
                        last = v.tensor_copy(Vx[0:n, i, :, hh, 16 * hh:16 * hh + 16], src[:, :, hh, :])
                last.then_inc(s("Vx"), 1)
                dve.wait_ge(s("hl_ps"), c + 1)
                hp = pp[:, 5, 0:64].rearrange("p (a n) -> p a n", n=16)

                def b16(ap):
                    return ap.broadcast_to([P, NT, 16])

                v.tensor_copy(hl[:, 0:3, :], hp[:, 0:3, :])
                chain(v.tensor_copy(hl[0:96, 3, :], hp[0:96, 3, :]))
                chain(v.tensor_reduce(f1[0][:, :, :], hl[:, :, :], AX, ALU.max))
                tt_(hl[:, :, :], hl[:, :, :], b16(f1[0][:, :, :]), ALU.subtract).then_inc(s("hl_sub"), 1)
                v.memset(PT[0], 0.0)
                v.memset(PT[1], 0.0).then_inc(s("PT0"), 1)
                dve.wait_ge(s("hl_exp"), c + 1)
                chain(v.tensor_reduce(f1[1][:, :, :], hl[:, :, :], AX, ALU.add))
                chain(v.reciprocal(f1[2][:, :, :], f1[1][:, :, :]))
                chain(tt_(hl[:, :, :], hl[:, :, :], b16(f1[2][:, :, :]), ALU.mult))

                def scores(i):
                    t0, n = TILES[i]
                    sc = pp[0:n, 2 + i % 2, :].rearrange("p (h n) -> p h n", n=32)
                    dve.wait_ge(s("sc_ps"), c * NT + i + 1)
                    v.tensor_reduce(mx[0:n, i, :], sc, AX, ALU.max).then_inc(s("mx"), 1)
                    dve.wait_ge(s("mx"), c * NT + i + 1)
                    tt_(P1[0:n, i % 2, :, :], sc, mx[0:n, i, :].unsqueeze(2).broadcast_to([n, 16, 32]),
                        ALU.subtract).then_inc(s("P1"), 1)

                def turn(i):
                    t0, n = TILES[i]
                    dve.wait_ge(s("P1e"), c * NT + i + 1)
                    v.tensor_reduce(Z[0:n, i, :], P1[0:n, i % 2, :, :], AX, ALU.add).then_inc(s("Z"), 1)
                    if i >= 2:
                        dve.wait_ge(s("av_ps"), c * NT + i - 1)
                    dve.wait_ge(s("PT0"), c + 1)
                    for qd in range(n // 32):
                        r = slice(32 * qd, 32 * qd + 32)
                        last = v.transpose(PT[i % 2][r, :, r], P1[r, i % 2, :, :])
                    last.then_inc(s("PT"), 1)

                scores(0)
                for i in range(NT):
                    if i + 1 < NT:
                        scores(i + 1)
                    turn(i)
                dve.wait_ge(s("Z"), c * NT + NT)
                chain(v.reciprocal(hl2[:, :, :], Z[:, :, :]))
                chain(tt_(hl2[:, :, :], hl2[:, :, :], hl[:, :, :], ALU.mult))
                v.tensor_copy(gz[:, :, :, :], hl2[:, :, :].unsqueeze(3).broadcast_to([P, NT, 16, 16]))\
                    .then_inc(s("gz"), 1)
                dve.wait_ge(s("gx_sb"), c + 1)
                dve.wait_ge(s("av_ps"), c * NT + NT)
                tt_(O[:, :, :], PA, Gx[:, :, :], ALU.mult).then_inc(s("O_sb"), 1)
                dve.wait_ge(s("wo1_ps"), c + 1)
                for h in range(2):
                    last = stt(out=H[:, h, :], in0=PB[:, h, :], scalar=col("bo", h), in1=H[:, h, :],
                               op0=ALU.add, op1=ALU.add)
                last.then_inc(s("l1_res"), 1)
                dve.wait_ge(s("l1_res"), c + 1)
                norm(c, 5, H[:, :, :], pp[:, 0, 0:N], xn[:, :, :]).then_inc(s("ln4_xn"), 1)
                assert steps[0] == SMALL

        @block.gpsimd
        def _(pool):
            g_ = nc.gpsimd
            g_.memset(zero_c[:, :], 0.0).then_inc(s("zero"), 1)
            pool.wait_ge(s("zero"), 1)
            with pool.Fori(0, CHUNKS) as c:
                for g in range(4):
                    pool.wait_ge(s("tmp"), c * 4 + g + 1)
                    g_.tensor_tensor(xm[g], tmps[g % 2], XN[:, :, B:], ALU.add).then_inc(s("xm"), 1)
                pool.wait_ge(s("ma_sb"), c + 1)
                pool.wait_ge(s("a_sb"), c + 1)
                pool.wait_ge(s("lo2_ps"), c * 4 + 4)
                g_.tensor_tensor(tmp0, ga, gma, ALU.mult).then_inc(s("g_chain"), 1)
                pool.wait_ge(s("g_chain"), c * 3 + 1)
                g_.tensor_tensor(tmp0, ga, tmp0, ALU.subtract).then_inc(s("g_chain"), 1)
                pool.wait_ge(s("g_chain"), c * 3 + 2)
                g_.tensor_tensor(tmp0, gma, tmp0, ALU.add).then_inc(s("g_chain"), 1)
                pool.wait_ge(s("g_chain"), c * 3 + 3)
                pool.wait_ge(s("k_sb"), c + 1)
                g_.tensor_tensor(k2, K0, tmp0, ALU.mult).then_inc(s("kmix"), 1)
                pool.wait_ge(s("kkn"), c + 1)
                pool.wait_ge(s("k2"), c + 1)
                g_.tensor_tensor(t1, kk, ga, ALU.mult).then_inc(s("bneg"), 1)
                with pool.Fori(0, TC // UN) as i:
                    pool.wait_ge(s("vk_in"), c + 1)
                    for q in range(UN):
                        t = i * UN + q
                        pool.wait_ge(s("upd1"), c * (TC + 1) + i * UN + q)
                        for hh in range(2):
                            last = g_.tensor_tensor(vk[:, q, hh, :, :],
                                                    V_s[:, t, hh, :].unsqueeze(2).broadcast_to([P, HS, HS]),
                                                    K_s[:, t, hh, :].unsqueeze(1).broadcast_to([P, HS, HS]), ALU.mult)
                        last.then_inc(s("vk"), 1)
                pool.wait_ge(s("y_ps"), c * (2 * BANK_T // UN) + 2 * BANK_T // UN)
                zz = zero_c[:, 0:1].broadcast_to([P, 2048])
                g_.tensor_tensor(steps_sb[:, 0:2048], zz, zz, ALU.add).then_inc(s("Vx0"), 1)


def kernel(**inp):
    import numpy as np
    import concourse.bacc as bacc
    from concourse.bass_utils import run_bass_kernel_spmd

    f = {k: np.asarray(v) for k, v in inp.items()}
    where, n_params = offsets(PACK)
    where_s, n_setup = offsets(SETUP)
    prm = np.zeros((P, n_params), np.float32)
    dft = np.zeros((P, n_setup), np.float32)

    def put(name, a, r0=0, c0=0):
        at = where[name][0] + c0
        prm[r0:r0 + a.shape[0], at:at + a.shape[1]] = a

    def vec(name, a):
        put(name, a.reshape(2, P).T)

    def rows(name, a, c0=0, n=None):
        n = n or a.shape[1]
        put(name, a[0:P], 0, c0)
        put(name, a[P:2 * P], 0, n + c0)

    L0, F0, L1 = "L0_attn_", "L0_ffn_", "L1_attn_"
    wt = f["L0_tok_w_temporal"][:, 0, :]
    put("w_temporal", np.concatenate([wt, wt]))
    put("w_proj", np.concatenate([f["L0_tok_w_proj"].T, f["L0_tok_w_proj"].T]))
    tg = np.arange(KG, dtype=np.float32) - (KG - 1) / 2
    g = np.exp(-tg ** 2 / 8.0).astype(np.float32)
    g = g / g.sum()
    band = np.zeros((P, SM1), np.float32)
    for j in range(SM1):
        band[j:j + KG, j] = g
    put("gauss", band)
    put("ident", np.eye(P, dtype=np.float32))
    vec("b_proj", f["L0_tok_b_proj"])
    vec("ln_gamma", f["L0_tok_ln_gamma"])
    vec("ln_beta", f["L0_tok_ln_beta"])
    put("ones256", np.full((P, P), 1.0 / D, np.float32))
    same = np.kron(np.eye(8, dtype=np.float32), np.ones((16, 16), np.float32))
    put("head_ones", same)
    put("head_mean", same * np.float32(1.0 / HS))
    keep = np.ones((P, 2 * B, TC), np.float32)
    keep[:, :, 0] = 0.0
    put("scan_mask", keep.reshape(P, -1))
    vec("maa_x", f[L0 + "time_maa_x"])
    put("maa", f[L0 + "time_maa"].reshape(8, P).T)
    rows("maa_w1", f[L0 + "maa_w1"].T)
    put("maa_w2", f[L0 + "maa_w2"].reshape(P, D))
    rows("wa_w1", f[L0 + "decay_w1"].T, 0, 112)
    rows("wa_w1", f[L0 + "aaa_w1"].T, 64, 112)
    rows("wa_w1", f[L0 + "ma_w1"].T, 96, 112)
    put("wa_w2", f[L0 + "decay_w2"])
    put("wa_w2", f[L0 + "aaa_w2"], 64)
    put("wa_w2", f[L0 + "ma_w2"], 96)
    rows("k_w1", f[L0 + "kkk_w1"].T, 0, 48)
    rows("k_w1", f[L0 + "mk_w1"].T, 32, 48)
    put("k_w2", f[L0 + "kkk_w2"])
    put("k_w2", f[L0 + "mk_w2"], 32)
    rows("gate_w1", f[L0 + "gate_w1"].T)
    put("gate_w2", f[L0 + "gate_w2"])
    for nm in ("Wr", "Wk", "Wv", "Wo"):
        rows(nm, f[L0 + nm].T)
    for nm, src in (("decay", "time_decay"), ("faaaa", "time_faaaa"), ("aaaaa", "time_aaaaa"),
                    ("misc_a", "time_misc_a"), ("misc_k", "time_misc_k"), ("ln_w", "ln_w"), ("ln_b", "ln_b")):
        vec(nm, f[L0 + src])
    rows("base_W", f[F0 + "base_W"].T)
    vec("base_b", f[F0 + "base_b"])
    put("shared_A", f[F0 + "shared_A"])
    put("shared_B", f[F0 + "shared_B"].T)
    rows("routed_A", f[F0 + "routed_A"].reshape(96, D).T)
    put("routed_B", f[F0 + "routed_B"].transpose(0, 2, 1).reshape(96, D))
    rows("router_W", f[F0 + "router_W"].T)
    put("router_b", f[F0 + "router_b"].reshape(1, 6))
    put("expert_before", np.tile(np.tril(np.ones((6, 6), np.float32), -1).reshape(1, 36), (P, 1)))
    for nm, src in (("Wq1", "Wq"), ("Wk1", "Wk"), ("Wv1", "Wv"), ("Wo1", "Wo"), ("W1", "W1"), ("W2", "W2")):
        rows(nm, f[L1 + src].T)
    put("sig", f[L1 + "head_signatures"].T)
    for nm in ("bq", "bk", "bo", "b1"):
        vec(nm, f[L1 + nm])
    put("bv", f[L1 + "bv"].reshape(1, D))
    put("b2", f[L1 + "b2"].reshape(64, 1))
    put("head_mask", np.kron(np.eye(8, dtype=np.float32), np.ones((16, 1), np.float32)))
    who = (np.arange(P) // 16) % 2
    put("pair_ind", np.stack([who == 0, who == 1]).astype(np.float32))
    key = (np.arange(512) // 16) % 2
    put("pair_neg", np.stack([key != 0, key != 1]).astype(np.float32) * np.float32(NEG))
    put("ones_row", np.ones((1, P), np.float32))
    put("f_bias", f["L1_ffn_bias"].reshape(1, D))

    ang = 2.0 * np.pi * ((np.arange(D)[:, None] * np.arange(D)[None, :]) % D) / D
    mats = {"wfr": f["L1_ffn_w_freq_real"], "wfi": f["L1_ffn_w_freq_imag"],
            "Fr": np.cos(ang), "Fi": -np.sin(ang), "nFi": np.sin(ang),
            "Gr": np.cos(ang) / D, "nGi": -np.sin(ang) / D}
    for nm, m in mats.items():
        at = where_s[nm][0]
        dft[:, at:at + D] = m[0:P]
        dft[:, at + D:at + 2 * D] = m[P:2 * P]

    rows_x = STRIDE * TC * (CHUNKS - 1) + SM1 + XROWS2
    xp = np.zeros((rows_x, B * C_IN), np.float32)
    xp[PAD:PAD + T_IN] = f["x"].reshape(2, 8, T_IN, C_IN).transpose(2, 1, 0, 3).reshape(T_IN, B * C_IN)[:rows_x - PAD]

    nc = bacc.Bacc("TRN2", target_bir_lowering=False, num_devices=1)
    arrays = {"x_in": xp, "params_in": prm, "dft_in": dft}
    args = [nc.dram_tensor(k, a.shape, mybir.dt.from_np(a.dtype), kind="ExternalInput").ap() for k, a in arrays.items()]
    out = nc.dram_tensor("out", (B, T, D), F32, kind="ExternalOutput").ap()
    tower(nc, *args, out)
    r = run_bass_kernel_spmd(nc, [arrays], core_ids=[0])
    return r.results[0]["out"]
```

```python
import math
from contextlib import ExitStack

import concourse.bass as bass
from concourse import mybir

P = 128
B, T_IN, C_IN = 16, 750, 64
D = 256
KT, STRIDE, KG, PAD = 32, 4, 9, 4
T = (T_IN - KT) // STRIDE + 1
TC = 30
CHUNKS = T // TC
N = TC * B
SM = STRIDE * (TC - 1) + KT
SM1 = P - (KG - 1)
SM2 = SM - SM1
XROWS2 = SM2 + KG - 1
HEADS, HS = 16, 16
EXPERTS, RANK = 6, 16
TILES = [(0, 128), (128, 128), (256, 128), (384, 96)]
NT = len(TILES)
NEG = -1.0e30
BANK_T = 15
YG = 3
RING = 3
F_NORMS, B_NORMS = 2, 4
SMALL = 21

F32 = mybir.dt.float32
BF16 = mybir.dt.bfloat16
ALU = mybir.AluOpType
ACT = mybir.ActivationFunctionType
AX = mybir.AxisListType.X
LN_EXP = "natural_log_exp_and_others"


PACK = [
    ("w_temporal", KT), ("w_proj", D), ("gauss", SM1), ("ident", P), ("b_proj", 2), ("ln_gamma", 2), ("ln_beta", 2),
    ("ones256", P), ("head_ones", P), ("head_mean", P), ("scan_mask", N * 2),
    ("maa_x", 2), ("maa", 8), ("maa_w1", 2 * 128), ("maa_w2", D), ("wa_w1", 2 * 112), ("wa_w2", D),
    ("k_w1", 2 * 48), ("k_w2", D), ("gate_w1", 2 * 128), ("gate_w2", D), ("Wr", 2 * D), ("Wk", 2 * D), ("Wv", 2 * D),
    ("Wo", 2 * D), ("decay", 2), ("faaaa", 2), ("aaaaa", 2), ("misc_a", 2), ("misc_k", 2), ("ln_w", 2), ("ln_b", 2),
    ("base_W", 2 * D), ("base_b", 2), ("shared_A", D), ("shared_B", D), ("routed_A", 2 * 96), ("routed_B", D),
    ("router_W", 2 * 6), ("router_b", 6), ("expert_before", 36),
    ("Wq1", 2 * D), ("Wk1", 2 * D), ("Wv1", 2 * D), ("Wo1", 2 * D), ("W1", 2 * D), ("W2", 2 * 64), ("sig", 16),
    ("bq", 2), ("bk", 2), ("bv", D), ("bo", 2), ("b1", 2), ("b2", 1), ("head_mask", 8),
    ("pair_ind", P), ("pair_neg", 512), ("ones_row", P), ("f_bias", 2),
]
SETUP = [("wfr", 2 * D), ("wfi", 2 * D), ("Fr", 2 * D), ("Fi", 2 * D), ("nFi", 2 * D), ("Gr", 2 * D), ("nGi", 2 * D)]


def offsets(pack):
    at, out = 0, {}
    for name, n in pack:
        out[name] = (at, n)
        at += n
    return out, at

BACK = """y_turn gn_mean gn_xc zero0 gn_sq G gn_var gn_std gn_out gn_affine bonus gated Wo h1
    ln2_mean ln2_xc zero1 ln2_sq ln2_var ln2_std ln2_out router h96 router_max base h96_sb router_exp zero2 gates rank top2
    top2_sum w96 hw experts h2 ln3_mean ln3_xc ln3_sq ln3_var ln3_std ln3_out k q k_bias q_sb W1 hid W2 V tsg Vx kx0
    hl hl_max hl_exp sc0 hl_gate kx1 p0 sc1 e0 kx2 p1 t0 av0 sc2 e1 kx3 p2 t1 av1 sc3 e2 p3 t2 av2 e3 t3 av3 gz gx gx_sb
    O Wo1 h3 ln4_mean ln4_xc ln4_sq h_bias ln4_var res_h ln4_std ln4_out result result_sb""".split()
FRONT = """proj proj_sb ln0_mean ln0_xc ln0_sq ln0_var ln0_std ln0_out ln0_affine ln1_mean ln1_xc ln1_sq ln1_var
    ln1_std ln1_out xx mix lo lo_sb lo2_0 lo2_1 tmp0 xm0 tmp1 xm1 lo2_2 tmp2 xm2 lo2_3 wa wa_sb k1 tmp3 xm3 r k1_sb g1
    r_sb kp g1_sb vp k_sb a v_sb ma a_sb z ma_sb z_sb z_abs mk mix0 kkl mk_sb mix1 kkr kk_sq mix2 ss z_log kmix lsig
    wm rn ld norm cum ek kkn k2 rkp Pd kka rk scaled_a scaled_k scaled_q scaled_b rkv""".split()
CONV = ["smooth0", "smooth_sb0", "smooth1", "smooth_sb1"] + [f"tap{k}" for k in range(KT)]
SLOTS = 4 * TC


def spread(*stages):
    levels = [(name, level) for name, lv in stages for level in lv]
    return [(name, level, k * SLOTS // len(levels)) for k, (name, level) in enumerate(levels)]


def woven():
    plan, conv = [], list(CONV)
    begin = BACK.index("ln2_mean")
    levels = [("back", lv) for lv in BACK] + [("keep", "keep")] + [("front", lv) for lv in FRONT]
    n = len(levels)
    for k, (name, level) in enumerate(levels):
        at = k * SLOTS // n
        plan.append((name, level, at))
        if name == "back" and k >= begin and conv:
            plan.append(("conv", conv.pop(0), at))
    assert not conv
    return plan


PROLOGUE = spread(("conv", CONV), ("front", FRONT))
FIRST = spread(("keep", ["keep"]), ("conv", CONV), ("front", FRONT))
BODY = woven()
LAST = spread(("back", BACK), ("keep", ["keep"]))
EPILOGUE = spread(("back", BACK))


def tower(nc: bass.Bass, x: bass.AP, params: bass.AP, dft: bass.AP, out: bass.AP):
    where, n_params = offsets(PACK)
    where_s, n_setup = offsets(SETUP)
    ctx = ExitStack()
    with ctx:
        def sb(name, shape, dt=F32):
            return ctx.enter_context(nc.sbuf_tensor(name, shape, dt))

        def pb(name, shape, dt=F32):
            return ctx.enter_context(nc.psum_tensor(name, shape, dt))

        sems = {}

        def s(name):
            if name not in sems:
                sems[name] = ctx.enter_context(nc.semaphore("s_" + name))
            return sems[name]

        state = pb("state", [P, 2, 512])
        pp = pb("pp", [P, 4, 512])
        PA, PB = pp[:, 0:2, 0:N], pp[:, 2:4, 0:N]
        y_ps = pb("y_ps", [P, 512])
        u_ps = pb("u_ps", [P, 512])
        u = u_ps[:, 0:32].rearrange("p (a i) -> p a i", a=2)
        prm = sb("prm", [P, n_params])

        def w(name, rows=P, r0=0):
            a, n = where[name]
            return prm[r0:r0 + rows, a:a + n]

        def w2(name, half, rows=P, r0=0):
            a, n = where[name]
            return prm[r0:r0 + rows, a + half * (n // 2):a + (half + 1) * (n // 2)]

        def col(name, k=0, rows=P, r0=0):
            a, _ = where[name]
            return prm[r0:r0 + rows, a + k:a + k + 1]

        baseW = sb("baseW", [P, 2, D])
        dftM = sb("dftM", [P, 2, D])
        indb = sb("indb", [2, P], BF16)
        negb = sb("negb", [2, 512], BF16)
        bqs = sb("bqs", [P, 2])
        half_c = sb("half_c", [P, 1])
        zero_c = sb("zero_c", [P, 1])
        eps_c = sb("eps_c", [P, 3])

        x1 = sb("x1", [P, B * C_IN])
        x2 = sb("x2", [XROWS2, B * C_IN])
        Xs = sb("Xs", [P, 8, SM])
        Xc = sb("Xc", [P, TC * 8])
        tap = sb("tap", [P, 2, TC * 8])

        def act_t(name):
            return sb(name, [P, 2, N])

        H, RKV, l_g = act_t("H"), act_t("RKV"), sb("l_g", [P, N])
        Hb, RKVb, l_gb = act_t("Hb"), act_t("RKVb"), sb("l_gb", [P, N])
        XN = sb("XN", [P, 2, B + N])
        xcsq = sb("xcsq", [P, 4 * N])
        xc, sq = [xcsq[:, k * 2 * N:(k + 1) * 2 * N].rearrange("p (a n) -> p a n", a=2) for k in range(2)]
        xn = act_t("xn")
        rstd = sb("rstd", [P, N])
        low = sb("low", [P, N])
        l_wa = sb("l_wa", [112, N])
        l_k = sb("l_k", [48, N])
        Pd = sb("Pd", [P, 2, B + N])
        ops_s = sb("ops_s", [P, 5, 960])
        A_s, B_s, K_s, Q_s, V_s = [ops_s[:, k, :].rearrange("p (t a i) -> p t a i", a=2, i=HS) for k in range(5)]
        P_s = sb("P_s", [P, 2, HS])
        S_sb = sb("S_sb", [P, 2, HS, HS])
        Ma, ub = [sb(nm, [P, 2, HS, HS]) for nm in ("Ma", "ub")]
        vk = sb("vk", [P, RING, 2, HS, HS])
        Mq = sb("Mq", [P, 3, 2, HS, HS])
        Mh = sb("Mh", [P, 2 * YG, 2, HS, HS // 2])
        Y_sb = sb("Y_sb", [P, 2, N])
        arena = sb("arena", [P, 13 * 960])

        def at_(a, n, k=2):
            return arena[:, a:a + n].rearrange("p (a n) -> p a n", a=k)

        def slot(k):
            return at_(k * 960, 960)

        xm = [slot(k) for k in range(4)]
        xrg, xwa, xk, xv = xm
        tmps = [slot(4), slot(5)]
        gma, ga, nz, gmk, mix4, mz, K0, kk, k2 = [slot(k) for k in range(9)]
        ld, Pinv = nz, nz
        ek, kka, cum, R, V, xx = gmk, ga, slot(9), slot(10), slot(11), slot(12)
        Asc, Bsc, Ksc, Qsc = mz, ga, cum, R
        rst, gna = slot(0), slot(1)
        hid = slot(0)
        kx = [arena[:, k * 2048:(k + 1) * 2048].rearrange("p (h e n) -> p h e n", h=2, e=8) for k in range(2)]
        PT = [arena[:, 4096 + i * 2048:4096 + (i + 1) * 2048].rearrange("p (h n) -> p h n", h=16) for i in range(2)]
        Vx = arena[:, 8192:10240].rearrange("p (i a b n) -> p i a b n", i=NT, a=8, b=2)
        q1, k1 = at_(10240, 960), at_(11200, 960)
        O, Gx = q1, k1
        sw96 = arena[:, 0:NT * 96].rearrange("p (i e r) -> p i e r", i=NT, e=6)
        gz = arena[:, 0:1024].rearrange("p (i h d) -> p i h d", i=NT, h=16)
        Out = arena[:, 0:NT * D].rearrange("p (i n) -> p i n", i=NT)
        P1 = xcsq[:, 0:1024].rearrange("p (k h n) -> p k h n", k=2, n=32)
        lg = sb("lg", [P, NT, 6])
        fs = [sb(f"fs{i}", [P, NT, 6]) for i in range(4)]
        f1 = [sb(f"f1{i}", [P, NT, 1]) for i in range(4)]
        cmp1 = sb("cmp1", [P, NT, 6, 6])
        cmp2 = sb("cmp2", [P, NT, 6, 6])
        h96 = low[0:96, :]
        hl = sb("hl", [P, NT, 16])
        hl2 = sb("hl2", [P, NT, 16])
        mx = sb("mx", [P, NT, 16])
        Z = sb("Z", [P, NT, 16])
        tsg = l_gb[0:64, :]

        def ws(name, half):
            a, n = where_s[name]
            return arena[:, a + half * D:a + (half + 1) * D]

        At = [xcsq[:, 0:512].rearrange("p (a n) -> p a n", a=2), xcsq[:, 512:1024].rearrange("p (a n) -> p a n", a=2)]
        block = ctx.enter_context(nc.Block())

        def tb(ap):
            return ap.rearrange("p a (t b) -> p a t b", b=B)

        def bh(ap):
            return ap.unsqueeze(1).broadcast_to([P, 2, N])

        def vq(bank0, i, n):
            return pp[0:n, bank0 + i // 2, (i % 2) * D:(i % 2 + 1) * D]

        def filler(plan, **stages):
            ahead = {name: next(stage, None) for name, stage in stages.items()}
            done = [0]

            def fill(k=SLOTS):
                while done[0] < len(plan) and (plan[done[0]][2] <= k or k == SLOTS):
                    name, level, _ = plan[done[0]]
                    done[0] += 1
                    while ahead[name] == level:
                        ahead[name] = next(stages[name], None)
                assert k < SLOTS or not any(ahead.values()), ahead
            return fill

        def whole(scan, conv, front, keep, back, tail, fori):
            filler(PROLOGUE, conv=conv(0, False, False), front=front(0, False, False))()
            tail(0, True)
            scan(0, filler(FIRST, keep=keep(0), conv=conv(1, True, False), front=front(1, True, False)), True)
            tail(1, False)
            with fori(1, CHUNKS - 1) as c:
                scan(c, filler(BODY, back=back(c - 1, c + 1, True), keep=keep(c), conv=conv(c + 1, True, True),
                               front=front(c + 1, True, True)), False)
                tail(c + 1, False)
            scan(CHUNKS - 1, filler(LAST, back=back(CHUNKS - 2, CHUNKS, False), keep=keep(CHUNKS - 1)), False)
            filler(EPILOGUE, back=back(CHUNKS - 1, CHUNKS, False))()

        @block.sync
        def _(sp):
            def load(c):
                sp.dma_start(x1[:, :], x[bass.ds(c * (STRIDE * TC), P), :]).then_inc(s("x_in"), 16)
                sp.dma_start(x2[:, :], x[bass.ds(c * (STRIDE * TC) + SM1, XROWS2), :]).then_inc(s("x_in"), 16)

            def store(c):
                for i, (t0, n) in enumerate(TILES):
                    dst = out.rearrange("b t c -> t b c")[bass.ds(c * TC + t0 // B, n // B)]
                    sp.dma_start(dst, Out[0:n, i, :]).then_inc(s("out_dram"), 16)

            load(0)
            sp.dma_start(prm[:, :], params).then_inc(s("params_in"), 16)
            sp.dma_start(arena[:, 0:n_setup], dft).then_inc(s("dft_in"), 16)
            for c in range(1, 3):
                sp.wait_ge(s("smooth_ps"), 2 * c)
                load(c)
            with sp.Fori(0, CHUNKS - 3) as c:
                sp.wait_ge(s("smooth_ps"), c * 2 + 6)
                load(c + 3)
                sp.wait_ge(s("out_sb"), c + 1)
                store(c)
            for c in range(CHUNKS - 3, CHUNKS):
                sp.wait_ge(s("out_sb"), c + 1)
                store(c)
            sp.wait_ge(s("out_dram"), 16 * NT * CHUNKS)

        @block.tensor
        def _(pe):
            mm = nc.tensor.matmul
            ident = w("ident")
            pe.wait_ge(s("params_in"), 16)
            pe.wait_ge(s("dft_in"), 16)
            for h in range(2):
                last = mm(pp[:, 0, h * D:(h + 1) * D], w("shared_A", 16)[:, h * P:(h + 1) * P], w("shared_B", 16),
                          start=True, stop=True)
            last.then_inc(s("fold_ps"), 1)
            for im in range(2):
                for m in range(2):
                    for k in range(2):
                        first, second = (("wfr", "Fr"), ("wfi", "nFi")) if im == 0 else (("wfi", "Fr"), ("wfr", "Fi"))
                        mm(pp[:, 1 + im, m * D:(m + 1) * D], ws(first[0], k)[:, m * P:(m + 1) * P], ws(first[1], k),
                           start=(k == 0), stop=False)
                        last = mm(pp[:, 1 + im, m * D:(m + 1) * D], ws(second[0], k)[:, m * P:(m + 1) * P],
                                  ws(second[1], k), start=False, stop=(k == 1))
            last.then_inc(s("fw_ps"), 1)
            pe.wait_ge(s("fw_sb"), 1)
            for m in range(2):
                for k in range(2):
                    mm(pp[:, 3, m * D:(m + 1) * D], At[0][:, k, m * P:(m + 1) * P], ws("Gr", k),
                       start=(k == 0), stop=False)
                    last = mm(pp[:, 3, m * D:(m + 1) * D], At[1][:, k, m * P:(m + 1) * P], ws("nGi", k),
                              start=False, stop=(k == 1))
            last.then_inc(s("dftM_ps"), 1)
            pe.wait_ge(s("setup"), 1)
            pe.wait_ge(s("setup_act"), 1)

            def stats(src, bank, sem):
                mm(pp[:, bank, 0:N], w("ones256"), src[:, 0, :], start=True, stop=False)
                mm(pp[:, bank, 0:N], w("ones256"), src[:, 1, :], start=False, stop=True).then_inc(sem, 1)

            def dense(dst, wt, src, sem):
                for h in range(2):
                    for k in range(2):
                        last = mm(dst[:, h, :], w2(wt, k)[:, h * P:(h + 1) * P], src[:, k, :],
                                  start=(k == 0), stop=(k == 1))
                last.then_inc(sem, 1)

            def lowrank(dst, wt, src, sem):
                for k in range(2):
                    last = mm(dst, w2(wt, k), src[:, k, :], start=(k == 0), stop=(k == 1))
                last.then_inc(sem, 1)

            def expand(dst, wt, r0, rows, src, sem):
                for h in range(2):
                    last = mm(dst[:, h, :], w(wt, rows, r0)[:, h * P:(h + 1) * P], src[r0:r0 + rows, :],
                              start=True, stop=True)
                last.then_inc(sem, 1)

            def per_head(dst, ones, src, sem):
                for h in range(2):
                    last = mm(dst[:, h, :], w(ones), src[:, h, :], start=True, stop=True)
                last.then_inc(sem, 1)

            def conv(c, again, later):
                for part in range(2):
                    yield f"smooth{part}"
                    if part == 0:
                        pe.wait_ge(s("x_in"), c * 32 + 32)
                        if again:
                            pe.wait_ge(s("rn"), c)
                        if later:
                            pe.wait_ge(s("h1"), c - 1)
                    else:
                        pe.wait_ge(s("smooth_sb"), c * 2 + 1)
                    for b in range(4):
                        dst = pp[:, 2 + b // 2, (b % 2) * SM:(b % 2 + 1) * SM]
                        b8 = (4 * part + b) * P
                        mm(dst[:, 0:SM1], x1[:, b8:b8 + P], w("gauss"), start=True, stop=True)
                        last = mm(dst[:, SM1:SM], x2[:, b8:b8 + P], w("gauss", XROWS2)[:, 0:SM2],
                                  start=True, stop=True)
                    last.then_inc(s("smooth_ps"), 1)

            def front(c, again, later):
                yield "proj"
                pe.wait_ge(s("conv"), c + 1)
                pe.wait_ge(s("smooth_sb"), c * 2 + 2)
                if again:
                    pe.wait_ge(s("rkv"), c)
                if later:
                    pe.wait_ge(s("out_sb"), c - 1)
                for h in range(2):
                    for g in range(2):
                        last = mm(pp[:, 2 * g + h, 0:TC * 8], w("w_proj", 64, 64 * g)[:, h * P:(h + 1) * P],
                                  Xc[64 * g:64 * g + 64, :], start=True, stop=True)
                last.then_inc(s("proj_ps"), 1)
                yield "ln0_mean"
                pe.wait_ge(s("proj_sb"), c + 1)
                stats(H, 0, s("f_mean"))
                yield "ln0_var"
                pe.wait_ge(s("f_sq"), c * F_NORMS + 1)
                stats(sq, 1, s("f_var"))
                yield "ln1_mean"
                pe.wait_ge(s("h0"), c + 1)
                stats(H, 2, s("f_mean"))
                yield "ln1_var"
                pe.wait_ge(s("f_sq"), c * F_NORMS + 2)
                stats(sq, 3, s("f_var"))
                yield "lo"
                pe.wait_ge(s("mix"), c + 1)
                lowrank(pp[:, 0, 0:N], "maa_w1", xn, s("lo_ps"))
                for g in range(4):
                    yield f"lo2_{g}"
                    if g == 0:
                        pe.wait_ge(s("lo_sb"), c + 1)
                    if g >= 2:
                        pe.wait_ge(s("tmp"), c * 4 + g - 1)
                    expand([PB, PA][g % 2], "maa_w2", 32 * g, 32, low, s("lo2_ps"))
                yield "wa"
                pe.wait_ge(s("xm"), c * 4 + 2)
                pe.wait_ge(s("tmp"), c * 4 + 3)
                lowrank(pp[0:112, 2, 0:N], "wa_w1", xwa, s("wa_ps"))
                yield "k1"
                pe.wait_ge(s("xm"), c * 4 + 3)
                lowrank(pp[0:48, 3, 0:N], "k_w1", xk, s("k1_ps"))
                yield "r"
                pe.wait_ge(s("tmp"), c * 4 + 4)
                dense(PA, "Wr", xrg, s("r_ps"))
                yield "g1"
                pe.wait_ge(s("wa_sb"), c + 1)
                lowrank(pp[:, 2, 0:N], "gate_w1", xrg, s("g1_ps"))
                yield "kp"
                pe.wait_ge(s("r_sb"), c + 1)
                dense(PA, "Wk", xk, s("k_ps"))
                yield "vp"
                pe.wait_ge(s("xm"), c * 4 + 4)
                pe.wait_ge(s("k1_sb"), c + 1)
                pe.wait_ge(s("g1_sb"), c + 1)
                dense(PB, "Wv", xv, s("v_ps"))
                yield "a"
                pe.wait_ge(s("k_sb"), c + 1)
                expand(PA, "wa_w2", 64, 16, l_wa, s("a_ps"))
                yield "ma"
                pe.wait_ge(s("v_sb"), c + 1)
                expand(PB, "wa_w2", 96, 16, l_wa, s("ma_ps"))
                yield "z"
                pe.wait_ge(s("a_sb"), c + 1)
                expand(PA, "wa_w2", 0, 64, l_wa, s("z_ps"))
                yield "mk"
                pe.wait_ge(s("ma_sb"), c + 1)
                expand(PB, "k_w2", 32, 16, l_k, s("mk_ps"))
                yield "kkl"
                pe.wait_ge(s("z_sb"), c + 1)
                pe.wait_ge(s("z_abs"), c + 1)
                expand(PA, "k_w2", 0, 16, l_k, s("kkl_ps"))
                yield "ss"
                pe.wait_ge(s("mk_sb"), c + 1)
                pe.wait_ge(s("kk_sq"), c + 1)
                per_head(PB, "head_ones", sq, s("ss_ps"))
                yield "rk"
                pe.wait_ge(s("rkp"), c + 1)
                per_head(PA, "head_ones", xx, s("rk_ps"))

            def keep(c):
                return
                yield

            def back(c, tails, tokenizer):
                yield "gn_mean"
                pe.wait_ge(s("y_ch"), c + 1)
                per_head(PA, "head_mean", xn, s("b_mean"))
                yield "G"
                pe.wait_ge(s("b_xc"), c * B_NORMS + 1)
                pe.wait_ge(s("keep"), c + 1)
                for h in range(2):
                    last = mm(PA[:, h, :], w("gate_w2")[:, h * P:(h + 1) * P], l_gb[:, :], start=True, stop=True)
                last.then_inc(s("g_ps"), 1)
                yield "gn_var"
                pe.wait_ge(s("b_sq"), c * B_NORMS + 1)
                per_head(PB, "head_mean", sq, s("b_var"))
                yield "Wo"
                pe.wait_ge(s("y_gated"), c + 1)
                dense(PB, "Wo", xn, s("wo_ps"))
                yield "ln2_mean"
                pe.wait_ge(s("h1"), c + 1)
                stats(Hb, 0, s("b_mean"))
                yield "ln2_var"
                pe.wait_ge(s("b_sq"), c * B_NORMS + 2)
                stats(sq, 1, s("b_var"))
                yield "router"
                pe.wait_ge(s("ln2_xn"), c + 1)
                for i, (t0, n) in enumerate(TILES):
                    dst = pp[0:n, 0, 8 * i:8 * i + 6]
                    for k in range(2):
                        mm(dst, xn[:, k, t0:t0 + n], w2("router_W", k), start=(k == 0), stop=False)
                    last = mm(dst, w("ones_row", 1)[:, 0:n], w("router_b", 1), start=False, stop=True)
                last.then_inc(s("router_ps"), 1)
                yield "h96"
                lowrank(pp[0:96, 1, 0:N], "routed_A", xn, s("h96_ps"))
                yield "base"
                if tokenizer:
                    pe.wait_ge(s("smooth_sb"), c * 2 + 6)
                for h in range(2):
                    for k in range(2):
                        mm(PB[:, h, :], baseW[:, k, h * P:(h + 1) * P], xn[:, k, :], start=(k == 0), stop=False,
                           skip_group_check=True)
                yield "w96"
                pe.wait_ge(s("sw96"), c + 1)
                for i, (t0, n) in enumerate(TILES):
                    last = mm(pp[0:96, 0, t0:t0 + n], sw96[0:n, i, :, :], ident[0:n, 0:n], start=True, stop=True)
                last.then_inc(s("w96_ps"), 1)
                yield "experts"
                pe.wait_ge(s("hw"), c + 1)
                for h in range(2):
                    last = mm(PB[:, h, :], w("routed_B", 96)[:, h * P:(h + 1) * P], h96[:, :], start=False, stop=True,
                              skip_group_check=True)
                last.then_inc(s("ffn_ps"), 1)
                yield "ln3_mean"
                pe.wait_ge(s("h2"), c + 1)
                stats(Hb, 0, s("b_mean"))
                yield "ln3_var"
                pe.wait_ge(s("b_sq"), c * B_NORMS + 3)
                stats(sq, 1, s("b_var"))
                yield "k"
                pe.wait_ge(s("ln3_xn"), c + 1)
                dense(PB, "Wk1", xn, s("k1b_ps"))
                yield "q"
                dense(PA, "Wq1", xn, s("q_ps"))
                yield "W1"
                pe.wait_ge(s("k1b_sb"), c + 1)
                dense(PB, "W1", xn, s("hid_ps"))
                yield "W2"
                pe.wait_ge(s("hid_sb"), c + 1)
                pe.wait_ge(s("q_sb"), c + 1)
                for k in range(2):
                    last = mm(pp[0:64, 0, 0:N], w2("W2", k), hid[:, k, :], start=(k == 0), stop=(k == 1))
                last.then_inc(s("tsg_ps"), 1)
                yield "V"
                for i, (t0, n) in enumerate(TILES):
                    for k in range(2):
                        last = mm(vq(2, i, n), xn[:, k, t0:t0 + n], w2("Wv1", k), start=(k == 0), stop=(k == 1))
                last.then_inc(s("v1_ps"), 1)
                yield "hl"
                pe.wait_ge(s("tsg_sb"), c + 1)
                for i, (t0, n) in enumerate(TILES):
                    last = mm(pp[0:n, 1, 16 * i:16 * i + 16], tsg[:, t0:t0 + n], w("sig", 64), start=True, stop=True)
                last.then_inc(s("hl_ps"), 1)

                def scores(i):
                    t0, n = TILES[i]
                    pe.wait_ge(s("kx"), c * NT + i + 1)
                    if i == 0:
                        pe.wait_ge(s("Vx"), c + 1)
                    if i >= 2:
                        pe.wait_ge(s("P1"), c * NT + i - 1)
                    bank = pp[:, 2 + i % 2, :]
                    mm(bank[0:n, :], indb[:, 0:n], negb[:, :], start=True, stop=False, skip_group_check=True)
                    for qd in range(n // 32):
                        for h in range(2):
                            last = mm(bank[32 * qd:32 * qd + 32, h * 256:(h + 1) * 256],
                                      q1[:, h, t0 + 32 * qd:t0 + 32 * qd + 32],
                                      kx[i % 2][:, h, :, 32 * qd:32 * qd + 32], start=False, stop=True,
                                      skip_group_check=True)
                    last.then_inc(s("sc_ps"), 1)

                def av(i):
                    t0, n = TILES[i]
                    pe.wait_ge(s("PT"), c * NT + i + 1)
                    if i == 0:
                        pe.wait_ge(s("hl_sub"), c + 1)
                    for h in range(16):
                        hp, hh = h // 2, h % 2
                        r = 32 * (hp % 4)
                        last = mm(pp[r:r + 32, hp // 4, t0:t0 + n], Vx[0:n, i, hp, hh, :], PT[i % 2][0:n, h, 0:n],
                                  start=(hh == 0), stop=(hh == 1), skip_group_check=True)
                    last.then_inc(s("av_ps"), 1)

                for i in range(NT):
                    yield f"sc{i}"
                    scores(i)
                    if i >= 1:
                        yield f"av{i - 1}"
                        av(i - 1)
                yield f"av{NT - 1}"
                av(NT - 1)
                yield "gx"
                pe.wait_ge(s("gz"), c + 1)
                for h in range(2):
                    for i, (t0, n) in enumerate(TILES):
                        last = mm(pp[:, 2 + h, t0:t0 + n], gz[0:n, i, 8 * h:8 * h + 8, :], ident[0:n, 0:n],
                                  start=True, stop=True)
                last.then_inc(s("gx_ps"), 1)
                yield "Wo1"
                pe.wait_ge(s("O_sb"), c + 1)
                dense(PB, "Wo1", O, s("wo1_ps"))
                yield "ln4_mean"
                pe.wait_ge(s("h3"), c + 1)
                stats(Hb, 0, s("b_mean"))
                yield "ln4_var"
                pe.wait_ge(s("b_sq"), c * B_NORMS + 4)
                stats(sq, 1, s("b_var"))
                yield "res_h"
                pe.wait_ge(s("h_bias"), c + 1)
                for i, (t0, n) in enumerate(TILES):
                    for k in range(2):
                        mm(vq(2, i, n)[:, k * P:(k + 1) * P], Hb[:, k, t0:t0 + n], ident,
                           start=(i % 2 == 0 and k == 0), stop=False, skip_group_check=True)
                yield "result"
                pe.wait_ge(s("ln4_xn"), c + 1)
                for i, (t0, n) in enumerate(TILES):
                    for k in range(2):
                        last = mm(vq(2, i, n), xn[:, k, t0:t0 + n], dftM[:, k, :], start=False, stop=(k == 1),
                                  skip_group_check=True)
                last.then_inc(s("out_ps"), 1)

            def tail(c, first):
                pe.wait_ge(s("S_sb"), c + 1)
                for hh in range(2):
                    mm(state[:, hh, 0:256], ident, S_sb[:, hh, :, :], start=True, stop=False,
                       skip_group_check=True).then_inc(s(f"upd{hh}"), 1)

            def outputs(c, g, first):
                t0 = g * YG
                pe.wait_ge(s("Mh"), c * TC + (t0 + YG))
                if t0 == 0:
                    if not first:
                        pe.wait_ge(s("y_sb"), c * 2)
                elif t0 == BANK_T:
                    pe.wait_ge(s("y_sb"), c * 2 + 1)
                dst = y_ps[:, (t0 % BANK_T) * 32:(t0 % BANK_T + YG) * 32]
                slots = (g % 2) * YG
                for j in range(HS // 2):
                    last = mm(dst, ident, Mh[:, slots:slots + YG, :, :, j], start=(j == 0), stop=(j == HS // 2 - 1))
                last.then_inc(s("y_ps"), 1)

            def scan(c, fill, first):
                for t in range(TC):
                    fill(4 * t)
                    if t % YG == 1 and t > YG:
                        outputs(c, t // YG - 1, first)
                    fill(4 * t + 1)
                    for hh in range(2):
                        pe.wait_ge(s("vk"), c * TC + (t + 1))
                        pe.wait_ge(s(f"Ma{hh}"), c * TC + (t + 1))
                        if t > 0:
                            pe.wait_ge(s("Mq"), c * TC + t)
                        mm(state[:, hh, 0:256], ident, vk[:, t % RING, hh, :, :], start=False, stop=False,
                           skip_group_check=True)
                    fill(4 * t + 2)
                    for hh in range(2):
                        pe.wait_ge(s(f"ub{hh}"), c * TC + (t + 1))
                        mm(state[:, hh, 0:256], ident, ub[:, hh, :, :], start=False, stop=False,
                           skip_group_check=True).then_inc(s(f"upd{hh}"), 1)
                    fill(4 * t + 3)
                fill()
                outputs(c, TC // YG - 1, first)

            whole(scan, conv, front, keep, back, tail, pe.Fori)

        @block.scalar
        def _(act):
            a = nc.scalar.activation
            act.wait_ge(s("params_in"), 16)
            a(bqs[:, :], w("bq"), ACT.Identity, scale=0.25)
            act.wait_ge(s("fw_ps"), 1)
            a(At[0], pp[:, 1, :], ACT.Identity)
            a(At[1], pp[:, 2, :], ACT.Identity).then_inc(s("fw_sb"), 1)
            act.wait_ge(s("dftM_ps"), 1)
            a(dftM[:, :, :], pp[:, 3, :], ACT.Identity).then_inc(s("setup_act"), 1)
            act.wait_ge(s("setup"), 1)
            act.wait_ge(s("setup_act"), 1)

            def halves(dst, src, f, sem, bias=None, scale=None):
                for h in range(2):
                    kw = {}
                    if bias is not None:
                        kw["bias"] = bias(h)
                    if scale is not None:
                        kw["scale"] = scale if isinstance(scale, float) else scale(h)
                    last = a(dst[:, h, :], src[:, h, :], f, **kw)
                last.then_inc(sem, 1)

            def squares(count, fam):
                act.wait_ge(s(fam + "xc"), count)
                a(sq[:, :, :], xc[:, :, :], ACT.Square).then_inc(s(fam + "sq"), 1)

            def inv_std(count, fam, var, dst=rstd[:, :], eps=eps_c[:, 0:1]):
                act.wait_ge(s(fam + "var"), count)
                a(dst, var, ACT.Ln, bias=eps).then_inc(s(fam + "log"), 1)
                act.wait_ge(s(fam + "log"), count)
                a(dst, dst, ACT.Exp, scale=-0.5).then_inc(s(fam + "rstd"), 1)

            nc.scalar.preload_act_table_set(LN_EXP)

            def conv(c, again, later):
                for part in range(2):
                    yield f"smooth_sb{part}"
                    act.wait_ge(s("smooth_ps"), c * 2 + (part + 1))
                    if again and part == 0:
                        act.wait_ge(s("conv"), c)
                    a(Xs[:, 4 * part:4 * part + 4, :], pp[:, 2:4, 0:2 * SM], ACT.Identity).then_inc(s("smooth_sb"), 1)

            def front(c, again, later):
                yield "proj_sb"
                act.wait_ge(s("proj_ps"), c + 1)
                if again:
                    act.wait_ge(s("keep"), c)
                for g in range(2):
                    for h in range(2):
                        last = a(tb(H[:, :, :])[:, h, :, 8 * g:8 * g + 8],
                                 pp[:, 2 * g + h, 0:TC * 8].rearrange("p (t b) -> p t b", b=8), ACT.Identity,
                                 bias=col("b_proj", h))
                last.then_inc(s("proj_sb"), 1)
                yield "ln0_sq"
                squares(c * F_NORMS + 1, "f_")
                yield "ln0_std"
                inv_std(c * F_NORMS + 1, "f_", pp[:, 1, 0:N])
                yield "ln0_affine"
                act.wait_ge(s("ln0_xn"), c + 1)
                halves(H, xn, ACT.Identity, s("h0"), bias=lambda h: col("ln_beta", h), scale=lambda h: col("ln_gamma", h))
                yield "ln1_sq"
                squares(c * F_NORMS + 2, "f_")
                yield "ln1_std"
                inv_std(c * F_NORMS + 2, "f_", pp[:, 3, 0:N])
                yield "lo_sb"
                act.wait_ge(s("lo_ps"), c + 1)
                a(low[:, :], pp[:, 0, 0:N], ACT.Tanh).then_inc(s("lo_sb"), 1)
                yield "wa_sb"
                act.wait_ge(s("wa_ps"), c + 1)
                a(l_wa[0:64, :], pp[0:64, 2, 0:N], ACT.Tanh)
                a(l_wa[64:112, :], pp[64:112, 2, 0:N], ACT.Identity).then_inc(s("wa_sb"), 1)
                yield "k1_sb"
                act.wait_ge(s("k1_ps"), c + 1)
                a(l_k[0:16, :], pp[0:16, 3, 0:N], ACT.Tanh)
                a(l_k[32:48, :], pp[32:48, 3, 0:N], ACT.Identity).then_inc(s("k1_sb"), 1)
                yield "r_sb"
                act.wait_ge(s("r_ps"), c + 1)
                a(R, PA, ACT.Identity).then_inc(s("r_sb"), 1)
                yield "g1_sb"
                act.wait_ge(s("g1_ps"), c + 1)
                a(l_g[:, :], pp[:, 2, 0:N], ACT.Tanh).then_inc(s("g1_sb"), 1)
                yield "k_sb"
                act.wait_ge(s("k_ps"), c + 1)
                a(K0, PA, ACT.Identity).then_inc(s("k_sb"), 1)
                yield "v_sb"
                act.wait_ge(s("v_ps"), c + 1)
                a(V, PB, ACT.Identity).then_inc(s("v_sb"), 1)
                yield "a_sb"
                act.wait_ge(s("a_ps"), c + 1)
                halves(ga, PA, ACT.Sigmoid, s("a_sb"), bias=lambda h: col("aaaaa", h))
                yield "ma_sb"
                act.wait_ge(s("ma_ps"), c + 1)
                halves(gma, PB, ACT.Sigmoid, s("ma_sb"), bias=lambda h: col("misc_a", h))
                yield "z_abs"
                act.wait_ge(s("z_sb"), c + 1)
                halves(nz, PA, ACT.Abs, s("z_abs"), bias=lambda h: col("decay", h))
                yield "mk_sb"
                act.wait_ge(s("mk_ps"), c + 1)
                halves(gmk, PB, ACT.Sigmoid, s("mk_sb"), bias=lambda h: col("misc_k", h))
                yield "kk_sq"
                act.wait_ge(s("kkr"), c + 1)
                a(sq[:, :, :], kk, ACT.Square).then_inc(s("kk_sq"), 1)
                nc.scalar.preload_act_table_set(LN_EXP)
                yield "z_log"
                act.wait_ge(s("z_abs"), c + 1)
                a(nz, nz, ACT.Exp, scale=-1.0).then_inc(s("a_e1"), 1)
                act.wait_ge(s("a_e1"), c + 1)
                a(nz, nz, ACT.Ln, bias=1.0).then_inc(s("l1p"), 1)
                yield "ld"
                act.wait_ge(s("lsig"), c + 1)
                a(ld.rearrange("p a n -> p (a n)").rearrange("p (a b t) -> p a t b", a=2, t=TC), tb(mz), ACT.Exp,
                  bias=half_c[:, 0:1]).then_inc(s("ld"), 1)
                yield "norm"
                act.wait_ge(s("rn"), c + 1)
                a(xc[:, :, :], xc[:, :, :], ACT.Ln, scale=2.0 ** 30).then_inc(s("norm_log"), 1)
                act.wait_ge(s("norm_log"), c + 1)
                a(xc[:, :, :], xc[:, :, :], ACT.Exp, scale=-0.5, bias=eps_c[:, 2:3]).then_inc(s("norm"), 1)
                yield "ek"
                act.wait_ge(s("wm"), c + 1)
                a(ek, ek, ACT.Exp).then_inc(s("ek"), 1)
                yield "Pd"
                act.wait_ge(s("cum"), c + 1)
                if again:
                    act.wait_ge(s("scan_in"), c)
                cumv = cum.rearrange("p a n -> p (a n)").rearrange("p (a b t) -> p a t b", a=2, t=TC)
                a(tb(Pd[:, :, B:]), cumv, ACT.Exp, scale=-1.0)
                a(tb(Pinv), cumv, ACT.Exp).then_inc(s("Pd"), 1)

            def keep(c):
                yield "keep"
                act.wait_ge(s("rkv"), c + 1)
                a(Hb[:, :, :], H[:, :, :], ACT.Identity)
                a(l_gb[:, :], l_g[:, :], ACT.Identity)
                a(RKVb[:, :, :], RKV[:, :, :], ACT.Identity).then_inc(s("keep"), 1)

            def back(c, tails, tokenizer):
                yield "gn_sq"
                squares(c * B_NORMS + 1, "b_")
                yield "gn_std"
                if not tokenizer:
                    act.wait_ge(s("out_dram"), c * (16 * NT))
                inv_std(c * B_NORMS + 1, "b_", PB, rst, eps_c[:, 1:2])
                yield "gn_affine"
                act.wait_ge(s("gn_yn"), c + 1)
                halves(gna, xn, ACT.Identity, s("gn_aff"), bias=lambda h: col("ln_b", h), scale=lambda h: col("ln_w", h))
                yield "ln2_sq"
                squares(c * B_NORMS + 2, "b_")
                yield "ln2_std"
                inv_std(c * B_NORMS + 2, "b_", pp[:, 1, 0:N])
                yield "h96_sb"
                act.wait_ge(s("h96_ps"), c + 1)
                a(h96[:, :], pp[0:96, 1, 0:N], ACT.Identity).then_inc(s("h96_sb"), 1)
                yield "router_exp"
                act.wait_ge(s("lg_sub"), c + 1)
                a(lg[:, :, :], lg[:, :, :], ACT.Exp).then_inc(s("lg_exp"), 1)
                yield "ln3_sq"
                squares(c * B_NORMS + 3, "b_")
                yield "ln3_std"
                inv_std(c * B_NORMS + 3, "b_", pp[:, 1, 0:N])
                yield "k_bias"
                act.wait_ge(s("k1b_ps"), c + 1)
                halves(k1, PB, ACT.Identity, s("k1b_sb"), bias=lambda h: col("bk", h))
                yield "q_sb"
                act.wait_ge(s("q_ps"), c + 1)
                halves(q1, PA, ACT.Identity, s("q_sb"), bias=lambda h: bqs[:, h:h + 1], scale=0.25)
                yield "hid"
                act.wait_ge(s("hid_ps"), c + 1)
                halves(hid, PB, ACT.Relu, s("hid_sb"), bias=lambda h: col("b1", h))
                yield "tsg"
                act.wait_ge(s("tsg_ps"), c + 1)
                a(tsg[:, :], pp[0:64, 0, 0:N], ACT.Identity, bias=col("b2", 0, 64)).then_inc(s("tsg_sb"), 1)

                def keys(i):
                    t0, n = TILES[i]
                    if i == 0:
                        act.wait_ge(s("k1b_sb"), c + 1)
                    if i >= 2:
                        act.wait_ge(s("sc_ps"), c * NT + i - 1)
                    for e in range(8):
                        last = a(kx[i % 2][:, :, e, 0:n], k1[:, :, t0:t0 + n], ACT.Identity, scale=col("head_mask", e))
                    last.then_inc(s("kx"), 1)

                yield "kx0"
                keys(0)
                yield "hl_exp"
                act.wait_ge(s("hl_sub"), c + 1)
                a(hl[:, :, :], hl[:, :, :], ACT.Exp).then_inc(s("hl_exp"), 1)
                yield "kx1"
                keys(1)
                for i, (t0, n) in enumerate(TILES):
                    yield f"e{i}"
                    act.wait_ge(s("P1"), c * NT + i + 1)
                    a(P1[0:n, i % 2, :, :], P1[0:n, i % 2, :, :], ACT.Exp).then_inc(s("P1e"), 1)
                    if i < 2:
                        yield f"kx{i + 2}"
                        keys(i + 2)
                yield "gx_sb"
                act.wait_ge(s("gx_ps"), c + 1)
                a(Gx, PB, ACT.Identity).then_inc(s("gx_sb"), 1)
                yield "ln4_sq"
                squares(c * B_NORMS + 4, "b_")
                yield "h_bias"
                halves(Hb, Hb, ACT.Identity, s("h_bias"), bias=lambda h: col("f_bias", h))
                yield "ln4_std"
                inv_std(c * B_NORMS + 4, "b_", pp[:, 1, 0:N])
                yield "result_sb"
                act.wait_ge(s("out_ps"), c + 1)
                a(Out[:, 0:3, :], pp[:, 2:4, :].rearrange("p a (b n) -> p (a b) n", b=2)[:, 0:3, :], ACT.Identity)
                a(Out[0:96, 3, :], pp[0:96, 3, 256:512], ACT.Identity).then_inc(s("out_sb"), 1)

            def tail(c, first):
                pass

            def half_out(c, half):
                act.wait_ge(s("y_ps"), c * (TC // YG) + (half + 1) * (BANK_T // YG))
                a(Y_sb[:, half, :], y_ps[:, 0:N], ACT.Identity).then_inc(s("y_sb"), 1)

            def scan(c, fill, first):
                for k in range(SLOTS):
                    fill(k)
                    if k == 4 * (BANK_T + 2):
                        if not first:
                            act.wait_ge(s("y_ch"), c)
                        half_out(c, 0)
                fill()
                half_out(c, 1)

            whole(scan, conv, front, keep, back, tail, act.Fori)

        @block.vector
        def _(dve):
            v = nc.vector
            tt_, stt, ts = v.tensor_tensor, v.scalar_tensor_tensor, v.tensor_scalar
            v.memset(XN[:, :, :], 0.0)
            v.memset(S_sb[:, :, :, :], 0.0)
            v.memset(Pd[:, :, 0:B], 1.0)
            v.memset(half_c[:, :], -0.5)
            v.memset(eps_c[:, 0:1], 1e-5)
            v.memset(eps_c[:, 1:2], 6.4e-4)
            v.memset(eps_c[:, 2:3], 15.0 * math.log(2.0))
            v.memset(lg[:, :, :], 0.0)
            v.memset(hl[:, :, :], 0.0)
            v.memset(Z[:, :, :], 1.0)
            dve.wait_ge(s("params_in"), 16)
            v.tensor_copy(indb[:, :], w("pair_ind", 2))
            v.tensor_copy(negb[:, :], w("pair_neg", 2))
            dve.wait_ge(s("fold_ps"), 1)
            tt_(baseW[:, :, :], pp[:, 0, :], w("base_W"), ALU.add).then_inc(s("setup"), 1)
            dve.wait_ge(s("setup"), 1)
            dve.wait_ge(s("setup_act"), 1)

            def centred(count, fam, src, mean):
                dve.wait_ge(s(fam + "mean"), count)
                tt_(xc[:, :, :], src, mean, ALU.subtract).then_inc(s(fam + "xc"), 1)

            def normed(count, fam, dst, r):
                dve.wait_ge(s(fam + "rstd"), count)
                dve.wait_ge(s(fam + "xc"), count)
                return tt_(dst, xc[:, :, :], r, ALU.mult)

            def conv(c, again, later):
                return
                yield

            def front(c, again, later):
                yield "ln0_xc"
                centred(c * F_NORMS + 1, "f_", H[:, :, :], bh(pp[:, 0, 0:N]))
                yield "ln0_out"
                normed(c * F_NORMS + 1, "f_", xn[:, :, :], bh(rstd[:, :])).then_inc(s("ln0_xn"), 1)
                v.tensor_copy(XN[:, :, 0:B], XN[:, :, N:N + B]).then_inc(s("carry"), 1)
                yield "ln1_xc"
                centred(c * F_NORMS + 2, "f_", H[:, :, :], bh(pp[:, 2, 0:N]))
                yield "ln1_out"
                dve.wait_ge(s("carry"), c + 1)
                normed(c * F_NORMS + 2, "f_", XN[:, :, B:], bh(rstd[:, :])).then_inc(s("ln1_xn"), 1)
                yield "xx"
                dve.wait_ge(s("ln1_xn"), c + 1)
                tt_(xx, XN[:, :, 0:N], XN[:, :, B:], ALU.subtract).then_inc(s("xx"), 1)
                yield "mix"
                dve.wait_ge(s("xx"), c + 1)
                for h in range(2):
                    last = stt(out=xn[:, h, :], in0=xx[:, h, :], scalar=col("maa_x", h), in1=XN[:, h, B:],
                               op0=ALU.mult, op1=ALU.add)
                last.then_inc(s("mix"), 1)
                for g in range(4):
                    yield f"tmp{g}"
                    src = [PB, PA][g % 2]
                    dve.wait_ge(s("lo2_ps"), c * 4 + g + 1)
                    if g >= 2:
                        dve.wait_ge(s("xm"), c * 4 + g - 1)
                    for h in range(2):
                        last = stt(out=tmps[g % 2][:, h, :], in0=src[:, h, :], scalar=col("maa", 2 * g + h),
                                   in1=xx[:, h, :], op0=ALU.add, op1=ALU.mult)
                    last.then_inc(s("tmp"), 1)
                yield "z_sb"
                dve.wait_ge(s("z_ps"), c + 1)
                dve.wait_ge(s("xm"), c * 4 + 4)
                for h in range(2):
                    last = ts(mz[:, h, :], PA[:, h, :], col("decay", h), 0.0, ALU.add, ALU.min)
                last.then_inc(s("z_sb"), 1)
                yield "kkr"
                dve.wait_ge(s("kkl_ps"), c + 1)
                dve.wait_ge(s("k_sb"), c + 1)
                tt_(kk, PA, K0, ALU.add).then_inc(s("kkr"), 1)
                yield "lsig"
                dve.wait_ge(s("l1p"), c + 1)
                dve.wait_ge(s("z_sb"), c + 1)
                tt_(mz, mz, nz, ALU.subtract).then_inc(s("lsig"), 1)
                yield "wm"
                dve.wait_ge(s("lsig"), c + 1)
                dve.wait_ge(s("mk_sb"), c + 1)
                stt(out=ek, in0=mz, scalar=-0.5, in1=gmk, op0=ALU.add, op1=ALU.mult).then_inc(s("wm"), 1)
                yield "rn"
                dve.wait_ge(s("ss_ps"), c + 1)
                ts(xc[:, :, :], PB, 1e-24, None, ALU.max).then_inc(s("rn"), 1)
                yield "cum"
                dve.wait_ge(s("ld"), c + 1)
                v.tensor_tensor_scan(arena[:, 9 * 960:10 * 960], w("scan_mask"), arena[:, 2 * 960:3 * 960], 0.0,
                                     ALU.mult, ALU.add).then_inc(s("cum"), 1)
                yield "kkn"
                dve.wait_ge(s("norm"), c + 1)
                dve.wait_ge(s("kk_sq"), c + 1)
                tt_(kk, kk, xc[:, :, :], ALU.mult).then_inc(s("kkn"), 1)
                yield "k2"
                dve.wait_ge(s("kmix"), c + 1)
                dve.wait_ge(s("ek"), c + 1)
                tt_(k2, k2, ek, ALU.mult).then_inc(s("k2"), 1)
                yield "rkp"
                dve.wait_ge(s("k2"), c + 1)
                for h in range(2):
                    last = stt(out=xx[:, h, :], in0=R[:, h, :], scalar=col("faaaa", h), in1=k2[:, h, :],
                               op0=ALU.mult, op1=ALU.mult)
                last.then_inc(s("rkp"), 1)
                yield "scaled_a"
                dve.wait_ge(s("Pd"), c + 1)
                dve.wait_ge(s("kkn"), c + 1)
                tt_(Asc, kk, Pd[:, :, 0:N], ALU.mult)
                yield "scaled_k"
                tt_(Ksc, k2, Pinv, ALU.mult)
                yield "scaled_q"
                dve.wait_ge(s("rkp"), c + 1)
                tt_(Qsc, R, Pd[:, :, B:], ALU.mult)
                yield "scaled_b"
                dve.wait_ge(s("kka"), c + 1)
                stt(out=Bsc, in0=kka, scalar=-1.0, in1=Pinv, op0=ALU.mult, op1=ALU.mult).then_inc(s("scaled"), 1)
                yield "rkv"
                dve.wait_ge(s("rk_ps"), c + 1)
                if again:
                    dve.wait_ge(s("keep"), c)
                tt_(RKV[:, :, :], PA, V, ALU.mult).then_inc(s("rkv"), 1)

            def keep(c):
                return
                yield

            def tail(c, first):
                def to_scan(dst, src):
                    return v.transpose(dst.rearrange("p t a i -> p t (a i)"),
                                       src.rearrange("p a (t b) -> p t a b", b=B))

                if not first:
                    for hh in range(2):
                        dve.wait_ge(s(f"upd{hh}"), c * (TC + 1))
                        last = s_times(S_sb[:, hh, :, :], hh, P_s[:, hh, :])
                    last.then_inc(s("S_sb"), 1)
                    dve.wait_ge(s("vk"), c * TC)
                dve.wait_ge(s("scaled"), c + 1)
                to_scan(V_s[:, :, :, :], V)
                to_scan(K_s[:, :, :, :], Ksc).then_inc(s("vk_in"), 1)
                to_scan(A_s[:, :, :, :], Asc)
                to_scan(B_s[:, :, :, :], Bsc)
                if not first:
                    dve.wait_ge(s("Mq"), c * TC)
                to_scan(Q_s[:, :, :, :], Qsc)
                if not first:
                    dve.wait_ge(s("S_sb"), c + 1)
                v.transpose(P_s[:, :, :].rearrange("p a i -> p (a i)"), Pd[:, :, N:N + B]).then_inc(s("scan_in"), 1)
                dve.wait_ge(s("scan_in"), c + 1)
                if first:
                    v.tensor_copy(S_sb[:, 0, 0, 0:1], S_sb[:, 0, 0, 0:1]).then_inc(s("S_sb"), 1)

            def s_times(dst, hh, vec):
                return tt_(dst, state[:, hh, 0:256].rearrange("p (i j) -> p i j", j=HS),
                           vec.unsqueeze(1).broadcast_to([P, HS, HS]), ALU.mult)

            def scan(c, fill, first):
                def outputs(t):
                    if t >= 3 or not first:
                        dve.wait_ge(s("Mh"), c * TC + (t - 2))
                    for hh in range(2):
                        last = s_times(Mq[:, t % 3, hh, :, :], hh, Q_s[:, t, hh, :])
                    last.then_inc(s("Mq"), 1)

                for t in range(TC):
                    fill(4 * t)
                    for hh in range(2):
                        dve.wait_ge(s(f"upd{hh}"), c * (TC + 1) + (t + 1))
                        s_times(Ma[:, hh, :, :], hh, A_s[:, t, hh, :]).then_inc(s(f"Ma{hh}"), 1)
                    if t > 0:
                        outputs(t - 1)
                    fill(4 * t + 1)
                    for hh in range(2):
                        dve.wait_ge(s(f"Ma{hh}"), c * TC + (t + 1))
                        v.tensor_reduce(u[:, hh, :], Ma[:, hh, :, :], AX, ALU.add).then_inc(s(f"u{hh}"), 1)
                    for hh in range(2):
                        dve.wait_ge(s(f"u{hh}"), c * TC + (t + 1))
                        tt_(ub[:, hh, :, :], u[:, hh, :].unsqueeze(2).broadcast_to([P, HS, HS]),
                            B_s[:, t, hh, :].unsqueeze(1).broadcast_to([P, HS, HS]), ALU.mult)\
                            .then_inc(s(f"ub{hh}"), 1)
                    fill(4 * t + 2)
                    fill(4 * t + 3)
                fill()
                dve.wait_ge(s("upd0"), c * (TC + 1) + (TC + 1))
                dve.wait_ge(s("upd1"), c * (TC + 1) + (TC + 1))
                outputs(TC - 1)

            def back(c, tails, tokenizer):
                yield "y_turn"
                dve.wait_ge(s("y_sb"), c * 2 + 2)
                v.transpose(tb(xn[:, :, :]).rearrange("p a t b -> p t a b"),
                            Y_sb[:, :, :].rearrange("p g (t n) -> p g t n", n=32)).then_inc(s("y_ch"), 1)
                yield "gn_xc"
                dve.wait_ge(s("y_ch"), c + 1)
                centred(c * B_NORMS + 1, "b_", xn[:, :, :], PA)
                yield "gn_out"
                normed(c * B_NORMS + 1, "b_", xn[:, :, :], rst).then_inc(s("gn_yn"), 1)
                yield "bonus"
                dve.wait_ge(s("keep"), c + 1)
                dve.wait_ge(s("gn_aff"), c + 1)
                tt_(xc[:, :, :], gna, RKVb[:, :, :], ALU.add).then_inc(s("y_bonus"), 1)
                yield "gated"
                dve.wait_ge(s("g_ps"), c + 1)
                dve.wait_ge(s("y_bonus"), c + 1)
                tt_(xn[:, :, :], PA, xc[:, :, :], ALU.mult).then_inc(s("y_gated"), 1)
                yield "h1"
                dve.wait_ge(s("wo_ps"), c + 1)
                tt_(Hb[:, :, :], PB, Hb[:, :, :], ALU.add).then_inc(s("h1"), 1)
                yield "ln2_xc"
                dve.wait_ge(s("h1"), c + 1)
                centred(c * B_NORMS + 2, "b_", Hb[:, :, :], bh(pp[:, 0, 0:N]))
                yield "ln2_out"
                normed(c * B_NORMS + 2, "b_", xn[:, :, :], bh(rstd[:, :])).then_inc(s("ln2_xn"), 1)
                steps = [0]

                def chain(ins):
                    steps[0] += 1
                    ins.then_inc(s("small"), 1)
                    dve.wait_ge(s("small"), c * SMALL + steps[0])

                def b6(ap):
                    return ap.broadcast_to([P, NT, 6])

                yield "router_max"
                dve.wait_ge(s("router_ps"), c + 1)
                rl = pp[:, 0, 0:32].rearrange("p (a n) -> p a n", n=8)[:, :, 0:6]
                v.tensor_copy(lg[:, 0:3, :], rl[:, 0:3, :])
                chain(v.tensor_copy(lg[0:96, 3, :], rl[0:96, 3, :]))
                chain(v.tensor_reduce(f1[0][:, :, :], lg[:, :, :], AX, ALU.max))
                tt_(lg[:, :, :], lg[:, :, :], b6(f1[0][:, :, :]), ALU.subtract).then_inc(s("lg_sub"), 1)
                yield "gates"
                dve.wait_ge(s("lg_exp"), c + 1)
                chain(v.tensor_reduce(f1[1][:, :, :], lg[:, :, :], AX, ALU.add))
                chain(v.reciprocal(f1[2][:, :, :], f1[1][:, :, :]))
                gt = fs[0][:, :, :]
                chain(tt_(gt, lg[:, :, :], b6(f1[2][:, :, :]), ALU.mult))
                yield "rank"
                other = gt.unsqueeze(2).broadcast_to([P, NT, 6, 6])
                this = gt.unsqueeze(3).broadcast_to([P, NT, 6, 6])
                tt_(cmp1[:, :, :, :], other, this, ALU.is_gt)
                chain(tt_(cmp2[:, :, :, :], other, this, ALU.is_equal))
                chain(tt_(cmp2[:, :, :, :], cmp2[:, :, :, :],
                          w("expert_before").rearrange("p (a b) -> p a b", b=6).unsqueeze(1).broadcast_to([P, NT, 6, 6]),
                          ALU.mult))
                chain(tt_(cmp1[:, :, :, :], cmp1[:, :, :, :], cmp2[:, :, :, :], ALU.add))
                yield "top2"
                chain(v.tensor_reduce(fs[1][:, :, :], cmp1[:, :, :, :], AX, ALU.add))
                chain(stt(out=fs[2][:, :, :], in0=fs[1][:, :, :], scalar=1.5, in1=gt, op0=ALU.is_lt, op1=ALU.mult))
                chain(v.tensor_reduce(f1[3][:, :, :], fs[2][:, :, :], AX, ALU.add))
                yield "top2_sum"
                chain(ts(f1[0][:, :, :], f1[3][:, :, :], 1e-6, None, ALU.add))
                chain(v.reciprocal(f1[1][:, :, :], f1[0][:, :, :]))
                chain(tt_(fs[3][:, :, :], fs[2][:, :, :], b6(f1[1][:, :, :]), ALU.mult))
                v.tensor_copy(sw96[:, :, :, :], fs[3][:, :, :].unsqueeze(3).broadcast_to([P, NT, 6, 16]))\
                    .then_inc(s("sw96"), 1)
                yield "hw"
                dve.wait_ge(s("w96_ps"), c + 1)
                dve.wait_ge(s("h96_sb"), c + 1)
                tt_(h96[:, :], pp[0:96, 0, 0:N], h96[:, :], ALU.mult).then_inc(s("hw"), 1)
                yield "h2"
                dve.wait_ge(s("ffn_ps"), c + 1)
                for h in range(2):
                    last = stt(out=Hb[:, h, :], in0=PB[:, h, :], scalar=col("base_b", h), in1=Hb[:, h, :],
                               op0=ALU.add, op1=ALU.add)
                last.then_inc(s("h2"), 1)

                yield "ln3_xc"
                dve.wait_ge(s("h2"), c + 1)
                centred(c * B_NORMS + 3, "b_", Hb[:, :, :], bh(pp[:, 0, 0:N]))
                yield "ln3_out"
                normed(c * B_NORMS + 3, "b_", xn[:, :, :], bh(rstd[:, :])).then_inc(s("ln3_xn"), 1)
                yield "Vx"
                dve.wait_ge(s("v1_ps"), c + 1)
                dve.wait_ge(s("PV0"), c + 1)
                bvx = w("bv").rearrange("p (a b d) -> p a b d", b=2, d=16)
                for i, (t0, n) in enumerate(TILES):
                    src = vq(2, i, n).rearrange("p (a b d) -> p a b d", b=2, d=16)
                    for hh in range(2):
                        last = tt_(Vx[0:n, i, :, hh, 16 * hh:16 * hh + 16], src[:, :, hh, :], bvx[0:n, :, hh, :],
                                   ALU.add)
                last.then_inc(s("Vx"), 1)
                yield "hl_max"
                dve.wait_ge(s("hl_ps"), c + 1)
                hp = pp[:, 1, 0:64].rearrange("p (a n) -> p a n", n=16)

                def b16(ap):
                    return ap.broadcast_to([P, NT, 16])

                v.tensor_copy(hl[:, 0:3, :], hp[:, 0:3, :])
                chain(v.tensor_copy(hl[0:96, 3, :], hp[0:96, 3, :]))
                chain(v.tensor_reduce(f1[0][:, :, :], hl[:, :, :], AX, ALU.max))
                tt_(hl[:, :, :], hl[:, :, :], b16(f1[0][:, :, :]), ALU.subtract).then_inc(s("hl_sub"), 1)
                yield "hl_gate"
                dve.wait_ge(s("hl_exp"), c + 1)
                chain(v.tensor_reduce(f1[1][:, :, :], hl[:, :, :], AX, ALU.add))
                chain(v.reciprocal(f1[2][:, :, :], f1[1][:, :, :]))
                chain(tt_(hl[:, :, :], hl[:, :, :], b16(f1[2][:, :, :]), ALU.mult))

                def scores(i):
                    t0, n = TILES[i]
                    sc = pp[0:n, 2 + i % 2, :].rearrange("p (h n) -> p h n", n=32)
                    dve.wait_ge(s("sc_ps"), c * NT + i + 1)
                    v.tensor_reduce(mx[0:n, i, :], sc, AX, ALU.max).then_inc(s("mx"), 1)
                    dve.wait_ge(s("mx"), c * NT + i + 1)
                    tt_(P1[0:n, i % 2, :, :], sc, mx[0:n, i, :].unsqueeze(2).broadcast_to([n, 16, 32]),
                        ALU.subtract).then_inc(s("P1"), 1)

                def turn(i):
                    t0, n = TILES[i]
                    dve.wait_ge(s("P1e"), c * NT + i + 1)
                    v.tensor_reduce(Z[0:n, i, :], P1[0:n, i % 2, :, :], AX, ALU.add).then_inc(s("Z"), 1)
                    if i >= 2:
                        dve.wait_ge(s("av_ps"), c * NT + i - 1)
                    for qd in range(n // 32):
                        r = slice(32 * qd, 32 * qd + 32)
                        last = v.transpose(PT[i % 2][r, :, r], P1[r, i % 2, :, :])
                    last.then_inc(s("PT"), 1)

                yield "p0"
                scores(0)
                for i in range(NT):
                    if i + 1 < NT:
                        yield f"p{i + 1}"
                        scores(i + 1)
                    yield f"t{i}"
                    turn(i)
                yield "gz"
                dve.wait_ge(s("Z"), c * NT + NT)
                chain(v.reciprocal(hl2[:, :, :], Z[:, :, :]))
                chain(tt_(hl2[:, :, :], hl2[:, :, :], hl[:, :, :], ALU.mult))
                v.tensor_copy(gz[:, :, :, :], hl2[:, :, :].unsqueeze(3).broadcast_to([P, NT, 16, 16]))\
                    .then_inc(s("gz"), 1)
                yield "O"
                dve.wait_ge(s("gx_sb"), c + 1)
                dve.wait_ge(s("av_ps"), c * NT + NT)
                tt_(O, PA, Gx, ALU.mult).then_inc(s("O_sb"), 1)
                yield "h3"
                dve.wait_ge(s("wo1_ps"), c + 1)
                for h in range(2):
                    last = stt(out=Hb[:, h, :], in0=PB[:, h, :], scalar=col("bo", h), in1=Hb[:, h, :],
                               op0=ALU.add, op1=ALU.add)
                last.then_inc(s("h3"), 1)
                yield "ln4_xc"
                dve.wait_ge(s("h3"), c + 1)
                centred(c * B_NORMS + 4, "b_", Hb[:, :, :], bh(pp[:, 0, 0:N]))
                yield "ln4_out"
                normed(c * B_NORMS + 4, "b_", xn[:, :, :], bh(rstd[:, :])).then_inc(s("ln4_xn"), 1)
                assert steps[0] == SMALL

            whole(scan, conv, front, keep, back, tail, dve.Fori)

        @block.gpsimd
        def _(pool):
            g_ = nc.gpsimd
            g_.memset(zero_c[:, :], 0.0).then_inc(s("zero"), 1)
            pool.wait_ge(s("zero"), 1)
            pool.wait_ge(s("params_in"), 16)

            def conv(c, again, later):
                wt = w("w_temporal")
                sums = Xc[:, :].rearrange("p (t a) -> p t a", a=8)
                for k in range(KT):
                    yield f"tap{k}"
                    if k == 0:
                        pool.wait_ge(s("smooth_sb"), c * 2 + 2)
                        if again:
                            pool.wait_ge(s("proj_ps"), c)
                    dst = sums if k == 0 else tap[:, k % 2, :].rearrange("p (t a) -> p t a", a=8)
                    g_.tensor_tensor(dst, Xs[:, :, k:k + STRIDE * (TC - 1) + 1:STRIDE].rearrange("p a t -> p t a"),
                                     wt[:, k:k + 1].unsqueeze(2).broadcast_to([P, TC, 8]), ALU.mult)\
                        .then_inc(s("tap"), 1)
                    if k > 0:
                        pool.wait_ge(s("tap"), c * (2 * KT - 2) + 2 * k)
                        last = g_.tensor_tensor(sums, sums, dst, ALU.add)
                        last.then_inc(s("conv" if k == KT - 1 else "tap"), 1)

            def front(c, again, later):
                for g in range(4):
                    yield f"xm{g}"
                    if g == 0 and later:
                        pool.wait_ge(s("out_dram"), (c - 1) * (16 * NT))
                    pool.wait_ge(s("tmp"), c * 4 + g + 1)
                    g_.tensor_tensor(xm[g], tmps[g % 2], XN[:, :, B:], ALU.add).then_inc(s("xm"), 1)
                yield "mix0"
                pool.wait_ge(s("ma_sb"), c + 1)
                pool.wait_ge(s("a_sb"), c + 1)
                g_.tensor_tensor(mix4, ga, gma, ALU.mult).then_inc(s("g_chain"), 1)
                yield "mix1"
                pool.wait_ge(s("g_chain"), c * 3 + 1)
                g_.tensor_tensor(mix4, ga, mix4, ALU.subtract).then_inc(s("g_chain"), 1)
                yield "mix2"
                pool.wait_ge(s("g_chain"), c * 3 + 2)
                g_.tensor_tensor(mix4, gma, mix4, ALU.add).then_inc(s("g_chain"), 1)
                yield "kmix"
                pool.wait_ge(s("g_chain"), c * 3 + 3)
                pool.wait_ge(s("k_sb"), c + 1)
                g_.tensor_tensor(k2, K0, mix4, ALU.mult).then_inc(s("kmix"), 1)
                yield "kka"
                pool.wait_ge(s("kkn"), c + 1)
                g_.tensor_tensor(kka, kk, ga, ALU.mult).then_inc(s("kka"), 1)

            def keep(c):
                return
                yield

            def back(c, tails, tokenizer):
                for k in range(3):
                    yield f"zero{k}"
                    pool.wait_ge(s("scan_in"), tails)
                    zz = zero_c[:, 0:1].broadcast_to([P, 2048])
                    last = g_.tensor_tensor(arena[:, 4096 + 2048 * k:6144 + 2048 * k], zz, zz, ALU.add)
                last.then_inc(s("PV0"), 1)

            def tail(c, first):
                pass

            def scan(c, fill, first):
                def outer(t):
                    pool.wait_ge(s("vk_in"), c + 1)
                    if t >= RING:
                        pool.wait_ge(s("upd1"), c * (TC + 1) + (t - RING + 2))
                    for hh in range(2):
                        last = g_.tensor_tensor(vk[:, t % RING, hh, :, :],
                                                V_s[:, t, hh, :].unsqueeze(2).broadcast_to([P, HS, HS]),
                                                K_s[:, t, hh, :].unsqueeze(1).broadcast_to([P, HS, HS]), ALU.mult)
                    last.then_inc(s("vk"), 1)

                def halve(t):
                    m = Mq[:, t % 3, :, :, :]
                    pool.wait_ge(s("Mq"), c * TC + (t + 1))
                    if t >= 2 * YG:
                        pool.wait_ge(s("y_ps"), c * (TC // YG) + (t // YG - 1))
                    elif not first:
                        pool.wait_ge(s("y_ps"), c * (TC // YG) + (t // YG - 1))
                    g_.tensor_tensor(Mh[:, t % (2 * YG), :, :, :], m[:, :, :, 0:HS // 2], m[:, :, :, HS // 2:], ALU.add)\
                        .then_inc(s("Mh"), 1)

                outer(0)
                outer(1)
                for t in range(TC):
                    fill(4 * t)
                    if t + 2 < TC:
                        outer(t + 2)
                    fill(4 * t + 1)
                    if t > 0:
                        halve(t - 1)
                    fill(4 * t + 2)
                    fill(4 * t + 3)
                fill()
                halve(TC - 1)

            whole(scan, conv, front, keep, back, tail, pool.Fori)


def kernel(**inp):
    import numpy as np
    import concourse.bacc as bacc
    from concourse.bass_utils import run_bass_kernel_spmd

    f = {k: np.asarray(v) for k, v in inp.items()}
    where, n_params = offsets(PACK)
    where_s, n_setup = offsets(SETUP)
    prm = np.zeros((P, n_params), np.float32)
    dft = np.zeros((P, n_setup), np.float32)

    def put(name, a, r0=0, c0=0):
        at = where[name][0] + c0
        prm[r0:r0 + a.shape[0], at:at + a.shape[1]] = a

    def vec(name, a):
        put(name, a.reshape(2, P).T)

    def rows(name, a, c0=0, n=None):
        n = n or a.shape[1]
        put(name, a[0:P], 0, c0)
        put(name, a[P:2 * P], 0, n + c0)

    L0, F0, L1 = "L0_attn_", "L0_ffn_", "L1_attn_"
    wt = f["L0_tok_w_temporal"][:, 0, :]
    put("w_temporal", np.concatenate([wt, wt]))
    put("w_proj", np.concatenate([f["L0_tok_w_proj"].T, f["L0_tok_w_proj"].T]))
    tg = np.arange(KG, dtype=np.float32) - (KG - 1) / 2
    g = np.exp(-tg ** 2 / 8.0).astype(np.float32)
    g = g / g.sum()
    band = np.zeros((P, SM1), np.float32)
    for j in range(SM1):
        band[j:j + KG, j] = g
    put("gauss", band)
    put("ident", np.eye(P, dtype=np.float32))
    vec("b_proj", f["L0_tok_b_proj"])
    vec("ln_gamma", f["L0_tok_ln_gamma"])
    vec("ln_beta", f["L0_tok_ln_beta"])
    put("ones256", np.full((P, P), 1.0 / D, np.float32))
    same = np.kron(np.eye(8, dtype=np.float32), np.ones((16, 16), np.float32))
    put("head_ones", same)
    put("head_mean", same * np.float32(1.0 / HS))
    keep = np.ones((P, 2 * B, TC), np.float32)
    keep[:, :, 0] = 0.0
    put("scan_mask", keep.reshape(P, -1))
    vec("maa_x", f[L0 + "time_maa_x"])
    put("maa", f[L0 + "time_maa"].reshape(8, P).T)
    rows("maa_w1", f[L0 + "maa_w1"].T)
    put("maa_w2", f[L0 + "maa_w2"].reshape(P, D))
    rows("wa_w1", f[L0 + "decay_w1"].T, 0, 112)
    rows("wa_w1", f[L0 + "aaa_w1"].T, 64, 112)
    rows("wa_w1", f[L0 + "ma_w1"].T, 96, 112)
    put("wa_w2", f[L0 + "decay_w2"])
    put("wa_w2", f[L0 + "aaa_w2"], 64)
    put("wa_w2", f[L0 + "ma_w2"], 96)
    rows("k_w1", f[L0 + "kkk_w1"].T, 0, 48)
    rows("k_w1", f[L0 + "mk_w1"].T, 32, 48)
    put("k_w2", f[L0 + "kkk_w2"])
    put("k_w2", f[L0 + "mk_w2"], 32)
    rows("gate_w1", f[L0 + "gate_w1"].T)
    put("gate_w2", f[L0 + "gate_w2"])
    for nm in ("Wr", "Wk", "Wv", "Wo"):
        rows(nm, f[L0 + nm].T)
    for nm, src in (("decay", "time_decay"), ("faaaa", "time_faaaa"), ("aaaaa", "time_aaaaa"),
                    ("misc_a", "time_misc_a"), ("misc_k", "time_misc_k"), ("ln_w", "ln_w"), ("ln_b", "ln_b")):
        vec(nm, f[L0 + src])
    rows("base_W", f[F0 + "base_W"].T)
    vec("base_b", f[F0 + "base_b"])
    put("shared_A", f[F0 + "shared_A"])
    put("shared_B", f[F0 + "shared_B"].T)
    rows("routed_A", f[F0 + "routed_A"].reshape(96, D).T)
    put("routed_B", f[F0 + "routed_B"].transpose(0, 2, 1).reshape(96, D))
    rows("router_W", f[F0 + "router_W"].T)
    put("router_b", f[F0 + "router_b"].reshape(1, 6))
    put("expert_before", np.tile(np.tril(np.ones((6, 6), np.float32), -1).reshape(1, 36), (P, 1)))
    for nm, src in (("Wq1", "Wq"), ("Wk1", "Wk"), ("Wv1", "Wv"), ("Wo1", "Wo"), ("W1", "W1"), ("W2", "W2")):
        rows(nm, f[L1 + src].T)
    put("sig", f[L1 + "head_signatures"].T)
    for nm in ("bq", "bk", "bo", "b1"):
        vec(nm, f[L1 + nm])
    put("bv", np.broadcast_to(f[L1 + "bv"].reshape(1, D), (P, D)))
    put("b2", f[L1 + "b2"].reshape(64, 1))
    put("head_mask", np.kron(np.eye(8, dtype=np.float32), np.ones((16, 1), np.float32)))
    who = (np.arange(P) // 16) % 2
    put("pair_ind", np.stack([who == 0, who == 1]).astype(np.float32))
    key = (np.arange(512) // 16) % 2
    put("pair_neg", np.stack([key != 0, key != 1]).astype(np.float32) * np.float32(NEG))
    put("ones_row", np.ones((1, P), np.float32))
    vec("f_bias", f["L1_ffn_bias"])

    ang = 2.0 * np.pi * ((np.arange(D)[:, None] * np.arange(D)[None, :]) % D) / D
    mats = {"wfr": f["L1_ffn_w_freq_real"], "wfi": f["L1_ffn_w_freq_imag"],
            "Fr": np.cos(ang), "Fi": -np.sin(ang), "nFi": np.sin(ang),
            "Gr": np.cos(ang) / D, "nGi": -np.sin(ang) / D}
    for nm, m in mats.items():
        at = where_s[nm][0]
        dft[:, at:at + D] = m[0:P]
        dft[:, at + D:at + 2 * D] = m[P:2 * P]

    rows_x = STRIDE * TC * (CHUNKS - 1) + SM1 + XROWS2
    xp = np.zeros((rows_x, B * C_IN), np.float32)
    xp[PAD:PAD + T_IN] = f["x"].reshape(2, 8, T_IN, C_IN).transpose(2, 1, 0, 3).reshape(T_IN, B * C_IN)[:rows_x - PAD]

    nc = bacc.Bacc("TRN2", target_bir_lowering=False, num_devices=1)
    arrays = {"x_in": xp, "params_in": prm, "dft_in": dft}
    args = [nc.dram_tensor(k, a.shape, mybir.dt.from_np(a.dtype), kind="ExternalInput").ap() for k, a in arrays.items()]
    out = nc.dram_tensor("out", (B, T, D), F32, kind="ExternalOutput").ap()
    tower(nc, *args, out)
    r = run_bass_kernel_spmd(nc, [arrays], core_ids=[0])
    return r.results[0]["out"]
```

```python
import math
from contextlib import ExitStack

import concourse.bass as bass
from concourse import mybir

P = 128
B, T_IN, C_IN = 16, 750, 64
D = 256
KT, STRIDE, KG, PAD = 32, 4, 9, 4
T = (T_IN - KT) // STRIDE + 1
TC = 30
CHUNKS = T // TC
N = TC * B
SM = STRIDE * (TC - 1) + KT
SM1 = P - (KG - 1)
SM2 = SM - SM1
XROWS2 = SM2 + KG - 1
HEADS, HS = 16, 16
EXPERTS, RANK = 6, 16
TILES = [(0, 128), (128, 128), (256, 128), (384, 96)]
NT = len(TILES)
NEG = -1.0e30
BANK_T = 15
YG = 3
RING = 3
F_NORMS, B_NORMS = 2, 4
F_OWN = 4
SMALL = 21

F32 = mybir.dt.float32
BF16 = mybir.dt.bfloat16
ALU = mybir.AluOpType
ACT = mybir.ActivationFunctionType
AX = mybir.AxisListType.X
LN_EXP = "natural_log_exp_and_others"


PACK = [
    ("w_temporal", KT), ("w_proj", D), ("gauss", SM1), ("ident", P), ("b_proj", 2), ("ln_gamma", 2), ("ln_beta", 2),
    ("ones256", P), ("head_ones", P), ("head_mean", P), ("scan_mask", N * 2),
    ("maa_x", 2), ("maa", 8), ("maa_w1", 2 * 128), ("maa_w2", D), ("wa_w1", 2 * 112), ("wa_w2", D),
    ("k_w1", 2 * 48), ("k_w2", D), ("gate_w1", 2 * 128), ("gate_w2", D), ("Wr", 2 * D), ("Wk", 2 * D), ("Wv", 2 * D),
    ("Wo", 2 * D), ("decay", 2), ("faaaa", 2), ("aaaaa", 2), ("misc_a", 2), ("misc_k", 2), ("ln_w", 2), ("ln_b", 2),
    ("base_W", 2 * D), ("base_b", 2), ("shared_A", D), ("shared_B", D), ("routed_A", 2 * 96), ("routed_B", D),
    ("router_W", 2 * 6), ("router_b", 6), ("expert_before", 36),
    ("Wq1", 2 * D), ("Wk1", 2 * D), ("Wv1", 2 * D), ("Wo1", 2 * D), ("W1", 2 * D), ("W2", 2 * 64), ("sig", 16),
    ("bq", 2), ("bk", 2), ("bv", D), ("bo", 2), ("b1", 2), ("b2", 1), ("head_mask", 8),
    ("pair_ind", P), ("pair_neg", 512), ("ones_row", P), ("f_bias", 2),
]
SETUP = [("wfr", 2 * D), ("wfi", 2 * D), ("Fr", 2 * D), ("Fi", 2 * D), ("nFi", 2 * D), ("Gr", 2 * D), ("nGi", 2 * D)]


def offsets(pack):
    at, out = 0, {}
    for name, n in pack:
        out[name] = (at, n)
        at += n
    return out, at



BACK = """y_turn gn_mean gn_xc zero0 gn_sq G gn_var gn_std gn_out gn_affine bonus gated Wo h1
    ln2_mean ln2_xc zero1 ln2_sq ln2_var ln2_std ln2_out router h96 router_max base h96_sb router_exp zero2 gates rank top2
    top2_sum w96 hw experts h2 ln3_mean ln3_xc ln3_sq ln3_var ln3_std ln3_out k q k_bias q_sb W1 hid W2 V tsg Vx kx0
    hl hl_max hl_exp sc0 hl_gate kx1 p0 sc1 e0 kx2 p1 t0 av0 sc2 e1 kx3 p2 t1 av1 sc3 e2 p3 t2 av2 e3 t3 av3 gz gx gx_sb
    O Wo1 h3 ln4_mean ln4_xc ln4_sq h_bias ln4_var res_h ln4_std ln4_out result result_sb""".split()
FRONT = """proj proj_sb ln0_mean ln0_xc ln0_sq ln0_var ln0_std ln0_out ln0_affine ln1_mean ln1_xc ln1_sq ln1_var
    ln1_std ln1_out xx mix lo lo_sb lo2_0 lo2_1 tmp0 xm0 tmp1 xm1 lo2_2 tmp2 xm2 lo2_3 wa wa_sb k1 tmp3 xm3 r k1_sb g1
    r_sb kp g1_sb vp k_sb a v_sb ma a_sb z ma_sb z_sb z_abs mk mix0 kkl mk_sb mix1 kkr kk_sq mix2 ss z_log kmix lsig
    wm rn ld norm cum ek kkn k2 rkp Pd kka rk scaled_a scaled_k scaled_b scaled_q rkv""".split()
CONV = ["smooth0", "smooth_sb0", "smooth1", "smooth_sb1"] + [f"tap{k}" for k in range(KT)]
SLOTS = 4 * TC
SETUP_LEVELS = ["fold", "folds", "fold_m", "fold_sb", "folded"]
STAGE_OF = {level: name for name, levels in (("back", BACK), ("keep", ["keep"]), ("front", FRONT), ("conv", CONV),
                                             ("setup", SETUP_LEVELS), ("clock", ["+"])) for level in levels}


def places(rows):
    rows = rows.split(";")
    assert len(rows) == TC
    return [(STAGE_OF[level], level, 4 * t + k) for t, row in enumerate(rows) for k, cell in enumerate(row.split("|"))
            for level in cell.split()]


def in_order(levels):
    return [(STAGE_OF[level], level, 0) for level in levels.split()]


PROLOGUE = in_order("""
    smooth0 smooth_sb0 smooth1 smooth_sb1 fold tap0 tap1 tap2 tap3 tap4 tap5 tap6 tap7 tap8 tap9 tap10 tap11
    tap12 tap13 tap14 tap15 tap16 tap17 tap18 tap19 tap20 tap21 tap22 tap23 tap24 tap25 tap26 tap27 tap28 tap29
    tap30 tap31 proj proj_sb folds ln0_mean ln0_xc ln0_sq ln0_var fold_m ln0_std ln0_out ln0_affine ln1_mean
    fold_sb ln1_xc ln1_sq + + ln1_var ln1_std ln1_out xx mix + + + + + lo lo_sb + + + + lo2_0 lo2_1 tmp0 xm0
    tmp1 xm1 + + lo2_2 tmp2 xm2 + + + + + lo2_3 wa wa_sb + k1 tmp3 xm3 r k1_sb + + + + + + g1 r_sb + + kp g1_sb
    + + + + + + vp k_sb + + a v_sb ma a_sb z ma_sb z_sb z_abs + + + + + mk mix0 kkl mk_sb mix1 kkr kk_sq mix2 +
    + + + + + + + + ss z_log kmix lsig wm rn ld norm cum ek kkn k2 rkp Pd kka scaled_k scaled_q + + + + + + + +
    + + + + + rk scaled_a scaled_b rkv folded""")
FIRST = places("""
    keep | smooth0 | smooth_sb0 smooth1 smooth_sb1 | ;
     | tap0 tap1 tap2 tap3 | tap4 tap5 | ;
     | tap6 |  | ;
     |  |  | tap7 ;
     |  |  | tap8 tap9 tap10 tap11 tap12 ;
    tap13 |  |  | ;
     |  | tap14 | ;
     |  | tap15 | ;
    tap16 tap17 |  | tap18 | ;
     | tap19 tap20 tap21 tap22 tap23 | tap24 | tap25 tap26 tap27 tap28 tap29 tap30 ;
    tap31 |  |  | proj_sb ;
    proj |  |  | ;
     | ln0_sq ln0_mean |  | ln0_xc ;
    ln0_var |  |  | ln1_mean ;
    ln0_out |  |  | ln1_var ;
    ln0_std ln1_xc |  |  | ln0_affine ;
    ln1_out xm0 ln1_sq xx ln1_std mix | lo xm1 | lo2_0 | ;
    lo2_1 tmp0 lo2_2 lo_sb |  |  | tmp1 wa_sb tmp2 lo2_3 ;
     |  |  | tmp3 k1_sb r_sb ;
    xm2 wa |  |  | k1 ;
    r |  |  | ;
     | g1 |  | ;
     | g1_sb | kp vp | xm3 a ;
     |  |  | ;
    k_sb ma |  |  | ;
    mix0 | z |  | mix1 v_sb z_sb mk ;
    a_sb |  |  | ;
    kkl |  | ma_sb kkr z_abs | ss ;
     | mix2 mk_sb | lsig kk_sq z_log ld kmix wm rn | cum kka rk ;
    scaled_k | kkn k2 | rkp | scaled_a norm scaled_b ek rkv scaled_q Pd""")
BODY = places("""
    gn_mean G zero0 gn_var |  | y_turn gn_xc | ;
     | gn_out gn_sq |  | gn_std ;
    bonus Wo gated h1 zero1 | ln2_mean smooth0 | gn_affine ln2_xc | ln2_sq smooth_sb0 ;
    ln2_std ln2_var | smooth1 | router h96 h96_sb | zero2 ln2_out router_max gates rank ;
    base router_exp w96 top2 experts top2_sum smooth_sb1 tap0 | ln3_mean hw h2 tap1 tap2 tap3 tap4 tap5 tap6 |
        tap7 tap8 tap9 | ln3_sq tap10 ;
    ln3_var ln3_xc ln3_std tap11 tap12 tap13 |  | tap14 tap15 tap16 tap17 | k ln3_out ;
     | tap18 tap19 tap20 |  | k_bias q tap21 tap22 ;
    W1 tap23 tap24 | tap25 | q_sb | hid tsg ;
    W2 | V hl kx0 |  | Vx hl_exp hl_max ;
    hl_gate | kx1 e0 sc0 sc1 p0 |  | kx2 p1 t0 e1 tap26 tap27 ;
     | av0 p2 t1 sc2 av1 sc3 av2 | tap28 | p3 t2 av3 kx3 t3 e2 e3 ;
    gx gz |  | tap29 | O ;
    tap30 tap31 | Wo1 gx_sb | ln4_sq | ;
    h3 |  | ln4_mean h_bias | ln4_std ln4_xc ln4_var ;
     | res_h result_sb |  | ;
    result ln4_out keep |  |  | proj proj_sb ;
     | ln0_mean ln0_xc ln0_var |  | ;
    ln1_mean ln0_out |  |  | ;
    ln1_xc ln0_sq ln1_var |  | ln0_std | ln1_out ;
     | xx ln0_affine | ln1_sq ln1_std lo mix lo_sb | lo2_0 lo2_1 ;
     | wa_sb lo2_2 | lo2_3 xm0 tmp0 k1_sb tmp1 | xm1 r_sb xm2 ;
    wa k1 tmp2 |  |  | ;
    g1_sb tmp3 xm3 r |  |  | ;
     | g1 kp |  | ;
    vp |  |  | ;
    a |  | k_sb ma | v_sb z a_sb ;
     |  |  | mix0 mk z_sb ;
    kkl mix1 |  | mix2 ma_sb | kkr z_abs ;
     |  |  | mk_sb kk_sq ;
    z_log ss kmix | ld norm ek lsig wm rn cum rk | kkn k2 rkp scaled_a | kka scaled_b Pd scaled_k rkv scaled_q""")
LAST = places("""
    gn_mean y_turn |  |  | gn_xc ;
     | G gn_sq |  | ;
    gn_var |  |  | ;
     | gn_out |  | ;
     |  |  | zero0 Wo bonus ;
    gn_std gn_affine gated | ln2_mean |  | h1 ln2_var ln2_xc ;
     |  |  | router h96 base ln2_out ln2_sq ;
     | ln2_std router_max w96 gates | rank top2 top2_sum zero1 h96_sb experts hw | ;
    h2 ln3_mean | zero2 |  | ln3_var ;
    ln3_xc | router_exp |  | ;
     |  | k ln3_out | q ;
     |  | ln3_sq | ;
     | W1 | ln3_std | ;
     | k_bias |  | ;
     | W2 |  | ;
     | V | q_sb hl hid tsg | ;
    Vx sc0 hl_max | hl_gate kx0 |  | sc1 hl_exp av0 kx1 p0 ;
    p1 sc2 e0 | t0 |  | ;
    kx2 p2 e1 av1 sc3 t1 |  | p3 | av2 t2 t3 kx3 e2 e3 gx_sb ln4_sq ;
     |  | gz av3 | ;
     |  |  | ;
    gx |  |  | ;
     |  |  | O ;
    Wo1 |  |  | h3 ln4_mean h_bias ;
     | ln4_std |  | ;
     |  |  | ln4_var ln4_xc ;
     |  | result_sb | ;
    res_h |  |  | ;
    ln4_out |  |  | result keep ;
     |  |  |""")
EPILOGUE = in_order("""
    y_turn + + gn_mean gn_xc zero0 gn_sq + + + G gn_var gn_std gn_out gn_affine bonus gated + + + + + + + + + +
    + + + + + + + Wo h1 ln2_mean ln2_xc zero1 ln2_sq ln2_var ln2_std ln2_out + + + + + + router h96 router_max
    base h96_sb router_exp zero2 gates rank top2 top2_sum + + + w96 hw experts h2 ln3_mean ln3_xc ln3_sq + + +
    ln3_var ln3_std ln3_out + + + + k q k_bias q_sb W1 hid + + W2 V tsg Vx kx0 + + hl hl_max hl_exp + + + + +
    sc0 hl_gate kx1 p0 + + sc1 e0 kx2 p1 t0 + + + + + + + + + + av0 sc2 e1 kx3 p2 t1 + + + + + + + + + av1 sc3
    e2 p3 t2 + + + + + + + + + + + + + + + av2 e3 t3 av3 gz gx gx_sb O + + + Wo1 h3 ln4_mean ln4_xc ln4_sq
    h_bias + + + ln4_var res_h ln4_std ln4_out result result_sb""")


def tower(nc: bass.Bass, x: bass.AP, params: bass.AP, dft: bass.AP, out: bass.AP):
    where, n_params = offsets(PACK)
    where_s, n_setup = offsets(SETUP)
    ctx = ExitStack()
    with ctx:
        def sb(name, shape, dt=F32):
            return ctx.enter_context(nc.sbuf_tensor(name, shape, dt))

        def pb(name, shape, dt=F32):
            return ctx.enter_context(nc.psum_tensor(name, shape, dt))

        sems = {}

        def s(name):
            if name not in sems:
                sems[name] = ctx.enter_context(nc.semaphore("s_" + name))
            return sems[name]

        state = pb("state", [P, 2, 512])
        pp = pb("pp", [P, 4, 512])
        PA, PB = pp[:, 0:2, 0:N], pp[:, 2:4, 0:N]
        y_ps = pb("y_ps", [P, 512])
        u_ps = pb("u_ps", [P, 512])
        u = u_ps[:, 0:32].rearrange("p (a i) -> p a i", a=2)
        prm = sb("prm", [P, n_params])

        def w(name, rows=P, r0=0):
            a, n = where[name]
            return prm[r0:r0 + rows, a:a + n]

        def w2(name, half, rows=P, r0=0):
            a, n = where[name]
            return prm[r0:r0 + rows, a + half * (n // 2):a + (half + 1) * (n // 2)]

        def col(name, k=0, rows=P, r0=0):
            a, _ = where[name]
            return prm[r0:r0 + rows, a + k:a + k + 1]

        baseW = sb("baseW", [P, 2, D])
        dftM = sb("dftM", [P, 2, D])
        indb = sb("indb", [2, P], BF16)
        negb = sb("negb", [2, 512], BF16)
        bqs = sb("bqs", [P, 2])
        half_c = sb("half_c", [P, 1])
        zero_c = sb("zero_c", [P, 1])
        eps_c = sb("eps_c", [P, 3])

        x1 = sb("x1", [P, B * C_IN])
        x2 = sb("x2", [XROWS2, B * C_IN])
        Xs = sb("Xs", [P, 8, SM])
        Xc = sb("Xc", [P, TC * 8])
        tap = sb("tap", [P, 4, TC * 8])

        def act_t(name):
            return sb(name, [P, 2, N])

        H, RKV, l_g = act_t("H"), act_t("RKV"), sb("l_g", [P, N])
        Hb, RKVb, l_gb = act_t("Hb"), act_t("RKVb"), sb("l_gb", [P, N])
        XN = sb("XN", [P, 2, B + N])
        xcsq = sb("xcsq", [P, 4 * N])
        xc, sq = [xcsq[:, k * 2 * N:(k + 1) * 2 * N].rearrange("p (a n) -> p a n", a=2) for k in range(2)]
        xn = act_t("xn")
        rstd = sb("rstd", [P, N])
        low = sb("low", [P, N])
        l_wa = sb("l_wa", [112, N])
        l_k = sb("l_k", [48, N])
        Pd = sb("Pd", [P, 2, B + N])
        ops_s = sb("ops_s", [P, 5, 960])
        A_s, B_s, K_s, Q_s, V_s = [ops_s[:, k, :].rearrange("p (t a i) -> p t a i", a=2, i=HS) for k in range(5)]
        P_s = sb("P_s", [P, 2, HS])
        S_sb = sb("S_sb", [P, 2, HS, HS])
        Ma, ub = [sb(nm, [P, 2, HS, HS]) for nm in ("Ma", "ub")]
        vk = sb("vk", [P, RING, 2, HS, HS])
        Mq = sb("Mq", [P, 3, 2, HS, HS])
        Mh = sb("Mh", [P, 2 * YG, 2, HS, HS // 2])
        Y_sb = sb("Y_sb", [P, 2, N])
        arena = sb("arena", [P, 13 * 960])

        def at_(a, n, k=2):
            return arena[:, a:a + n].rearrange("p (a n) -> p a n", a=k)

        def slot(k):
            return at_(k * 960, 960)

        xm = [slot(k) for k in range(4)]
        xrg, xwa, xk, xv = xm
        tmps = [slot(4), slot(5)]
        gma, ga, nz, gmk, mix4, mz, K0, kk, k2 = [slot(k) for k in range(9)]
        ld, Pinv = nz, nz
        ek, kka, cum, R, V, xx = gmk, ga, slot(9), slot(10), slot(11), slot(12)
        Asc, Bsc, Ksc, Qsc = mz, ga, cum, R
        rst, gna = slot(0), slot(1)
        hid = slot(0)
        kx = [arena[:, k * 2048:(k + 1) * 2048].rearrange("p (h e n) -> p h e n", h=2, e=8) for k in range(2)]
        PT = [arena[:, 4096 + i * 2048:4096 + (i + 1) * 2048].rearrange("p (h n) -> p h n", h=16) for i in range(2)]
        Vx = arena[:, 8192:10240].rearrange("p (i a b n) -> p i a b n", i=NT, a=8, b=2)
        q1, k1 = at_(10240, 960), at_(11200, 960)
        O, Gx = q1, k1
        sw96 = arena[:, 0:NT * 96].rearrange("p (i e r) -> p i e r", i=NT, e=6)
        gz = arena[:, 0:1024].rearrange("p (i h d) -> p i h d", i=NT, h=16)
        Out = arena[:, 0:NT * D].rearrange("p (i n) -> p i n", i=NT)
        P1 = xcsq[:, 0:1024].rearrange("p (k h n) -> p k h n", k=2, n=32)
        lg = sb("lg", [P, NT, 6])
        fs = [arena[:, 2048 + 24 * i:2072 + 24 * i].rearrange("p (i e) -> p i e", i=NT) for i in range(4)]
        f1 = [sb(f"f1{i}", [P, NT, 1]) for i in range(4)]
        cmp1, cmp2 = [arena[:, 2144 + 144 * i:2288 + 144 * i].rearrange("p (i e f) -> p i e f", i=NT, e=6)
                      for i in range(2)]
        h96 = low[0:96, :]
        hl = sb("hl", [P, NT, 16])
        hl2 = arena[:, 2432:2496].rearrange("p (i h) -> p i h", i=NT)
        mx = sb("mx", [P, NT, 16])
        Z = sb("Z", [P, NT, 16])
        tsg = l_gb[0:64, :]

        dft_s = ops_s[:, :, :].rearrange("p k n -> p (k n)")[:, 0:n_setup]
        At = [ub[:, :, :, :].rearrange("p a i j -> p a (i j)"), Ma[:, :, :, :].rearrange("p a i j -> p a (i j)")]
        fold_ps, dftM_ps, At_ps = y_ps[:, :], u_ps[:, :], [state[:, 0, :], state[:, 1, :]]

        def ws(name, half):
            a, n = where_s[name]
            return dft_s[:, a + half * D:a + (half + 1) * D]

        block = ctx.enter_context(nc.Block())

        def tb(ap):
            return ap.rearrange("p a (t b) -> p a t b", b=B)

        def bh(ap):
            return ap.unsqueeze(1).broadcast_to([P, 2, N])

        def vq(bank0, i, n):
            return pp[0:n, bank0 + i // 2, (i % 2) * D:(i % 2 + 1) * D]

        def filler(plan, clock, **stages):
            stages["clock"] = clock() if clock else iter(())
            ahead = {name: next(stage, None) for name, stage in stages.items()}
            done = [0]

            def fill(k=SLOTS):
                while done[0] < len(plan) and (plan[done[0]][2] <= k or k == SLOTS):
                    name, level, _ = plan[done[0]]
                    done[0] += 1
                    while ahead[name] == level:
                        ahead[name] = next(stages[name], None)
                        if name == "clock":
                            break
                assert k < SLOTS or not any(ahead[name] for name in ahead if name != "clock"), ahead
            return fill

        def whole(scan, clock, setup, conv, front, keep, back, tail, fori):
            filler(PROLOGUE, clock, conv=conv(0, False, False), setup=setup(), front=front(0, False, False))()
            tail(0, True)
            scan(0, filler(FIRST, clock, keep=keep(0), conv=conv(1, True, False), front=front(1, True, False)), True, False)
            tail(1, False)
            with fori(1, CHUNKS - 1) as c:
                scan(c, filler(BODY, clock, back=back(c - 1, c + 1, True), keep=keep(c), conv=conv(c + 1, True, True),
                               front=front(c + 1, True, True)), False, False)
                tail(c + 1, False)
            scan(CHUNKS - 1, filler(LAST, clock, back=back(CHUNKS - 2, CHUNKS, False), keep=keep(CHUNKS - 1)), False, True)
            filler(EPILOGUE, clock, back=back(CHUNKS - 1, CHUNKS, False))()

        @block.sync
        def _(sp):
            def load(c):
                sp.dma_start(x1[:, :], x[bass.ds(c * (STRIDE * TC), P), :]).then_inc(s("x_in"), 16)
                sp.dma_start(x2[:, :], x[bass.ds(c * (STRIDE * TC) + SM1, XROWS2), :]).then_inc(s("x_in"), 16)

            def store(c):
                for i, (t0, n) in enumerate(TILES):
                    dst = out.rearrange("b t c -> t b c")[bass.ds(c * TC + t0 // B, n // B)]
                    sp.dma_start(dst, Out[0:n, i, :]).then_inc(s("out_dram"), 16)

            load(0)
            cuts = [0, where["ones256"][0], where["base_W"][0], n_params]
            for k, name in enumerate(["tok_in", "mix_in", "rest_in"]):
                sp.dma_start(prm[:, cuts[k]:cuts[k + 1]], params[:, cuts[k]:cuts[k + 1]]).then_inc(s(name), 16)
            sp.dma_start(dft_s, dft).then_inc(s("dft_in"), 16)
            for c in range(1, 3):
                sp.wait_ge(s("smooth_ps"), 2 * c)
                load(c)
            with sp.Fori(0, CHUNKS - 3) as c:
                sp.wait_ge(s("smooth_ps"), c * 2 + 6)
                load(c + 3)
                sp.wait_ge(s("out_sb"), c + 1)
                store(c)
            for c in range(CHUNKS - 3, CHUNKS):
                sp.wait_ge(s("out_sb"), c + 1)
                store(c)
            sp.wait_ge(s("out_dram"), 16 * NT * CHUNKS)

        @block.tensor
        def _(pe):
            mm = nc.tensor.matmul
            ident = w("ident")
            def stats(src, bank, sem, half_ready, n):
                for k in range(2):
                    pe.wait_ge(half_ready, n + (k + 1))
                    last = mm(pp[:, bank, 0:N], w("ones256"), src[:, k, :], start=(k == 0), stop=(k == 1))
                last.then_inc(sem, 1)

            def dense(dst, wt, src, sem, each=False):
                for h in range(2):
                    for k in range(2):
                        last = mm(dst[:, h, :], w2(wt, k)[:, h * P:(h + 1) * P], src[:, k, :],
                                  start=(k == 0), stop=(k == 1))
                    if each or h == 1:
                        last.then_inc(sem, 1)

            def lowrank(dst, wt, src, sem):
                for k in range(2):
                    last = mm(dst, w2(wt, k), src[:, k, :], start=(k == 0), stop=(k == 1))
                last.then_inc(sem, 1)

            def expand(dst, wt, r0, rows, src, sem):
                for h in range(2):
                    last = mm(dst[:, h, :], w(wt, rows, r0)[:, h * P:(h + 1) * P], src[r0:r0 + rows, :],
                              start=True, stop=True)
                last.then_inc(sem, 1)

            def per_head(dst, ones, src, sem):
                for h in range(2):
                    last = mm(dst[:, h, :], w(ones), src[:, h, :], start=True, stop=True)
                last.then_inc(sem, 1)

            def setup():
                yield "fold"
                pe.wait_ge(s("rest_in"), 16)
                pe.wait_ge(s("dft_in"), 16)
                for h in range(2):
                    last = mm(fold_ps[:, h * D:(h + 1) * D], w("shared_A", 16)[:, h * P:(h + 1) * P],
                              w("shared_B", 16), start=True, stop=True)
                last.then_inc(s("fold_ps"), 1)
                for im in range(2):
                    first, second = (("wfr", "Fr"), ("wfi", "nFi")) if im == 0 else (("wfi", "Fr"), ("wfr", "Fi"))
                    for m in range(2):
                        dst = At_ps[im][:, m * D:(m + 1) * D]
                        for k in range(2):
                            mm(dst, ws(first[0], k)[:, m * P:(m + 1) * P], ws(first[1], k), start=(k == 0), stop=False)
                            last = mm(dst, ws(second[0], k)[:, m * P:(m + 1) * P], ws(second[1], k),
                                      start=False, stop=(k == 1))
                last.then_inc(s("fw_ps"), 1)
                yield "fold_m"
                pe.wait_ge(s("fw_sb"), 1)
                for m in range(2):
                    dst = dftM_ps[:, m * D:(m + 1) * D]
                    for k in range(2):
                        mm(dst, At[0][:, k, m * P:(m + 1) * P], ws("Gr", k), start=(k == 0), stop=False)
                        last = mm(dst, At[1][:, k, m * P:(m + 1) * P], ws("nGi", k), start=False, stop=(k == 1))
                last.then_inc(s("dftM_ps"), 1)
                yield "folded"
                pe.wait_ge(s("baseW"), 1)
                pe.wait_ge(s("dftM"), 1)

            def conv(c, again, later):
                for part in range(2):
                    yield f"smooth{part}"
                    if part == 0:
                        if not again:
                            pe.wait_ge(s("tok_in"), 16)
                        pe.wait_ge(s("x_in"), c * 32 + 32)
                        if again:
                            pe.wait_ge(s("rn"), c)
                        if later:
                            pe.wait_ge(s("h1"), c * 2 - 2)
                    else:
                        pe.wait_ge(s("smooth_sb"), c * 2 + 1)
                    for b in range(4):
                        dst = pp[:, 2 + b // 2, (b % 2) * SM:(b % 2 + 1) * SM]
                        b8 = (4 * part + b) * P
                        mm(dst[:, 0:SM1], x1[:, b8:b8 + P], w("gauss"), start=True, stop=True)
                        last = mm(dst[:, SM1:SM], x2[:, b8:b8 + P], w("gauss", XROWS2)[:, 0:SM2],
                                  start=True, stop=True)
                    last.then_inc(s("smooth_ps"), 1)

            def front(c, again, later):
                yield "proj"
                pe.wait_ge(s("conv"), c + 1)
                pe.wait_ge(s("smooth_sb"), c * 2 + 2)
                if again:
                    pe.wait_ge(s("rkv"), c)
                if later:
                    pe.wait_ge(s("out_sb"), c - 1)
                for h in range(2):
                    for g in range(2):
                        last = mm(pp[:, 2 * g + h, 0:TC * 8], w("w_proj", 64, 64 * g)[:, h * P:(h + 1) * P],
                                  Xc[64 * g:64 * g + 64, :], start=True, stop=True)
                last.then_inc(s("proj_ps"), 1)
                yield "ln0_mean"
                if not again:
                    pe.wait_ge(s("mix_in"), 16)
                stats(H, 0, s("f_mean"), s("proj_sb"), c * 2)
                yield "ln0_var"
                stats(sq, 1, s("f_var"), s("f_sq"), c * (2 * F_NORMS))
                yield "ln1_mean"
                stats(H, 2, s("f_mean"), s("h0"), c * 2)
                yield "ln1_var"
                stats(sq, 3, s("f_var"), s("f_sq"), c * (2 * F_NORMS) + 2)
                yield "lo"
                pe.wait_ge(s("mix"), c + 1)
                lowrank(pp[:, 0, 0:N], "maa_w1", xn, s("lo_ps"))
                for g in range(4):
                    yield f"lo2_{g}"
                    if g == 0:
                        pe.wait_ge(s("lo_sb"), c + 1)
                    if g >= 2:
                        pe.wait_ge(s("tmp"), c * 4 + g - 1)
                    expand([PB, PA][g % 2], "maa_w2", 32 * g, 32, low, s("lo2_ps"))
                yield "wa"
                pe.wait_ge(s("xm"), c * 4 + 2)
                pe.wait_ge(s("tmp"), c * 4 + 3)
                lowrank(pp[0:112, 2, 0:N], "wa_w1", xwa, s("wa_ps"))
                yield "k1"
                pe.wait_ge(s("xm"), c * 4 + 3)
                lowrank(pp[0:48, 3, 0:N], "k_w1", xk, s("k1_ps"))
                yield "r"
                pe.wait_ge(s("tmp"), c * 4 + 4)
                dense(PA, "Wr", xrg, s("r_ps"))
                yield "g1"
                pe.wait_ge(s("wa_sb"), c + 1)
                lowrank(pp[:, 2, 0:N], "gate_w1", xrg, s("g1_ps"))
                yield "kp"
                pe.wait_ge(s("r_sb"), c + 1)
                dense(PA, "Wk", xk, s("k_ps"))
                yield "vp"
                pe.wait_ge(s("xm"), c * 4 + 4)
                pe.wait_ge(s("k1_sb"), c + 1)
                pe.wait_ge(s("g1_sb"), c + 1)
                dense(PB, "Wv", xv, s("v_ps"))
                yield "a"
                pe.wait_ge(s("k_sb"), c + 1)
                expand(PA, "wa_w2", 64, 16, l_wa, s("a_ps"))
                yield "ma"
                pe.wait_ge(s("v_sb"), c + 1)
                expand(PB, "wa_w2", 96, 16, l_wa, s("ma_ps"))
                yield "z"
                pe.wait_ge(s("a_sb"), c + 1)
                expand(PA, "wa_w2", 0, 64, l_wa, s("z_ps"))
                yield "mk"
                pe.wait_ge(s("ma_sb"), c + 1)
                expand(PB, "k_w2", 32, 16, l_k, s("mk_ps"))
                yield "kkl"
                pe.wait_ge(s("z_sb"), c + 1)
                pe.wait_ge(s("z_abs"), c + 1)
                expand(PA, "k_w2", 0, 16, l_k, s("kkl_ps"))
                yield "ss"
                pe.wait_ge(s("mk_sb"), c + 1)
                pe.wait_ge(s("kk_sq"), c + 1)
                per_head(PB, "head_ones", sq, s("ss_ps"))
                yield "rk"
                pe.wait_ge(s("rkp"), c + 1)
                per_head(PA, "head_ones", xx, s("rk_ps"))

            def keep(c):
                return
                yield

            def back(c, tails, tokenizer):
                yield "gn_mean"
                pe.wait_ge(s("y_ch"), c + 1)
                per_head(PA, "head_mean", xn, s("b_mean"))
                yield "G"
                pe.wait_ge(s("b_xc"), c * (2 * B_NORMS) + 2)
                pe.wait_ge(s("keep"), c + 1)
                for h in range(2):
                    last = mm(PA[:, h, :], w("gate_w2")[:, h * P:(h + 1) * P], l_gb[:, :], start=True, stop=True)
                last.then_inc(s("g_ps"), 1)
                yield "gn_var"
                for h in range(2):
                    pe.wait_ge(s("b_sq"), c * (2 * B_NORMS) + (h + 1))
                    last = mm(PB[:, h, :], w("head_mean"), sq[:, h, :], start=True, stop=True)
                last.then_inc(s("b_var"), 1)
                yield "Wo"
                pe.wait_ge(s("y_gated"), c + 1)
                dense(PB, "Wo", xn, s("wo_ps"), each=True)
                yield "ln2_mean"
                stats(Hb, 0, s("b_mean"), s("h1"), c * 2)
                yield "ln2_var"
                stats(sq, 1, s("b_var"), s("b_sq"), c * (2 * B_NORMS) + 2)
                yield "router"
                pe.wait_ge(s("ln2_xn"), c + 1)
                for i, (t0, n) in enumerate(TILES):
                    dst = pp[0:n, 0, 8 * i:8 * i + 6]
                    for k in range(2):
                        mm(dst, xn[:, k, t0:t0 + n], w2("router_W", k), start=(k == 0), stop=False)
                    last = mm(dst, w("ones_row", 1)[:, 0:n], w("router_b", 1), start=False, stop=True)
                last.then_inc(s("router_ps"), 1)
                yield "h96"
                lowrank(pp[0:96, 1, 0:N], "routed_A", xn, s("h96_ps"))
                yield "base"
                if tokenizer:
                    pe.wait_ge(s("smooth_sb"), c * 2 + 6)
                for h in range(2):
                    for k in range(2):
                        mm(PB[:, h, :], baseW[:, k, h * P:(h + 1) * P], xn[:, k, :], start=(k == 0), stop=False,
                           skip_group_check=True)
                yield "w96"
                pe.wait_ge(s("sw96"), c + 1)
                for i, (t0, n) in enumerate(TILES):
                    last = mm(pp[0:96, 0, t0:t0 + n], sw96[0:n, i, :, :], ident[0:n, 0:n], start=True, stop=True)
                last.then_inc(s("w96_ps"), 1)
                yield "experts"
                pe.wait_ge(s("hw"), c + 1)
                for h in range(2):
                    mm(PB[:, h, :], w("routed_B", 96)[:, h * P:(h + 1) * P], h96[:, :], start=False, stop=True,
                       skip_group_check=True).then_inc(s("ffn_ps"), 1)
                yield "ln3_mean"
                stats(Hb, 0, s("b_mean"), s("h2"), c * 2)
                yield "ln3_var"
                stats(sq, 1, s("b_var"), s("b_sq"), c * (2 * B_NORMS) + 4)
                yield "k"
                pe.wait_ge(s("ln3_xn"), c + 1)
                dense(PB, "Wk1", xn, s("k1b_ps"))
                yield "q"
                dense(PA, "Wq1", xn, s("q_ps"))
                yield "W1"
                pe.wait_ge(s("k1b_sb"), c + 1)
                dense(PB, "W1", xn, s("hid_ps"))
                yield "W2"
                pe.wait_ge(s("hid_sb"), c + 1)
                pe.wait_ge(s("q_sb"), c + 1)
                for k in range(2):
                    last = mm(pp[0:64, 0, 0:N], w2("W2", k), hid[:, k, :], start=(k == 0), stop=(k == 1))
                last.then_inc(s("tsg_ps"), 1)
                yield "V"
                for i, (t0, n) in enumerate(TILES):
                    for k in range(2):
                        last = mm(vq(2, i, n), xn[:, k, t0:t0 + n], w2("Wv1", k), start=(k == 0), stop=(k == 1))
                last.then_inc(s("v1_ps"), 1)
                yield "hl"
                pe.wait_ge(s("tsg_sb"), c + 1)
                for i, (t0, n) in enumerate(TILES):
                    last = mm(pp[0:n, 1, 16 * i:16 * i + 16], tsg[:, t0:t0 + n], w("sig", 64), start=True, stop=True)
                last.then_inc(s("hl_ps"), 1)

                def scores(i):
                    t0, n = TILES[i]
                    pe.wait_ge(s("kx"), c * NT + i + 1)
                    if i == 0:
                        pe.wait_ge(s("Vx"), c + 1)
                    if i >= 2:
                        pe.wait_ge(s("P1"), c * NT + i - 1)
                    bank = pp[:, 2 + i % 2, :]
                    mm(bank[0:n, :], indb[:, 0:n], negb[:, :], start=True, stop=False, skip_group_check=True)
                    for qd in range(n // 32):
                        for h in range(2):
                            last = mm(bank[32 * qd:32 * qd + 32, h * 256:(h + 1) * 256],
                                      q1[:, h, t0 + 32 * qd:t0 + 32 * qd + 32],
                                      kx[i % 2][:, h, :, 32 * qd:32 * qd + 32], start=False, stop=True,
                                      skip_group_check=True)
                    last.then_inc(s("sc_ps"), 1)

                def av(i):
                    t0, n = TILES[i]
                    pe.wait_ge(s("PT"), c * NT + i + 1)
                    if i == 0:
                        pe.wait_ge(s("hl_sub"), c + 1)
                    for h in range(16):
                        hp, hh = h // 2, h % 2
                        r = 32 * (hp % 4)
                        last = mm(pp[r:r + 32, hp // 4, t0:t0 + n], Vx[0:n, i, hp, hh, :], PT[i % 2][0:n, h, 0:n],
                                  start=(hh == 0), stop=(hh == 1), skip_group_check=True)
                    last.then_inc(s("av_ps"), 1)

                for i in range(NT):
                    yield f"sc{i}"
                    scores(i)
                    if i >= 1:
                        yield f"av{i - 1}"
                        av(i - 1)
                yield f"av{NT - 1}"
                av(NT - 1)
                yield "gx"
                pe.wait_ge(s("gz"), c + 1)
                for h in range(2):
                    for i, (t0, n) in enumerate(TILES):
                        last = mm(pp[:, 2 + h, t0:t0 + n], gz[0:n, i, 8 * h:8 * h + 8, :], ident[0:n, 0:n],
                                  start=True, stop=True)
                last.then_inc(s("gx_ps"), 1)
                yield "Wo1"
                pe.wait_ge(s("O_sb"), c + 1)
                dense(PB, "Wo1", O, s("wo1_ps"), each=True)
                yield "ln4_mean"
                stats(Hb, 0, s("b_mean"), s("h3"), c * 2)
                yield "ln4_var"
                stats(sq, 1, s("b_var"), s("b_sq"), c * (2 * B_NORMS) + 6)
                yield "res_h"
                pe.wait_ge(s("h_bias"), c + 1)
                for i, (t0, n) in enumerate(TILES):
                    for k in range(2):
                        mm(vq(2, i, n)[:, k * P:(k + 1) * P], Hb[:, k, t0:t0 + n], ident,
                           start=(i % 2 == 0 and k == 0), stop=False, skip_group_check=True)
                yield "result"
                pe.wait_ge(s("ln4_xn"), c + 1)
                for i, (t0, n) in enumerate(TILES):
                    for k in range(2):
                        last = mm(vq(2, i, n), xn[:, k, t0:t0 + n], dftM[:, k, :], start=False, stop=(k == 1),
                                  skip_group_check=True)
                last.then_inc(s("out_ps"), 1)

            def tail(c, first):
                pe.wait_ge(s("S_sb"), c + 1)
                for hh in range(2):
                    mm(state[:, hh, 0:256], ident, S_sb[:, hh, :, :], start=True, stop=False,
                       skip_group_check=True).then_inc(s(f"upd{hh}"), 1)

            def outputs(c, g, first):
                t0 = g * YG
                pe.wait_ge(s("Mh"), c * TC + (t0 + YG))
                if t0 == 0:
                    if not first:
                        pe.wait_ge(s("y_sb"), c * 2)
                elif t0 == BANK_T:
                    pe.wait_ge(s("y_sb"), c * 2 + 1)
                dst = y_ps[:, (t0 % BANK_T) * 32:(t0 % BANK_T + YG) * 32]
                slots = (g % 2) * YG
                for j in range(HS // 2):
                    last = mm(dst, ident, Mh[:, slots:slots + YG, :, :, j], start=(j == 0), stop=(j == HS // 2 - 1))
                last.then_inc(s("y_ps"), 1)

            def scan(c, fill, first, last_chunk):
                for t in range(TC):
                    fill(4 * t)
                    if t % YG == 1 and t > YG:
                        outputs(c, t // YG - 1, first)
                    fill(4 * t + 1)
                    for hh in range(2):
                        pe.wait_ge(s("vk"), c * TC + (t + 1))
                        pe.wait_ge(s("Ma"), c * (2 * TC) + (2 * t + hh + 1))
                        if t > 0:
                            pe.wait_ge(s("Mq"), c * TC + t)
                        mm(state[:, hh, 0:256], ident, vk[:, t % RING, hh, :, :], start=False, stop=False,
                           skip_group_check=True)
                    fill(4 * t + 2)
                    for hh in range(2):
                        pe.wait_ge(s("ub"), c * (2 * TC) + (2 * t + hh + 1))
                        mm(state[:, hh, 0:256], ident, ub[:, hh, :, :], start=False, stop=False,
                           skip_group_check=True).then_inc(s(f"upd{hh}"), 1)
                    fill(4 * t + 3)
                fill()
                outputs(c, TC // YG - 1, first)

            def clock():
                while True:
                    yield "+"
                    mm(state[:, 0, 0:256], ident, prm[:, 0:256], start=True, stop=True)

            whole(scan, clock, setup, conv, front, keep, back, tail, pe.Fori)

        @block.scalar
        def _(act):
            a = nc.scalar.activation
            act.wait_ge(s("consts"), 1)
            def halves(dst, src, f, sem, bias=None, scale=None, each=False):
                for h in range(2):
                    kw = {}
                    if bias is not None:
                        kw["bias"] = bias(h)
                    if scale is not None:
                        kw["scale"] = scale if isinstance(scale, float) else scale(h)
                    last = a(dst[:, h, :], src[:, h, :], f, **kw)
                    if each or h == 1:
                        last.then_inc(sem, 1)

            def squares(n, fam):
                for h in range(2):
                    act.wait_ge(s(fam + "xc"), n + (h + 1))
                    a(sq[:, h, :], xc[:, h, :], ACT.Square).then_inc(s(fam + "sq"), 1)

            def inv_std(count, own, fam, var, dst=rstd[:, :], eps=eps_c[:, 0:1]):
                act.wait_ge(s(fam + "var"), count)
                a(dst, var, ACT.Ln, bias=eps).then_inc(s(fam + "own"), 1)
                act.wait_ge(s(fam + "own"), own)
                a(dst, dst, ACT.Exp, scale=-0.5).then_inc(s(fam + "rstd"), 1)

            nc.scalar.preload_act_table_set(LN_EXP)
            act.wait_ge(s("tok_in"), 16)

            def setup():
                yield "folds"
                act.wait_ge(s("rest_in"), 16)
                a(bqs[:, :], w("bq"), ACT.Identity, scale=0.25)
                act.wait_ge(s("fw_ps"), 1)
                a(At[0], At_ps[0], ACT.Identity)
                a(At[1], At_ps[1], ACT.Identity).then_inc(s("fw_sb"), 1)
                yield "fold_sb"
                act.wait_ge(s("dftM_ps"), 1)
                a(dftM[:, :, :], dftM_ps, ACT.Identity).then_inc(s("dftM"), 1)
                yield "folded"
                act.wait_ge(s("dftM"), 1)

            def conv(c, again, later):
                for part in range(2):
                    yield f"smooth_sb{part}"
                    act.wait_ge(s("smooth_ps"), c * 2 + (part + 1))
                    if again and part == 0:
                        act.wait_ge(s("conv"), c)
                    a(Xs[:, 4 * part:4 * part + 4, :], pp[:, 2:4, 0:2 * SM], ACT.Identity).then_inc(s("smooth_sb"), 1)
                for k in range(KT):
                    yield f"tap{k}"
                    if k == 0:
                        act.wait_ge(s("smooth_sb"), c * 2 + 2)
                    if k >= 4:
                        act.wait_ge(s("tap_sum"), c * (KT - 2) + max(k - 4, 1))
                    a(tap[:, k % 4, :].rearrange("p (t a) -> p t a", a=8),
                      Xs[:, :, k:k + STRIDE * (TC - 1) + 1:STRIDE].rearrange("p a t -> p t a"), ACT.Identity,
                      scale=col("w_temporal", k)).then_inc(s("tap"), 1)

            def front(c, again, later):
                yield "proj_sb"
                act.wait_ge(s("proj_ps"), c + 1)
                if again:
                    act.wait_ge(s("keep"), c)
                for h in range(2):
                    for g in range(2):
                        last = a(tb(H[:, :, :])[:, h, :, 8 * g:8 * g + 8],
                                 pp[:, 2 * g + h, 0:TC * 8].rearrange("p (t b) -> p t b", b=8), ACT.Identity,
                                 bias=col("b_proj", h))
                    last.then_inc(s("proj_sb"), 1)
                yield "ln0_sq"
                squares(c * (2 * F_NORMS) + 0, "f_")
                yield "ln0_std"
                inv_std(c * F_NORMS + 1, c * F_OWN + 1, "f_", pp[:, 1, 0:N])
                yield "ln0_affine"
                act.wait_ge(s("ln0_xn"), c + 1)
                halves(H, xn, ACT.Identity, s("h0"), bias=lambda h: col("ln_beta", h), scale=lambda h: col("ln_gamma", h),
                       each=True)
                yield "ln1_sq"
                squares(c * (2 * F_NORMS) + 2, "f_")
                yield "ln1_std"
                inv_std(c * F_NORMS + 2, c * F_OWN + 2, "f_", pp[:, 3, 0:N])
                yield "lo_sb"
                act.wait_ge(s("lo_ps"), c + 1)
                a(low[:, :], pp[:, 0, 0:N], ACT.Tanh).then_inc(s("lo_sb"), 1)
                yield "wa_sb"
                act.wait_ge(s("wa_ps"), c + 1)
                a(l_wa[0:64, :], pp[0:64, 2, 0:N], ACT.Tanh)
                a(l_wa[64:112, :], pp[64:112, 2, 0:N], ACT.Identity).then_inc(s("wa_sb"), 1)
                yield "k1_sb"
                act.wait_ge(s("k1_ps"), c + 1)
                a(l_k[0:16, :], pp[0:16, 3, 0:N], ACT.Tanh)
                a(l_k[32:48, :], pp[32:48, 3, 0:N], ACT.Identity).then_inc(s("k1_sb"), 1)
                yield "r_sb"
                act.wait_ge(s("r_ps"), c + 1)
                a(R, PA, ACT.Identity).then_inc(s("r_sb"), 1)
                yield "g1_sb"
                act.wait_ge(s("g1_ps"), c + 1)
                a(l_g[:, :], pp[:, 2, 0:N], ACT.Tanh).then_inc(s("g1_sb"), 1)
                yield "k_sb"
                act.wait_ge(s("k_ps"), c + 1)
                a(K0, PA, ACT.Identity).then_inc(s("k_sb"), 1)
                yield "v_sb"
                act.wait_ge(s("v_ps"), c + 1)
                a(V, PB, ACT.Identity).then_inc(s("v_sb"), 1)
                yield "a_sb"
                act.wait_ge(s("a_ps"), c + 1)
                halves(ga, PA, ACT.Sigmoid, s("a_sb"), bias=lambda h: col("aaaaa", h))
                yield "ma_sb"
                act.wait_ge(s("ma_ps"), c + 1)
                halves(gma, PB, ACT.Sigmoid, s("ma_sb"), bias=lambda h: col("misc_a", h))
                yield "z_abs"
                act.wait_ge(s("z_sb"), c + 1)
                halves(nz, PA, ACT.Abs, s("z_abs"), bias=lambda h: col("decay", h))
                yield "mk_sb"
                act.wait_ge(s("mk_ps"), c + 1)
                halves(gmk, PB, ACT.Sigmoid, s("mk_sb"), bias=lambda h: col("misc_k", h))
                yield "kk_sq"
                act.wait_ge(s("kkr"), c + 1)
                a(sq[:, :, :], kk, ACT.Square).then_inc(s("kk_sq"), 1)
                nc.scalar.preload_act_table_set(LN_EXP)
                yield "z_log"
                act.wait_ge(s("z_abs"), c + 1)
                a(nz, nz, ACT.Exp, scale=-1.0).then_inc(s("f_own"), 1)
                act.wait_ge(s("f_own"), c * F_OWN + 3)
                a(nz, nz, ACT.Ln, bias=1.0).then_inc(s("l1p"), 1)
                yield "ld"
                act.wait_ge(s("lsig"), c + 1)
                a(ld.rearrange("p a n -> p (a n)").rearrange("p (a b t) -> p a t b", a=2, t=TC), tb(mz), ACT.Exp,
                  bias=half_c[:, 0:1]).then_inc(s("ld"), 1)
                yield "norm"
                act.wait_ge(s("rn"), c + 1)
                a(xc[:, :, :], xc[:, :, :], ACT.Ln, scale=2.0 ** 30).then_inc(s("f_own"), 1)
                act.wait_ge(s("f_own"), c * F_OWN + 4)
                a(xc[:, :, :], xc[:, :, :], ACT.Exp, scale=-0.5, bias=eps_c[:, 2:3]).then_inc(s("norm"), 1)
                yield "ek"
                act.wait_ge(s("wm"), c + 1)
                a(ek, ek, ACT.Exp).then_inc(s("ek"), 1)
                yield "Pd"
                act.wait_ge(s("cum"), c + 1)
                if again:
                    act.wait_ge(s("scan_in"), c)
                cumv = cum.rearrange("p a n -> p (a n)").rearrange("p (a b t) -> p a t b", a=2, t=TC)
                a(tb(Pd[:, :, B:]), cumv, ACT.Exp, scale=-1.0)
                a(tb(Pinv), cumv, ACT.Exp).then_inc(s("Pd"), 1)

            def keep(c):
                yield "keep"
                act.wait_ge(s("rkv"), c + 1)
                a(Hb[:, :, :], H[:, :, :], ACT.Identity)
                a(l_gb[:, :], l_g[:, :], ACT.Identity)
                a(RKVb[:, :, :], RKV[:, :, :], ACT.Identity).then_inc(s("keep"), 1)

            def back(c, tails, tokenizer):
                yield "gn_sq"
                squares(c * (2 * B_NORMS) + 0, "b_")
                yield "gn_std"
                if not tokenizer:
                    act.wait_ge(s("out_dram"), c * (16 * NT))
                inv_std(c * B_NORMS + 1, c * B_NORMS + 1, "b_", PB, rst, eps_c[:, 1:2])
                yield "gn_affine"
                act.wait_ge(s("gn_yn"), c + 1)
                halves(gna, xn, ACT.Identity, s("gn_aff"), bias=lambda h: col("ln_b", h), scale=lambda h: col("ln_w", h))
                yield "ln2_sq"
                squares(c * (2 * B_NORMS) + 2, "b_")
                yield "ln2_std"
                inv_std(c * B_NORMS + 2, c * B_NORMS + 2, "b_", pp[:, 1, 0:N])
                yield "h96_sb"
                act.wait_ge(s("h96_ps"), c + 1)
                a(h96[:, :], pp[0:96, 1, 0:N], ACT.Identity).then_inc(s("h96_sb"), 1)
                yield "router_exp"
                act.wait_ge(s("lg_sub"), c + 1)
                a(lg[:, :, :], lg[:, :, :], ACT.Exp).then_inc(s("lg_exp"), 1)
                yield "ln3_sq"
                squares(c * (2 * B_NORMS) + 4, "b_")
                yield "ln3_std"
                inv_std(c * B_NORMS + 3, c * B_NORMS + 3, "b_", pp[:, 1, 0:N])
                yield "k_bias"
                act.wait_ge(s("k1b_ps"), c + 1)
                halves(k1, PB, ACT.Identity, s("k1b_sb"), bias=lambda h: col("bk", h))
                yield "q_sb"
                act.wait_ge(s("q_ps"), c + 1)
                halves(q1, PA, ACT.Identity, s("q_sb"), bias=lambda h: bqs[:, h:h + 1], scale=0.25)
                yield "hid"
                act.wait_ge(s("hid_ps"), c + 1)
                halves(hid, PB, ACT.Relu, s("hid_sb"), bias=lambda h: col("b1", h))
                yield "tsg"
                act.wait_ge(s("tsg_ps"), c + 1)
                a(tsg[:, :], pp[0:64, 0, 0:N], ACT.Identity, bias=col("b2", 0, 64)).then_inc(s("tsg_sb"), 1)

                def keys(i):
                    t0, n = TILES[i]
                    if i == 0:
                        act.wait_ge(s("k1b_sb"), c + 1)
                    if i >= 2:
                        act.wait_ge(s("sc_ps"), c * NT + i - 1)
                    for e in range(8):
                        last = a(kx[i % 2][:, :, e, 0:n], k1[:, :, t0:t0 + n], ACT.Identity, scale=col("head_mask", e))
                    last.then_inc(s("kx"), 1)

                yield "kx0"
                keys(0)
                yield "hl_exp"
                act.wait_ge(s("hl_sub"), c + 1)
                a(hl[:, :, :], hl[:, :, :], ACT.Exp).then_inc(s("hl_exp"), 1)
                yield "kx1"
                keys(1)
                for i, (t0, n) in enumerate(TILES):
                    yield f"e{i}"
                    act.wait_ge(s("P1"), c * NT + i + 1)
                    a(P1[0:n, i % 2, :, :], P1[0:n, i % 2, :, :], ACT.Exp).then_inc(s("P1e"), 1)
                    if i < 2:
                        yield f"kx{i + 2}"
                        keys(i + 2)
                yield "gx_sb"
                act.wait_ge(s("gx_ps"), c + 1)
                a(Gx, PB, ACT.Identity).then_inc(s("gx_sb"), 1)
                yield "ln4_sq"
                squares(c * (2 * B_NORMS) + 6, "b_")
                yield "h_bias"
                halves(Hb, Hb, ACT.Identity, s("h_bias"), bias=lambda h: col("f_bias", h))
                yield "ln4_std"
                inv_std(c * B_NORMS + 4, c * B_NORMS + 4, "b_", pp[:, 1, 0:N])
                yield "result_sb"
                act.wait_ge(s("out_ps"), c + 1)
                a(Out[:, 0:3, :], pp[:, 2:4, :].rearrange("p a (b n) -> p (a b) n", b=2)[:, 0:3, :], ACT.Identity)
                a(Out[0:96, 3, :], pp[0:96, 3, 256:512], ACT.Identity).then_inc(s("out_sb"), 1)

            def tail(c, first):
                pass

            def half_out(c, half):
                act.wait_ge(s("y_ps"), c * (TC // YG) + (half + 1) * (BANK_T // YG))
                a(Y_sb[:, half, :], y_ps[:, 0:N], ACT.Identity).then_inc(s("y_sb"), 1)

            def scan(c, fill, first, last_chunk):
                for k in range(SLOTS):
                    fill(k)
                    if k == 4 * (BANK_T + 2):
                        if not first:
                            act.wait_ge(s("y_ch"), c)
                        half_out(c, 0)
                fill()
                half_out(c, 1)

            whole(scan, None, setup, conv, front, keep, back, tail, act.Fori)

        @block.vector
        def _(dve):
            v = nc.vector
            tt_, stt, ts = v.tensor_tensor, v.scalar_tensor_tensor, v.tensor_scalar
            v.memset(XN[:, :, :], 0.0)
            v.memset(S_sb[:, :, :, :], 0.0)
            v.memset(Pd[:, :, 0:B], 1.0)
            v.memset(half_c[:, :], -0.5)
            v.memset(eps_c[:, 0:1], 1e-5)
            v.memset(eps_c[:, 1:2], 6.4e-4)
            v.memset(eps_c[:, 2:3], 15.0 * math.log(2.0))
            v.memset(lg[:, :, :], 0.0)
            v.memset(hl[:, :, :], 0.0)
            v.memset(Z[:, :, :], 1.0).then_inc(s("consts"), 1)
            dve.wait_ge(s("consts"), 1)
            dve.wait_ge(s("mix_in"), 16)

            def setup():
                yield "fold_sb"
                dve.wait_ge(s("rest_in"), 16)
                v.tensor_copy(indb[:, :], w("pair_ind", 2))
                v.tensor_copy(negb[:, :], w("pair_neg", 2))
                dve.wait_ge(s("fold_ps"), 1)
                tt_(baseW[:, :, :], fold_ps, w("base_W"), ALU.add).then_inc(s("baseW"), 1)

            def centred(count, fam, src, mean):
                for h in range(2):
                    if h == 0:
                        dve.wait_ge(s(fam + "mean"), count)
                    tt_(xc[:, h, :], src[:, h, :], mean[:, h, :], ALU.subtract).then_inc(s(fam + "xc"), 1)

            def normed(count, halves, fam, dst, r):
                dve.wait_ge(s(fam + "rstd"), count)
                dve.wait_ge(s(fam + "xc"), halves)
                return tt_(dst, xc[:, :, :], r, ALU.mult)

            def conv(c, again, later):
                return
                yield

            def front(c, again, later):
                yield "ln0_xc"
                centred(c * F_NORMS + 1, "f_", H[:, :, :], bh(pp[:, 0, 0:N]))
                yield "ln0_out"
                normed(c * F_NORMS + 1, c * (2 * F_NORMS) + 2, "f_", xn[:, :, :], bh(rstd[:, :])).then_inc(s("ln0_xn"), 1)
                v.tensor_copy(XN[:, :, 0:B], XN[:, :, N:N + B]).then_inc(s("carry"), 1)
                yield "ln1_xc"
                centred(c * F_NORMS + 2, "f_", H[:, :, :], bh(pp[:, 2, 0:N]))
                yield "ln1_out"
                dve.wait_ge(s("carry"), c + 1)
                normed(c * F_NORMS + 2, c * (2 * F_NORMS) + 4, "f_", XN[:, :, B:], bh(rstd[:, :])).then_inc(s("ln1_xn"), 1)
                yield "xx"
                dve.wait_ge(s("ln1_xn"), c + 1)
                tt_(xx, XN[:, :, 0:N], XN[:, :, B:], ALU.subtract).then_inc(s("xx"), 1)
                yield "mix"
                dve.wait_ge(s("xx"), c + 1)
                for h in range(2):
                    last = stt(out=xn[:, h, :], in0=xx[:, h, :], scalar=col("maa_x", h), in1=XN[:, h, B:],
                               op0=ALU.mult, op1=ALU.add)
                last.then_inc(s("mix"), 1)
                for g in range(4):
                    yield f"tmp{g}"
                    src = [PB, PA][g % 2]
                    dve.wait_ge(s("lo2_ps"), c * 4 + g + 1)
                    if g >= 2:
                        dve.wait_ge(s("xm"), c * 4 + g - 1)
                    for h in range(2):
                        last = stt(out=tmps[g % 2][:, h, :], in0=src[:, h, :], scalar=col("maa", 2 * g + h),
                                   in1=xx[:, h, :], op0=ALU.add, op1=ALU.mult)
                    last.then_inc(s("tmp"), 1)
                yield "z_sb"
                dve.wait_ge(s("z_ps"), c + 1)
                dve.wait_ge(s("xm"), c * 4 + 4)
                for h in range(2):
                    last = ts(mz[:, h, :], PA[:, h, :], col("decay", h), 0.0, ALU.add, ALU.min)
                last.then_inc(s("z_sb"), 1)
                yield "kkr"
                dve.wait_ge(s("kkl_ps"), c + 1)
                dve.wait_ge(s("k_sb"), c + 1)
                tt_(kk, PA, K0, ALU.add).then_inc(s("kkr"), 1)
                yield "lsig"
                dve.wait_ge(s("l1p"), c + 1)
                dve.wait_ge(s("z_sb"), c + 1)
                tt_(mz, mz, nz, ALU.subtract).then_inc(s("lsig"), 1)
                yield "wm"
                dve.wait_ge(s("lsig"), c + 1)
                dve.wait_ge(s("mk_sb"), c + 1)
                stt(out=ek, in0=mz, scalar=-0.5, in1=gmk, op0=ALU.add, op1=ALU.mult).then_inc(s("wm"), 1)
                yield "rn"
                dve.wait_ge(s("ss_ps"), c + 1)
                ts(xc[:, :, :], PB, 1e-24, None, ALU.max).then_inc(s("rn"), 1)
                yield "cum"
                dve.wait_ge(s("ld"), c + 1)
                v.tensor_tensor_scan(arena[:, 9 * 960:10 * 960], w("scan_mask"), arena[:, 2 * 960:3 * 960], 0.0,
                                     ALU.mult, ALU.add).then_inc(s("cum"), 1)
                yield "kkn"
                dve.wait_ge(s("norm"), c + 1)
                dve.wait_ge(s("kk_sq"), c + 1)
                tt_(kk, kk, xc[:, :, :], ALU.mult).then_inc(s("kkn"), 1)
                yield "k2"
                dve.wait_ge(s("kmix"), c * 6 + 4)
                dve.wait_ge(s("ek"), c + 1)
                tt_(k2, k2, ek, ALU.mult).then_inc(s("k2"), 1)
                yield "rkp"
                dve.wait_ge(s("k2"), c + 1)
                for h in range(2):
                    last = stt(out=xx[:, h, :], in0=R[:, h, :], scalar=col("faaaa", h), in1=k2[:, h, :],
                               op0=ALU.mult, op1=ALU.mult)
                last.then_inc(s("rkp"), 1)
                yield "scaled_a"
                dve.wait_ge(s("Pd"), c + 1)
                dve.wait_ge(s("kkn"), c + 1)
                tt_(Asc, kk, Pd[:, :, 0:N], ALU.mult)
                yield "scaled_b"
                dve.wait_ge(s("kka"), c + 1)
                stt(out=Bsc, in0=kka, scalar=-1.0, in1=Pinv, op0=ALU.mult, op1=ALU.mult).then_inc(s("scaled"), 1)
                yield "rkv"
                dve.wait_ge(s("rk_ps"), c + 1)
                if again:
                    dve.wait_ge(s("keep"), c)
                tt_(RKV[:, :, :], PA, V, ALU.mult).then_inc(s("rkv"), 1)

            def keep(c):
                return
                yield

            def to_scan(dst, src):
                return v.transpose(dst.rearrange("p t a i -> p t (a i)"), src.rearrange("p a (t b) -> p t a b", b=B))

            def values_keys(c, first):
                dve.wait_ge(s("scaled"), c + 1)
                dve.wait_ge(s("kmix"), c * 6 + 5)
                if not first:
                    dve.wait_ge(s("vk"), c * TC)
                to_scan(V_s[:, :, :, :], V)
                to_scan(K_s[:, :, :, :], Ksc).then_inc(s("vk_in"), 1)

            def tail(c, first):
                if first:
                    values_keys(c, first)
                    v.tensor_copy(S_sb[:, 0, 0, 0:1], S_sb[:, 0, 0, 0:1]).then_inc(s("S_sb"), 1)
                else:
                    for hh in range(2):
                        last = s_times(S_sb[:, hh, :, :], hh, P_s[:, hh, :])
                    last.then_inc(s("S_sb"), 1)
                    dve.wait_ge(s("ub"), c * (2 * TC))
                to_scan(A_s[:, :, :, :], Asc)
                to_scan(B_s[:, :, :, :], Bsc).then_inc(s("AB_in"), 1)
                dve.wait_ge(s("AB_in"), c + 1)

            def queries_decay(c, first):
                dve.wait_ge(s("kmix"), c * 6 + 6)
                if not first:
                    dve.wait_ge(s("Mq"), c * TC)
                    dve.wait_ge(s("S_sb"), c + 1)
                to_scan(Q_s[:, :, :, :], Qsc)
                v.transpose(P_s[:, :, :].rearrange("p a i -> p (a i)"), Pd[:, :, N:N + B]).then_inc(s("scan_in"), 1)
                dve.wait_ge(s("scan_in"), c + 1)

            def s_times(dst, hh, vec):
                return tt_(dst, state[:, hh, 0:256].rearrange("p (i j) -> p i j", j=HS),
                           vec.unsqueeze(1).broadcast_to([P, HS, HS]), ALU.mult)

            def scan(c, fill, first, last_chunk):
                def outputs(t):
                    if t >= 3 or not first:
                        dve.wait_ge(s("Mh"), c * TC + (t - 2))
                    for hh in range(2):
                        last = s_times(Mq[:, t % 3, hh, :, :], hh, Q_s[:, t, hh, :])
                    last.then_inc(s("Mq"), 1)

                for t in range(TC):
                    fill(4 * t)
                    for hh in range(2):
                        dve.wait_ge(s(f"upd{hh}"), c * (TC + 1) + (t + 1))
                        s_times(Ma[:, hh, :, :], hh, A_s[:, t, hh, :]).then_inc(s("Ma"), 1)
                    fill(4 * t + 1)
                    if t > 0:
                        outputs(t - 1)
                    fill(4 * t + 2)
                    for hh in range(2):
                        dve.wait_ge(s("Ma"), c * (2 * TC) + (2 * t + hh + 1))
                        v.tensor_reduce(u[:, hh, :], Ma[:, hh, :, :], AX, ALU.add).then_inc(s("u"), 1)
                    for hh in range(2):
                        dve.wait_ge(s("u"), c * (2 * TC) + (2 * t + hh + 1))
                        tt_(ub[:, hh, :, :], u[:, hh, :].unsqueeze(2).broadcast_to([P, HS, HS]),
                            B_s[:, t, hh, :].unsqueeze(1).broadcast_to([P, HS, HS]), ALU.mult)\
                            .then_inc(s("ub"), 1)
                    if t == 0:
                        queries_decay(c, first)
                    fill(4 * t + 3)
                fill()
                if not last_chunk:
                    values_keys(c + 1, False)
                dve.wait_ge(s("upd0"), c * (TC + 1) + (TC + 1))
                dve.wait_ge(s("upd1"), c * (TC + 1) + (TC + 1))
                outputs(TC - 1)

            def back(c, tails, tokenizer):
                yield "y_turn"
                dve.wait_ge(s("y_sb"), c * 2 + 2)
                v.transpose(tb(xn[:, :, :]).rearrange("p a t b -> p t a b"),
                            Y_sb[:, :, :].rearrange("p g (t n) -> p g t n", n=32)).then_inc(s("y_ch"), 1)
                yield "gn_xc"
                dve.wait_ge(s("y_ch"), c + 1)
                centred(c * B_NORMS + 1, "b_", xn[:, :, :], PA)
                yield "gn_out"
                normed(c * B_NORMS + 1, c * (2 * B_NORMS) + 2, "b_", xn[:, :, :], rst).then_inc(s("gn_yn"), 1)
                yield "bonus"
                dve.wait_ge(s("keep"), c + 1)
                dve.wait_ge(s("gn_aff"), c + 1)
                tt_(xc[:, :, :], gna, RKVb[:, :, :], ALU.add).then_inc(s("y_bonus"), 1)
                yield "gated"
                dve.wait_ge(s("g_ps"), c + 1)
                dve.wait_ge(s("y_bonus"), c + 1)
                tt_(xn[:, :, :], PA, xc[:, :, :], ALU.mult).then_inc(s("y_gated"), 1)
                yield "h1"
                for h in range(2):
                    dve.wait_ge(s("wo_ps"), c * 2 + (h + 1))
                    tt_(Hb[:, h, :], PB[:, h, :], Hb[:, h, :], ALU.add).then_inc(s("h1"), 1)
                yield "ln2_xc"
                dve.wait_ge(s("h1"), c * 2 + 2)
                centred(c * B_NORMS + 2, "b_", Hb[:, :, :], bh(pp[:, 0, 0:N]))
                yield "ln2_out"
                normed(c * B_NORMS + 2, c * (2 * B_NORMS) + 4, "b_", xn[:, :, :], bh(rstd[:, :])).then_inc(s("ln2_xn"), 1)
                steps = [0]

                def chain(ins):
                    steps[0] += 1
                    ins.then_inc(s("small"), 1)
                    dve.wait_ge(s("small"), c * SMALL + steps[0])

                def b6(ap):
                    return ap.broadcast_to([P, NT, 6])

                yield "router_max"
                dve.wait_ge(s("router_ps"), c + 1)
                rl = pp[:, 0, 0:32].rearrange("p (a n) -> p a n", n=8)[:, :, 0:6]
                v.tensor_copy(lg[:, 0:3, :], rl[:, 0:3, :])
                chain(v.tensor_copy(lg[0:96, 3, :], rl[0:96, 3, :]))
                chain(v.tensor_reduce(f1[0][:, :, :], lg[:, :, :], AX, ALU.max))
                tt_(lg[:, :, :], lg[:, :, :], b6(f1[0][:, :, :]), ALU.subtract).then_inc(s("lg_sub"), 1)
                yield "gates"
                dve.wait_ge(s("lg_exp"), c + 1)
                chain(v.tensor_reduce(f1[1][:, :, :], lg[:, :, :], AX, ALU.add))
                chain(v.reciprocal(f1[2][:, :, :], f1[1][:, :, :]))
                gt = fs[0][:, :, :]
                chain(tt_(gt, lg[:, :, :], b6(f1[2][:, :, :]), ALU.mult))
                yield "rank"
                other = gt.unsqueeze(2).broadcast_to([P, NT, 6, 6])
                this = gt.unsqueeze(3).broadcast_to([P, NT, 6, 6])
                tt_(cmp1[:, :, :, :], other, this, ALU.is_gt)
                chain(tt_(cmp2[:, :, :, :], other, this, ALU.is_equal))
                chain(tt_(cmp2[:, :, :, :], cmp2[:, :, :, :],
                          w("expert_before").rearrange("p (a b) -> p a b", b=6).unsqueeze(1).broadcast_to([P, NT, 6, 6]),
                          ALU.mult))
                chain(tt_(cmp1[:, :, :, :], cmp1[:, :, :, :], cmp2[:, :, :, :], ALU.add))
                yield "top2"
                chain(v.tensor_reduce(fs[1][:, :, :], cmp1[:, :, :, :], AX, ALU.add))
                chain(stt(out=fs[2][:, :, :], in0=fs[1][:, :, :], scalar=1.5, in1=gt, op0=ALU.is_lt, op1=ALU.mult))
                chain(v.tensor_reduce(f1[3][:, :, :], fs[2][:, :, :], AX, ALU.add))
                yield "top2_sum"
                chain(ts(f1[0][:, :, :], f1[3][:, :, :], 1e-6, None, ALU.add))
                chain(v.reciprocal(f1[1][:, :, :], f1[0][:, :, :]))
                chain(tt_(fs[3][:, :, :], fs[2][:, :, :], b6(f1[1][:, :, :]), ALU.mult))
                v.tensor_copy(sw96[:, :, :, :], fs[3][:, :, :].unsqueeze(3).broadcast_to([P, NT, 6, 16]))\
                    .then_inc(s("sw96"), 1)
                yield "hw"
                dve.wait_ge(s("w96_ps"), c + 1)
                dve.wait_ge(s("h96_sb"), c + 1)
                tt_(h96[:, :], pp[0:96, 0, 0:N], h96[:, :], ALU.mult).then_inc(s("hw"), 1)
                yield "h2"
                for h in range(2):
                    dve.wait_ge(s("ffn_ps"), c * 2 + (h + 1))
                    stt(out=Hb[:, h, :], in0=PB[:, h, :], scalar=col("base_b", h), in1=Hb[:, h, :],
                        op0=ALU.add, op1=ALU.add).then_inc(s("h2"), 1)

                yield "ln3_xc"
                dve.wait_ge(s("h2"), c * 2 + 2)
                centred(c * B_NORMS + 3, "b_", Hb[:, :, :], bh(pp[:, 0, 0:N]))
                yield "ln3_out"
                normed(c * B_NORMS + 3, c * (2 * B_NORMS) + 6, "b_", xn[:, :, :], bh(rstd[:, :])).then_inc(s("ln3_xn"), 1)
                yield "Vx"
                dve.wait_ge(s("v1_ps"), c + 1)
                dve.wait_ge(s("PV0"), c + 1)
                bvx = w("bv").rearrange("p (a b d) -> p a b d", b=2, d=16)
                for i, (t0, n) in enumerate(TILES):
                    src = vq(2, i, n).rearrange("p (a b d) -> p a b d", b=2, d=16)
                    for hh in range(2):
                        last = tt_(Vx[0:n, i, :, hh, 16 * hh:16 * hh + 16], src[:, :, hh, :], bvx[0:n, :, hh, :],
                                   ALU.add)
                last.then_inc(s("Vx"), 1)
                yield "hl_max"
                dve.wait_ge(s("hl_ps"), c + 1)
                hp = pp[:, 1, 0:64].rearrange("p (a n) -> p a n", n=16)

                def b16(ap):
                    return ap.broadcast_to([P, NT, 16])

                v.tensor_copy(hl[:, 0:3, :], hp[:, 0:3, :])
                chain(v.tensor_copy(hl[0:96, 3, :], hp[0:96, 3, :]))
                chain(v.tensor_reduce(f1[0][:, :, :], hl[:, :, :], AX, ALU.max))
                tt_(hl[:, :, :], hl[:, :, :], b16(f1[0][:, :, :]), ALU.subtract).then_inc(s("hl_sub"), 1)
                yield "hl_gate"
                dve.wait_ge(s("hl_exp"), c + 1)
                chain(v.tensor_reduce(f1[1][:, :, :], hl[:, :, :], AX, ALU.add))
                chain(v.reciprocal(f1[2][:, :, :], f1[1][:, :, :]))
                chain(tt_(hl[:, :, :], hl[:, :, :], b16(f1[2][:, :, :]), ALU.mult))

                def scores(i):
                    t0, n = TILES[i]
                    sc = pp[0:n, 2 + i % 2, :].rearrange("p (h n) -> p h n", n=32)
                    dve.wait_ge(s("sc_ps"), c * NT + i + 1)
                    v.tensor_reduce(mx[0:n, i, :], sc, AX, ALU.max).then_inc(s("mx"), 1)
                    dve.wait_ge(s("mx"), c * NT + i + 1)
                    tt_(P1[0:n, i % 2, :, :], sc, mx[0:n, i, :].unsqueeze(2).broadcast_to([n, 16, 32]),
                        ALU.subtract).then_inc(s("P1"), 1)

                def turn(i):
                    t0, n = TILES[i]
                    dve.wait_ge(s("P1e"), c * NT + i + 1)
                    v.tensor_reduce(Z[0:n, i, :], P1[0:n, i % 2, :, :], AX, ALU.add).then_inc(s("Z"), 1)
                    if i >= 2:
                        dve.wait_ge(s("av_ps"), c * NT + i - 1)
                    for qd in range(n // 32):
                        r = slice(32 * qd, 32 * qd + 32)
                        last = v.transpose(PT[i % 2][r, :, r], P1[r, i % 2, :, :])
                    last.then_inc(s("PT"), 1)

                yield "p0"
                scores(0)
                for i in range(NT):
                    if i + 1 < NT:
                        yield f"p{i + 1}"
                        scores(i + 1)
                    yield f"t{i}"
                    turn(i)
                yield "gz"
                dve.wait_ge(s("Z"), c * NT + NT)
                chain(v.reciprocal(hl2[:, :, :], Z[:, :, :]))
                chain(tt_(hl2[:, :, :], hl2[:, :, :], hl[:, :, :], ALU.mult))
                v.tensor_copy(gz[:, :, :, :], hl2[:, :, :].unsqueeze(3).broadcast_to([P, NT, 16, 16]))\
                    .then_inc(s("gz"), 1)
                yield "O"
                dve.wait_ge(s("gx_sb"), c + 1)
                dve.wait_ge(s("av_ps"), c * NT + NT)
                tt_(O, PA, Gx, ALU.mult).then_inc(s("O_sb"), 1)
                yield "h3"
                for h in range(2):
                    dve.wait_ge(s("wo1_ps"), c * 2 + (h + 1))
                    stt(out=Hb[:, h, :], in0=PB[:, h, :], scalar=col("bo", h), in1=Hb[:, h, :],
                        op0=ALU.add, op1=ALU.add).then_inc(s("h3"), 1)
                yield "ln4_xc"
                dve.wait_ge(s("h3"), c * 2 + 2)
                centred(c * B_NORMS + 4, "b_", Hb[:, :, :], bh(pp[:, 0, 0:N]))
                yield "ln4_out"
                normed(c * B_NORMS + 4, c * (2 * B_NORMS) + 8, "b_", xn[:, :, :], bh(rstd[:, :])).then_inc(s("ln4_xn"), 1)
                assert steps[0] == SMALL

            whole(scan, None, setup, conv, front, keep, back, tail, dve.Fori)

        @block.gpsimd
        def _(pool):
            g_ = nc.gpsimd
            g_.memset(zero_c[:, :], 0.0).then_inc(s("zero"), 1)
            pool.wait_ge(s("zero"), 1)

            def setup():
                return
                yield

            def conv(c, again, later):
                for k in range(1, KT):
                    yield f"tap{k}"
                    pool.wait_ge(s("tap"), c * KT + (k + 1))
                    if k == 1 and again:
                        pool.wait_ge(s("proj_ps"), c)
                    if k >= 2:
                        pool.wait_ge(s("tap_sum"), c * (KT - 2) + (k - 1))
                    g_.tensor_tensor(Xc[:, :], tap[:, 0, :] if k == 1 else Xc[:, :], tap[:, k % 4, :], ALU.add)\
                        .then_inc(s("conv" if k == KT - 1 else "tap_sum"), 1)

            def front(c, again, later):
                for g in range(4):
                    yield f"xm{g}"
                    if g == 0 and later:
                        pool.wait_ge(s("out_dram"), (c - 1) * (16 * NT))
                    pool.wait_ge(s("tmp"), c * 4 + g + 1)
                    g_.tensor_tensor(xm[g], tmps[g % 2], XN[:, :, B:], ALU.add).then_inc(s("xm"), 1)
                yield "mix0"
                pool.wait_ge(s("ma_sb"), c + 1)
                pool.wait_ge(s("a_sb"), c + 1)
                g_.tensor_tensor(mix4, ga, gma, ALU.mult).then_inc(s("kmix"), 1)
                yield "mix1"
                pool.wait_ge(s("kmix"), c * 6 + 1)
                g_.tensor_tensor(mix4, ga, mix4, ALU.subtract).then_inc(s("kmix"), 1)
                yield "mix2"
                pool.wait_ge(s("kmix"), c * 6 + 2)
                g_.tensor_tensor(mix4, gma, mix4, ALU.add).then_inc(s("kmix"), 1)
                yield "kmix"
                pool.wait_ge(s("kmix"), c * 6 + 3)
                pool.wait_ge(s("k_sb"), c + 1)
                g_.tensor_tensor(k2, K0, mix4, ALU.mult).then_inc(s("kmix"), 1)
                yield "kka"
                pool.wait_ge(s("kkn"), c + 1)
                g_.tensor_tensor(kka, kk, ga, ALU.mult).then_inc(s("kka"), 1)
                yield "scaled_k"
                pool.wait_ge(s("Pd"), c + 1)
                pool.wait_ge(s("rkp"), c + 1)
                g_.tensor_tensor(Ksc, k2, Pinv, ALU.mult).then_inc(s("kmix"), 1)
                yield "scaled_q"
                g_.tensor_tensor(Qsc, R, Pd[:, :, B:], ALU.mult).then_inc(s("kmix"), 1)

            def keep(c):
                return
                yield

            def back(c, tails, tokenizer):
                for k in range(3):
                    yield f"zero{k}"
                    pool.wait_ge(s("scan_in"), tails)
                    zz = zero_c[:, 0:1].broadcast_to([P, 2048])
                    last = g_.tensor_tensor(arena[:, 4096 + 2048 * k:6144 + 2048 * k], zz, zz, ALU.add)
                last.then_inc(s("PV0"), 1)

            def tail(c, first):
                pass

            def scan(c, fill, first, last_chunk):
                def outer(t):
                    pool.wait_ge(s("vk_in"), c + 1)
                    if t >= RING:
                        pool.wait_ge(s("upd1"), c * (TC + 1) + (t - RING + 2))
                    for hh in range(2):
                        last = g_.tensor_tensor(vk[:, t % RING, hh, :, :],
                                                V_s[:, t, hh, :].unsqueeze(2).broadcast_to([P, HS, HS]),
                                                K_s[:, t, hh, :].unsqueeze(1).broadcast_to([P, HS, HS]), ALU.mult)
                    last.then_inc(s("vk"), 1)

                def halve(t):
                    m = Mq[:, t % 3, :, :, :]
                    pool.wait_ge(s("Mq"), c * TC + (t + 1))
                    if t >= 2 * YG:
                        pool.wait_ge(s("y_ps"), c * (TC // YG) + (t // YG - 1))
                    elif not first:
                        pool.wait_ge(s("y_ps"), c * (TC // YG) + (t // YG - 1))
                    g_.tensor_tensor(Mh[:, t % (2 * YG), :, :, :], m[:, :, :, 0:HS // 2], m[:, :, :, HS // 2:], ALU.add)\
                        .then_inc(s("Mh"), 1)

                outer(0)
                outer(1)
                for t in range(TC):
                    fill(4 * t)
                    if t + 2 < TC:
                        outer(t + 2)
                    fill(4 * t + 1)
                    if t > 0:
                        halve(t - 1)
                    fill(4 * t + 2)
                    fill(4 * t + 3)
                fill()
                halve(TC - 1)

            whole(scan, None, setup, conv, front, keep, back, tail, pool.Fori)


def kernel(**inp):
    import numpy as np
    import concourse.bacc as bacc
    from concourse.bass_utils import run_bass_kernel_spmd

    f = {k: np.asarray(v) for k, v in inp.items()}
    where, n_params = offsets(PACK)
    where_s, n_setup = offsets(SETUP)
    prm = np.zeros((P, n_params), np.float32)
    dft = np.zeros((P, n_setup), np.float32)

    def put(name, a, r0=0, c0=0):
        at = where[name][0] + c0
        prm[r0:r0 + a.shape[0], at:at + a.shape[1]] = a

    def vec(name, a):
        put(name, a.reshape(2, P).T)

    def rows(name, a, c0=0, n=None):
        n = n or a.shape[1]
        put(name, a[0:P], 0, c0)
        put(name, a[P:2 * P], 0, n + c0)

    L0, F0, L1 = "L0_attn_", "L0_ffn_", "L1_attn_"
    wt = f["L0_tok_w_temporal"][:, 0, :]
    put("w_temporal", np.concatenate([wt, wt]))
    put("w_proj", np.concatenate([f["L0_tok_w_proj"].T, f["L0_tok_w_proj"].T]))
    tg = np.arange(KG, dtype=np.float32) - (KG - 1) / 2
    g = np.exp(-tg ** 2 / 8.0).astype(np.float32)
    g = g / g.sum()
    band = np.zeros((P, SM1), np.float32)
    for j in range(SM1):
        band[j:j + KG, j] = g
    put("gauss", band)
    put("ident", np.eye(P, dtype=np.float32))
    vec("b_proj", f["L0_tok_b_proj"])
    vec("ln_gamma", f["L0_tok_ln_gamma"])
    vec("ln_beta", f["L0_tok_ln_beta"])
    put("ones256", np.full((P, P), 1.0 / D, np.float32))
    same = np.kron(np.eye(8, dtype=np.float32), np.ones((16, 16), np.float32))
    put("head_ones", same)
    put("head_mean", same * np.float32(1.0 / HS))
    keep = np.ones((P, 2 * B, TC), np.float32)
    keep[:, :, 0] = 0.0
    put("scan_mask", keep.reshape(P, -1))
    vec("maa_x", f[L0 + "time_maa_x"])
    put("maa", f[L0 + "time_maa"].reshape(8, P).T)
    rows("maa_w1", f[L0 + "maa_w1"].T)
    put("maa_w2", f[L0 + "maa_w2"].reshape(P, D))
    rows("wa_w1", f[L0 + "decay_w1"].T, 0, 112)
    rows("wa_w1", f[L0 + "aaa_w1"].T, 64, 112)
    rows("wa_w1", f[L0 + "ma_w1"].T, 96, 112)
    put("wa_w2", f[L0 + "decay_w2"])
    put("wa_w2", f[L0 + "aaa_w2"], 64)
    put("wa_w2", f[L0 + "ma_w2"], 96)
    rows("k_w1", f[L0 + "kkk_w1"].T, 0, 48)
    rows("k_w1", f[L0 + "mk_w1"].T, 32, 48)
    put("k_w2", f[L0 + "kkk_w2"])
    put("k_w2", f[L0 + "mk_w2"], 32)
    rows("gate_w1", f[L0 + "gate_w1"].T)
    put("gate_w2", f[L0 + "gate_w2"])
    for nm in ("Wr", "Wk", "Wv", "Wo"):
        rows(nm, f[L0 + nm].T)
    for nm, src in (("decay", "time_decay"), ("faaaa", "time_faaaa"), ("aaaaa", "time_aaaaa"),
                    ("misc_a", "time_misc_a"), ("misc_k", "time_misc_k"), ("ln_w", "ln_w"), ("ln_b", "ln_b")):
        vec(nm, f[L0 + src])
    rows("base_W", f[F0 + "base_W"].T)
    vec("base_b", f[F0 + "base_b"])
    put("shared_A", f[F0 + "shared_A"])
    put("shared_B", f[F0 + "shared_B"].T)
    rows("routed_A", f[F0 + "routed_A"].reshape(96, D).T)
    put("routed_B", f[F0 + "routed_B"].transpose(0, 2, 1).reshape(96, D))
    rows("router_W", f[F0 + "router_W"].T)
    put("router_b", f[F0 + "router_b"].reshape(1, 6))
    put("expert_before", np.tile(np.tril(np.ones((6, 6), np.float32), -1).reshape(1, 36), (P, 1)))
    for nm, src in (("Wq1", "Wq"), ("Wk1", "Wk"), ("Wv1", "Wv"), ("Wo1", "Wo"), ("W1", "W1"), ("W2", "W2")):
        rows(nm, f[L1 + src].T)
    put("sig", f[L1 + "head_signatures"].T)
    for nm in ("bq", "bk", "bo", "b1"):
        vec(nm, f[L1 + nm])
    put("bv", np.broadcast_to(f[L1 + "bv"].reshape(1, D), (P, D)))
    put("b2", f[L1 + "b2"].reshape(64, 1))
    put("head_mask", np.kron(np.eye(8, dtype=np.float32), np.ones((16, 1), np.float32)))
    who = (np.arange(P) // 16) % 2
    put("pair_ind", np.stack([who == 0, who == 1]).astype(np.float32))
    key = (np.arange(512) // 16) % 2
    put("pair_neg", np.stack([key != 0, key != 1]).astype(np.float32) * np.float32(NEG))
    put("ones_row", np.ones((1, P), np.float32))
    vec("f_bias", f["L1_ffn_bias"])

    ang = 2.0 * np.pi * ((np.arange(D)[:, None] * np.arange(D)[None, :]) % D) / D
    mats = {"wfr": f["L1_ffn_w_freq_real"], "wfi": f["L1_ffn_w_freq_imag"],
            "Fr": np.cos(ang), "Fi": -np.sin(ang), "nFi": np.sin(ang),
            "Gr": np.cos(ang) / D, "nGi": -np.sin(ang) / D}
    for nm, m in mats.items():
        at = where_s[nm][0]
        dft[:, at:at + D] = m[0:P]
        dft[:, at + D:at + 2 * D] = m[P:2 * P]

    rows_x = STRIDE * TC * (CHUNKS - 1) + SM1 + XROWS2
    xp = np.zeros((rows_x, B * C_IN), np.float32)
    xp[PAD:PAD + T_IN] = f["x"].reshape(2, 8, T_IN, C_IN).transpose(2, 1, 0, 3).reshape(T_IN, B * C_IN)[:rows_x - PAD]

    nc = bacc.Bacc("TRN2", target_bir_lowering=False, num_devices=1)
    arrays = {"x_in": xp, "params_in": prm, "dft_in": dft}
    args = [nc.dram_tensor(k, a.shape, mybir.dt.from_np(a.dtype), kind="ExternalInput").ap() for k, a in arrays.items()]
    out = nc.dram_tensor("out", (B, T, D), F32, kind="ExternalOutput").ap()
    tower(nc, *args, out)
    r = run_bass_kernel_spmd(nc, [arrays], core_ids=[0])
    return r.results[0]["out"]
```
